# Optimizing a Trainium2 kernel written in Bass

```python
import numpy as np
import jax
import jax.numpy as jnp

def _softmax(x, axis=-1):
    return jax.nn.softmax(x, axis=axis)

def _gelu(x):
    return jax.nn.gelu(x, approximate=True)

def _silu(x):
    return jax.nn.silu(x)

def _sigmoid(x):
    return jax.nn.sigmoid(x)

def _layernorm(x, axis=-1, eps=1e-05):
    m = jnp.mean(x, axis=axis, keepdims=True)
    v = jnp.var(x, axis=axis, keepdims=True)
    return (x - m) / jnp.sqrt(v + eps)

def _scatter_add(tgt, idx, src, axis=0):
    return tgt.at[idx].add(src)

def _segment_sum(src, seg, n):
    return jax.ops.segment_sum(src, seg, n)
kernel_name = 'mk_gnn_ffn_d4_gnn_r32_be2b57'

def setup_inputs(seed: int=0):
    np.random.seed(seed)
    _w = jnp.asarray

    def _rec_inputs():
        import jax
        import jax.numpy as jnp
        _gk = jax.random.key(seed)
        x = -0.000364 + 1 * jax.random.normal(jax.random.fold_in(_gk, 1), (625, 768), jnp.float32)
        src = jax.random.randint(jax.random.fold_in(_gk, 2), (20000,), 0, 625, jnp.int32)
        dst = jnp.minimum((625 * jax.random.uniform(jax.random.fold_in(_gk, 3), (20000,)) ** 2.0).astype(jnp.int32), 19999)
        _o = jnp.argsort(dst, stable=True)
        src = src[_o]
        dst = dst[_o]
        return (x, src, dst)
    x, src, dst = _rec_inputs()

    def _L0_gnn_setup():
        import jax, jax.numpy as jnp
        import numpy as np
        N, E, DIM, HEADS = (625, 10000, 768, 8)
        HD = DIM // HEADS
        EPS = 1e-05

        def layer_norm(x, w, b):
            mu = jnp.mean(x, axis=-1, keepdims=True)
            var = jnp.var(x, axis=-1, keepdims=True)
            return (x - mu) * jax.lax.rsqrt(var + EPS) * w + b

        def gatv2(x, src, dst, Ws, bs, Wd, bd, attn):
            H, D = attn.shape
            fs = (x @ Ws + bs).reshape(-1, H, D)
            fd = (x @ Wd + bd).reshape(-1, H, D)
            e = jax.nn.leaky_relu(fs[src] + fd[dst], 0.2)
            logits = jnp.einsum('ehd,hd->eh', e, attn)
            m = jax.ops.segment_max(logits, dst, num_segments=N)
            ex = jnp.exp(logits - m[dst])
            denom = jax.ops.segment_sum(ex, dst, num_segments=N)
            alpha = ex / denom[dst]
            out = jax.ops.segment_sum(alpha[:, :, None] * fs[src], dst, num_segments=N)
            return jax.nn.elu(out)
        key = jax.random.key(seed)
        ks = jax.random.split(key, 10)
        s = 1.0 / np.sqrt(DIM)
        return {'x': jax.random.normal(ks[0], (N, DIM), jnp.float32), 'src': jax.random.randint(ks[1], (E,), 0, N, jnp.int32), 'dst': jax.random.randint(ks[2], (E,), 0, N, jnp.int32), 'W1s': jax.random.normal(ks[3], (DIM, DIM), jnp.float32) * s, 'b1s': jnp.zeros((DIM,), jnp.float32), 'W1d': jax.random.normal(ks[4], (DIM, DIM), jnp.float32) * s, 'b1d': jnp.zeros((DIM,), jnp.float32), 'attn1': jax.random.normal(ks[5], (HEADS, HD), jnp.float32) * s, 'ln1_w': jnp.ones((DIM,), jnp.float32), 'ln1_b': jnp.zeros((DIM,), jnp.float32), 'Wos': jax.random.normal(ks[6], (DIM, DIM), jnp.float32) * s, 'bos': jnp.zeros((DIM,), jnp.float32), 'Wod': jax.random.normal(ks[7], (DIM, DIM), jnp.float32) * s, 'bod': jnp.zeros((DIM,), jnp.float32), 'attno': jax.random.normal(ks[8], (1, DIM), jnp.float32) * s, 'lno_w': jnp.ones((DIM,), jnp.float32), 'lno_b': jnp.zeros((DIM,), jnp.float32)}
    _L0_gnn_all = _L0_gnn_setup()
    _L0_gnn_in = {k: v for k, v in _L0_gnn_all.items() if k in ('W1s', 'b1s', 'W1d', 'b1d', 'attn1', 'ln1_w', 'ln1_b', 'Wos', 'bos', 'Wod', 'bod', 'attno', 'lno_w', 'lno_b')}
    del _L0_gnn_all

    def _L0_ffn_setup():
        import jax, jax.numpy as jnp
        import numpy as np
        TOP_K = 2
        key = jax.random.key(seed)
        ks = jax.random.split(key, 8)
        B, S, D, E = (4, 64, 768, 8)
        F = 4 * D
        scale = 0.02
        x = jax.random.normal(ks[0], (B, S, D), dtype=jnp.float32)
        router_w = jax.random.normal(ks[1], (D, E), dtype=jnp.float32) * scale
        router_b = jnp.zeros((E,), dtype=jnp.float32)
        w1 = jax.random.normal(ks[2], (E, D, F), dtype=jnp.float32) * scale
        b1 = jnp.zeros((E, F), dtype=jnp.float32)
        w2 = jax.random.normal(ks[3], (E, F, D), dtype=jnp.float32) * scale
        b2 = jnp.zeros((E, D), dtype=jnp.float32)
        return {'x': x, 'router_w': router_w, 'router_b': router_b, 'w1': w1, 'b1': b1, 'w2': w2, 'b2': b2}
    _L0_ffn_all = _L0_ffn_setup()
    _L0_ffn_in = {k: v for k, v in _L0_ffn_all.items() if k in ('router_w', 'router_b', 'w1', 'b1', 'w2', 'b2')}
    del _L0_ffn_all

    def _L1_gnn_setup():
        import jax, jax.numpy as jnp
        import numpy as np
        N_NODES = 10000
        NEG_SLOPE = 0.2
        EPS = 1e-16

        def gat_layer(x, W, att_src, att_dst, bias, src, dst, heads, out_ch, concat):
            n = x.shape[0]
            h = (x @ W.T).reshape(n, heads, out_ch)
            a_src = jnp.einsum('nhc,hc->nh', h, att_src)
            a_dst = jnp.einsum('nhc,hc->nh', h, att_dst)
            e = a_src[src] + a_dst[dst]
            e = jax.nn.leaky_relu(e, NEG_SLOPE)
            m = jax.ops.segment_max(e, dst, num_segments=n)
            ex = jnp.exp(e - m[dst])
            denom = jax.ops.segment_sum(ex, dst, num_segments=n)
            alpha = ex / (denom[dst] + EPS)
            msg = alpha[:, :, None] * h[src]
            out = jax.ops.segment_sum(msg, dst, num_segments=n)
            if concat:
                out = out.reshape(n, heads * out_ch)
            else:
                out = out.mean(axis=1)
            return out + bias
        key = jax.random.key(seed)
        ks = jax.random.split(key, 12)
        x = jax.random.normal(ks[0], (N_NODES, 768), dtype=jnp.float32)
        edge_index = jax.random.randint(ks[1], (2, 5000), 0, N_NODES, dtype=jnp.int64)
        s1 = 1.0 / np.sqrt(768.0)
        W1 = jax.random.normal(ks[2], (8 * 128, 768), dtype=jnp.float32) * s1
        att_src1 = jax.random.normal(ks[3], (8, 128), dtype=jnp.float32) * (1.0 / np.sqrt(128.0))
        att_dst1 = jax.random.normal(ks[4], (8, 128), dtype=jnp.float32) * (1.0 / np.sqrt(128.0))
        b1 = jnp.zeros((8 * 128,), dtype=jnp.float32)
        s2 = 1.0 / np.sqrt(1024.0)
        W2 = jax.random.normal(ks[5], (1 * 768, 1024), dtype=jnp.float32) * s2
        att_src2 = jax.random.normal(ks[6], (1, 768), dtype=jnp.float32) * (1.0 / np.sqrt(768.0))
        att_dst2 = jax.random.normal(ks[7], (1, 768), dtype=jnp.float32) * (1.0 / np.sqrt(768.0))
        b2 = jnp.zeros((768,), dtype=jnp.float32)
        return {'x': x, 'edge_index': edge_index, 'W1': W1, 'att_src1': att_src1, 'att_dst1': att_dst1, 'b1': b1, 'W2': W2, 'att_src2': att_src2, 'att_dst2': att_dst2, 'b2': b2}
    _L1_gnn_all = _L1_gnn_setup()
    _L1_gnn_in = {k: v for k, v in _L1_gnn_all.items() if k in ('W1', 'att_src1', 'att_dst1', 'b1', 'W2', 'att_src2', 'att_dst2', 'b2')}
    del _L1_gnn_all

    def _L1_ffn_setup():
        import jax, jax.numpy as jnp
        import numpy as np
        EPS_NORM = 1e-06
        EPS_Q = 1e-05

        def rmsnorm(x, g):
            return x * jax.lax.rsqrt(jnp.mean(x * x, axis=-1, keepdims=True) + EPS_NORM) * g

        def activation_quant(x):
            scale = 127.0 / jnp.maximum(jnp.max(jnp.abs(x), axis=-1, keepdims=True), EPS_Q)
            return jnp.clip(jnp.round(x * scale), -128, 127) / scale

        def weight_quant(w):
            scale = 1.0 / jnp.maximum(jnp.mean(jnp.abs(w)), EPS_Q)
            return jnp.clip(jnp.round(w * scale), -1, 1) / scale

        def bitlinear(x, w, g):
            x_norm = rmsnorm(x, g)
            x_q = x_norm + jax.lax.stop_gradient(activation_quant(x_norm) - x_norm)
            w_q = w + jax.lax.stop_gradient(weight_quant(w) - w)
            return jnp.einsum('bsd,od->bso', x_q, w_q)
        key = jax.random.key(seed)
        k1, k2, k3 = jax.random.split(key, 3)
        B, S, D, H = (8, 128, 768, 64)
        x = jax.random.normal(k1, (B, S, D), dtype=jnp.float32)
        w_in = jax.random.normal(k2, (2 * H, D), dtype=jnp.float32) * 0.002
        w_out = jax.random.normal(k3, (D, H), dtype=jnp.float32) * 0.002
        g_in = jnp.ones((D,), dtype=jnp.float32)
        g_out = jnp.ones((H,), dtype=jnp.float32)
        return {'x': x, 'w_in': w_in, 'g_in': g_in, 'w_out': w_out, 'g_out': g_out}
    _L1_ffn_all = _L1_ffn_setup()
    _L1_ffn_in = {k: v for k, v in _L1_ffn_all.items() if k in ('w_in', 'g_in', 'w_out', 'g_out')}
    del _L1_ffn_all

    def _L2_gnn_setup():
        import jax, jax.numpy as jnp
        import numpy as np
        N_NODES = 10000
        key = jax.random.key(seed)
        k1, k2, k3 = jax.random.split(key, 3)
        x = jax.random.normal(k1, (N_NODES, 768), dtype=jnp.float32)
        edge_index = jax.random.randint(k2, (2, 3125), 0, N_NODES, dtype=jnp.int32)
        W = jax.random.normal(k3, (768, 768), dtype=jnp.float32) * (1.0 / np.sqrt(768))
        b = jnp.zeros((768,), dtype=jnp.float32)
        return {'x': x, 'edge_index': edge_index, 'W': W, 'b': b}
    _L2_gnn_all = _L2_gnn_setup()
    _L2_gnn_in = {k: v for k, v in _L2_gnn_all.items() if k in ('W', 'b')}
    del _L2_gnn_all

    def _L2_ffn_setup():
        import jax, jax.numpy as jnp
        import numpy as np
        B, S, H, F, E = (8, 512, 768, 96, 6)
        TOP_K = 2
        key = jax.random.key(seed)
        ks = jax.random.split(key, 7)
        sH = 1.0 / np.sqrt(H)
        sF = 1.0 / np.sqrt(F)
        return {'x': jax.random.normal(ks[0], (B, S, H), dtype=jnp.float32), 'gate_w': jax.random.normal(ks[1], (H, E), dtype=jnp.float32) * sH, 'gate_b': jax.random.normal(ks[2], (E,), dtype=jnp.float32) * 0.01, 'w1': jax.random.normal(ks[3], (E, H, F), dtype=jnp.float32) * sH, 'b1': jax.random.normal(ks[4], (E, F), dtype=jnp.float32) * 0.01, 'w2': jax.random.normal(ks[5], (E, F, H), dtype=jnp.float32) * sF, 'b2': jax.random.normal(ks[6], (E, H), dtype=jnp.float32) * 0.01}
    _L2_ffn_all = _L2_ffn_setup()
    _L2_ffn_in = {k: v for k, v in _L2_ffn_all.items() if k in ('gate_w', 'gate_b', 'w1', 'b1', 'w2', 'b2')}
    del _L2_ffn_all

    def _L3_gnn_setup():
        import jax, jax.numpy as jnp
        import numpy as np
        N = 625
        E = 10000
        D = 768
        H = 4
        C = D // H
        NEG_SLOPE = 0.2

        def gat_layer(x, src, dst, W, a_src, a_dst, b):
            h = (x @ W).reshape(-1, H, C)
            as_ = jnp.sum(h * a_src, axis=-1)
            ad_ = jnp.sum(h * a_dst, axis=-1)
            e = jax.nn.leaky_relu(as_[src] + ad_[dst], NEG_SLOPE)
            m = jax.ops.segment_max(e, dst, num_segments=N)
            e = jnp.exp(e - m[dst])
            s = jax.ops.segment_sum(e, dst, num_segments=N)
            alpha = e / s[dst]
            msg = h[src] * alpha[:, :, None]
            out = jax.ops.segment_sum(msg, dst, num_segments=N)
            return out.reshape(-1, H * C) + b
        key = jax.random.key(seed)
        ks = jax.random.split(key, 10)
        x = jax.random.normal(ks[0], (N, D), dtype=jnp.float32)
        edge_index = jax.random.randint(ks[1], (2, E), 0, N, dtype=jnp.int64)
        sc = 0.05
        W1 = jax.random.normal(ks[2], (D, H * C), dtype=jnp.float32) * sc
        a_src1 = jax.random.normal(ks[3], (H, C), dtype=jnp.float32) * sc
        a_dst1 = jax.random.normal(ks[4], (H, C), dtype=jnp.float32) * sc
        b1 = jnp.zeros((H * C,), dtype=jnp.float32)
        W2 = jax.random.normal(ks[5], (H * C, H * C), dtype=jnp.float32) * sc
        a_src2 = jax.random.normal(ks[6], (H, C), dtype=jnp.float32) * sc
        a_dst2 = jax.random.normal(ks[7], (H, C), dtype=jnp.float32) * sc
        b2 = jnp.zeros((H * C,), dtype=jnp.float32)
        return {'x': x, 'edge_index': edge_index, 'W1': W1, 'a_src1': a_src1, 'a_dst1': a_dst1, 'b1': b1, 'W2': W2, 'a_src2': a_src2, 'a_dst2': a_dst2, 'b2': b2}
    _L3_gnn_all = _L3_gnn_setup()
    _L3_gnn_in = {k: v for k, v in _L3_gnn_all.items() if k in ('W1', 'a_src1', 'a_dst1', 'b1', 'W2', 'a_src2', 'a_dst2', 'b2')}
    del _L3_gnn_all

    def _L3_ffn_setup():
        import jax, jax.numpy as jnp
        import numpy as np
        B, S, H = (4, 256, 768)
        E, K = (8, 2)
        key = jax.random.key(seed)
        ks = jax.random.split(key, 5)
        scale = 1.0 / np.sqrt(H)
        x = jax.random.normal(ks[0], (B, S, H), dtype=jnp.float32)
        router_w = jax.random.uniform(ks[1], (E, H), jnp.float32, -scale, scale)
        router_b = jax.random.uniform(ks[2], (E,), jnp.float32, -scale, scale)
        expert_w = jax.random.uniform(ks[3], (E, H, H), jnp.float32, -scale, scale)
        expert_b = jax.random.uniform(ks[4], (E, H), jnp.float32, -scale, scale)
        return {'x': x, 'router_w': router_w, 'router_b': router_b, 'expert_w': expert_w, 'expert_b': expert_b}
    _L3_ffn_all = _L3_ffn_setup()
    _L3_ffn_in = {k: v for k, v in _L3_ffn_all.items() if k in ('router_w', 'router_b', 'expert_w', 'expert_b')}
    del _L3_ffn_all
    return {'x': x, 'src': src, 'dst': dst, 'L0_gnn_W1s': _L0_gnn_in['W1s'], 'L0_gnn_b1s': _L0_gnn_in['b1s'], 'L0_gnn_W1d': _L0_gnn_in['W1d'], 'L0_gnn_b1d': _L0_gnn_in['b1d'], 'L0_gnn_attn1': _L0_gnn_in['attn1'], 'L0_gnn_ln1_w': _L0_gnn_in['ln1_w'], 'L0_gnn_ln1_b': _L0_gnn_in['ln1_b'], 'L0_gnn_Wos': _L0_gnn_in['Wos'], 'L0_gnn_bos': _L0_gnn_in['bos'], 'L0_gnn_Wod': _L0_gnn_in['Wod'], 'L0_gnn_bod': _L0_gnn_in['bod'], 'L0_gnn_attno': _L0_gnn_in['attno'], 'L0_gnn_lno_w': _L0_gnn_in['lno_w'], 'L0_gnn_lno_b': _L0_gnn_in['lno_b'], 'L0_ffn_router_w': _L0_ffn_in['router_w'], 'L0_ffn_router_b': _L0_ffn_in['router_b'], 'L0_ffn_w1': _L0_ffn_in['w1'], 'L0_ffn_b1': _L0_ffn_in['b1'], 'L0_ffn_w2': _L0_ffn_in['w2'], 'L0_ffn_b2': _L0_ffn_in['b2'], 'L1_gnn_W1': _L1_gnn_in['W1'], 'L1_gnn_att_src1': _L1_gnn_in['att_src1'], 'L1_gnn_att_dst1': _L1_gnn_in['att_dst1'], 'L1_gnn_b1': _L1_gnn_in['b1'], 'L1_gnn_W2': _L1_gnn_in['W2'], 'L1_gnn_att_src2': _L1_gnn_in['att_src2'], 'L1_gnn_att_dst2': _L1_gnn_in['att_dst2'], 'L1_gnn_b2': _L1_gnn_in['b2'], 'L1_ffn_w_in': _L1_ffn_in['w_in'], 'L1_ffn_g_in': _L1_ffn_in['g_in'], 'L1_ffn_w_out': _L1_ffn_in['w_out'], 'L1_ffn_g_out': _L1_ffn_in['g_out'], 'L2_gnn_W': _L2_gnn_in['W'], 'L2_gnn_b': _L2_gnn_in['b'], 'L2_ffn_gate_w': _L2_ffn_in['gate_w'], 'L2_ffn_gate_b': _L2_ffn_in['gate_b'], 'L2_ffn_w1': _L2_ffn_in['w1'], 'L2_ffn_b1': _L2_ffn_in['b1'], 'L2_ffn_w2': _L2_ffn_in['w2'], 'L2_ffn_b2': _L2_ffn_in['b2'], 'L3_gnn_W1': _L3_gnn_in['W1'], 'L3_gnn_a_src1': _L3_gnn_in['a_src1'], 'L3_gnn_a_dst1': _L3_gnn_in['a_dst1'], 'L3_gnn_b1': _L3_gnn_in['b1'], 'L3_gnn_W2': _L3_gnn_in['W2'], 'L3_gnn_a_src2': _L3_gnn_in['a_src2'], 'L3_gnn_a_dst2': _L3_gnn_in['a_dst2'], 'L3_gnn_b2': _L3_gnn_in['b2'], 'L3_ffn_router_w': _L3_ffn_in['router_w'], 'L3_ffn_router_b': _L3_ffn_in['router_b'], 'L3_ffn_expert_w': _L3_ffn_in['expert_w'], 'L3_ffn_expert_b': _L3_ffn_in['expert_b']}

def reference(x, src, dst, L0_gnn_W1s, L0_gnn_b1s, L0_gnn_W1d, L0_gnn_b1d, L0_gnn_attn1, L0_gnn_ln1_w, L0_gnn_ln1_b, L0_gnn_Wos, L0_gnn_bos, L0_gnn_Wod, L0_gnn_bod, L0_gnn_attno, L0_gnn_lno_w, L0_gnn_lno_b, L0_ffn_router_w, L0_ffn_router_b, L0_ffn_w1, L0_ffn_b1, L0_ffn_w2, L0_ffn_b2, L1_gnn_W1, L1_gnn_att_src1, L1_gnn_att_dst1, L1_gnn_b1, L1_gnn_W2, L1_gnn_att_src2, L1_gnn_att_dst2, L1_gnn_b2, L1_ffn_w_in, L1_ffn_g_in, L1_ffn_w_out, L1_ffn_g_out, L2_gnn_W, L2_gnn_b, L2_ffn_gate_w, L2_ffn_gate_b, L2_ffn_w1, L2_ffn_b1, L2_ffn_w2, L2_ffn_b2, L3_gnn_W1, L3_gnn_a_src1, L3_gnn_a_dst1, L3_gnn_b1, L3_gnn_W2, L3_gnn_a_src2, L3_gnn_a_dst2, L3_gnn_b2, L3_ffn_router_w, L3_ffn_router_b, L3_ffn_expert_w, L3_ffn_expert_b):
    import jax
    import jax.numpy as jnp

    def _L0_gnn_ref(x, src, dst, W1s, b1s, W1d, b1d, attn1, ln1_w, ln1_b, Wos, bos, Wod, bod, attno, lno_w, lno_b):
        import jax, jax.numpy as jnp
        import numpy as np
        N, E, DIM, HEADS = (625, 10000, 768, 8)
        HD = DIM // HEADS
        EPS = 1e-05

        def layer_norm(x, w, b):
            mu = jnp.mean(x, axis=-1, keepdims=True)
            var = jnp.var(x, axis=-1, keepdims=True)
            return (x - mu) * jax.lax.rsqrt(var + EPS) * w + b

        def gatv2(x, src, dst, Ws, bs, Wd, bd, attn):
            H, D = attn.shape
            fs = (x @ Ws + bs).reshape(-1, H, D)
            fd = (x @ Wd + bd).reshape(-1, H, D)
            e = jax.nn.leaky_relu(fs[src] + fd[dst], 0.2)
            logits = jnp.einsum('ehd,hd->eh', e, attn)
            m = jax.ops.segment_max(logits, dst, num_segments=N)
            ex = jnp.exp(logits - m[dst])
            denom = jax.ops.segment_sum(ex, dst, num_segments=N)
            alpha = ex / denom[dst]
            out = jax.ops.segment_sum(alpha[:, :, None] * fs[src], dst, num_segments=N)
            return jax.nn.elu(out)
        h = gatv2(x, src, dst, W1s, b1s, W1d, b1d, attn1).reshape(N, DIM)
        h = layer_norm(h + x, ln1_w, ln1_b)
        out = gatv2(h, src, dst, Wos, bos, Wod, bod, attno).reshape(N, DIM)
        return layer_norm(out, lno_w, lno_b)

    def _L0_ffn_ref(x, router_w, router_b, w1, b1, w2, b2):
        import jax, jax.numpy as jnp
        import numpy as np
        TOP_K = 2
        E = w1.shape[0]
        logits = jnp.einsum('bsd,de->bse', x, router_w) + router_b
        probs = jax.nn.softmax(logits, axis=-1)
        top_p, top_i = jax.lax.top_k(probs, TOP_K)
        top_p = top_p / jnp.sum(top_p, axis=-1, keepdims=True)
        combine = jnp.sum(jax.nn.one_hot(top_i, E, dtype=x.dtype) * top_p[..., None], axis=-2)
        out = jnp.zeros_like(x)
        for e in range(E):
            h = jax.nn.gelu(jnp.einsum('bsd,df->bsf', x, w1[e]) + b1[e], approximate=False)
            y = jnp.einsum('bsf,fd->bsd', h, w2[e]) + b2[e]
            out = out + combine[..., e:e + 1] * y
        return out

    def _L1_gnn_ref(x, edge_index, W1, att_src1, att_dst1, b1, W2, att_src2, att_dst2, b2):
        import jax, jax.numpy as jnp
        import numpy as np
        N_NODES = 10000
        NEG_SLOPE = 0.2
        EPS = 1e-16

        def gat_layer(x, W, att_src, att_dst, bias, src, dst, heads, out_ch, concat):
            n = x.shape[0]
            h = (x @ W.T).reshape(n, heads, out_ch)
            a_src = jnp.einsum('nhc,hc->nh', h, att_src)
            a_dst = jnp.einsum('nhc,hc->nh', h, att_dst)
            e = a_src[src] + a_dst[dst]
            e = jax.nn.leaky_relu(e, NEG_SLOPE)
            m = jax.ops.segment_max(e, dst, num_segments=n)
            ex = jnp.exp(e - m[dst])
            denom = jax.ops.segment_sum(ex, dst, num_segments=n)
            alpha = ex / (denom[dst] + EPS)
            msg = alpha[:, :, None] * h[src]
            out = jax.ops.segment_sum(msg, dst, num_segments=n)
            if concat:
                out = out.reshape(n, heads * out_ch)
            else:
                out = out.mean(axis=1)
            return out + bias
        src, dst = (edge_index[0], edge_index[1])
        h = gat_layer(x, W1, att_src1, att_dst1, b1, src, dst, heads=8, out_ch=128, concat=True)
        h = jax.nn.relu(h)
        out = gat_layer(h, W2, att_src2, att_dst2, b2, src, dst, heads=1, out_ch=768, concat=True)
        return out

    def _L1_ffn_ref(x, w_in, g_in, w_out, g_out):
        import jax, jax.numpy as jnp
        import numpy as np
        EPS_NORM = 1e-06
        EPS_Q = 1e-05

        def rmsnorm(x, g):
            return x * jax.lax.rsqrt(jnp.mean(x * x, axis=-1, keepdims=True) + EPS_NORM) * g

        def activation_quant(x):
            scale = 127.0 / jnp.maximum(jnp.max(jnp.abs(x), axis=-1, keepdims=True), EPS_Q)
            return jnp.clip(jnp.round(x * scale), -128, 127) / scale

        def weight_quant(w):
            scale = 1.0 / jnp.maximum(jnp.mean(jnp.abs(w)), EPS_Q)
            return jnp.clip(jnp.round(w * scale), -1, 1) / scale

        def bitlinear(x, w, g):
            x_norm = rmsnorm(x, g)
            x_q = x_norm + jax.lax.stop_gradient(activation_quant(x_norm) - x_norm)
            w_q = w + jax.lax.stop_gradient(weight_quant(w) - w)
            return jnp.einsum('bsd,od->bso', x_q, w_q)
        h = bitlinear(x, w_in, g_in)
        up, gate = jnp.split(h, 2, axis=-1)
        y = jax.nn.silu(gate) * up
        return bitlinear(y, w_out, g_out)

    def _L2_gnn_ref(x, edge_index, W, b):
        import jax, jax.numpy as jnp
        import numpy as np
        N_NODES = 10000
        n = x.shape[0]
        loops = jnp.arange(n, dtype=edge_index.dtype)
        row = jnp.concatenate([edge_index[0], loops])
        col = jnp.concatenate([edge_index[1], loops])
        ones = jnp.ones(row.shape[0], dtype=x.dtype)
        deg = jax.ops.segment_sum(ones, col, num_segments=n)
        dinv = jnp.where(deg > 0, jax.lax.rsqrt(deg), 0.0)
        norm = dinv[row] * dinv[col]
        h = x @ W
        msg = h[row] * norm[:, None]
        out = jax.ops.segment_sum(msg, col, num_segments=n) + b
        return out

    def _L2_ffn_ref(x, gate_w, gate_b, w1, b1, w2, b2):
        import jax, jax.numpy as jnp
        import numpy as np
        B, S, H, F, E = (8, 512, 768, 96, 6)
        TOP_K = 2
        b, s, h = x.shape
        xf = x.reshape(-1, h)
        gate_scores = xf @ gate_w + gate_b
        topk_scores, topk_idx = jax.lax.top_k(gate_scores, TOP_K)
        topk_weights = jax.nn.softmax(topk_scores, axis=1)
        hmid = jax.nn.gelu(jnp.einsum('nh,ehf->nef', xf, w1) + b1, approximate=False)
        expert_out = jnp.einsum('nef,efh->neh', hmid, w2) + b2
        sel = jnp.take_along_axis(expert_out, topk_idx[:, :, None], axis=1)
        out = jnp.einsum('nk,nkh->nh', topk_weights, sel)
        return out.reshape(b, s, h)

    def _L3_gnn_ref(x, edge_index, W1, a_src1, a_dst1, b1, W2, a_src2, a_dst2, b2):
        import jax, jax.numpy as jnp
        import numpy as np
        N = 625
        E = 10000
        D = 768
        H = 4
        C = D // H
        NEG_SLOPE = 0.2

        def gat_layer(x, src, dst, W, a_src, a_dst, b):
            h = (x @ W).reshape(-1, H, C)
            as_ = jnp.sum(h * a_src, axis=-1)
            ad_ = jnp.sum(h * a_dst, axis=-1)
            e = jax.nn.leaky_relu(as_[src] + ad_[dst], NEG_SLOPE)
            m = jax.ops.segment_max(e, dst, num_segments=N)
            e = jnp.exp(e - m[dst])
            s = jax.ops.segment_sum(e, dst, num_segments=N)
            alpha = e / s[dst]
            msg = h[src] * alpha[:, :, None]
            out = jax.ops.segment_sum(msg, dst, num_segments=N)
            return out.reshape(-1, H * C) + b
        loop = jnp.arange(N, dtype=edge_index.dtype)
        src = jnp.concatenate([edge_index[0], loop])
        dst = jnp.concatenate([edge_index[1], loop])
        h = gat_layer(x, src, dst, W1, a_src1, a_dst1, b1)
        h = jax.nn.relu(h)
        out = gat_layer(h, src, dst, W2, a_src2, a_dst2, b2)
        return out

    def _L3_ffn_ref(x, router_w, router_b, expert_w, expert_b):
        import jax, jax.numpy as jnp
        import numpy as np
        B, S, H = (4, 256, 768)
        E, K = (8, 2)
        scores = jnp.einsum('bsh,eh->bse', x, router_w) + router_b
        probs = jax.nn.softmax(scores, axis=-1)
        top_probs, expert_ids = jax.lax.top_k(probs, K)
        y = jnp.einsum('bsh,edh->bsed', x, expert_w) + expert_b
        out_k = jnp.take_along_axis(y, expert_ids[..., None], axis=2)
        w = top_probs / (jnp.sum(top_probs, axis=-1, keepdims=True) + 1e-09)
        out = jnp.einsum('bsk,bskh->bsh', w, out_k)
        return out
    edge_index = jnp.stack([src, dst])
    x = x + _L0_gnn_ref(_layernorm(x, axis=-1), src, dst, L0_gnn_W1s, L0_gnn_b1s, L0_gnn_W1d, L0_gnn_b1d, L0_gnn_attn1, L0_gnn_ln1_w, L0_gnn_ln1_b, L0_gnn_Wos, L0_gnn_bos, L0_gnn_Wod, L0_gnn_bod, L0_gnn_attno, L0_gnn_lno_w, L0_gnn_lno_b)
    x = x + _L0_ffn_ref(_layernorm(x, axis=-1)[None], L0_ffn_router_w, L0_ffn_router_b, L0_ffn_w1, L0_ffn_b1, L0_ffn_w2, L0_ffn_b2)[0]
    x = x + _L1_gnn_ref(_layernorm(x, axis=-1), edge_index, L1_gnn_W1, L1_gnn_att_src1, L1_gnn_att_dst1, L1_gnn_b1, L1_gnn_W2, L1_gnn_att_src2, L1_gnn_att_dst2, L1_gnn_b2)
    x = x + _L1_ffn_ref(_layernorm(x, axis=-1)[None], L1_ffn_w_in, L1_ffn_g_in, L1_ffn_w_out, L1_ffn_g_out)[0]
    x = x + _L2_gnn_ref(_layernorm(x, axis=-1), edge_index, L2_gnn_W, L2_gnn_b)
    x = x + _L2_ffn_ref(_layernorm(x, axis=-1)[None], L2_ffn_gate_w, L2_ffn_gate_b, L2_ffn_w1, L2_ffn_b1, L2_ffn_w2, L2_ffn_b2)[0]
    x = x + _L3_gnn_ref(_layernorm(x, axis=-1), edge_index, L3_gnn_W1, L3_gnn_a_src1, L3_gnn_a_dst1, L3_gnn_b1, L3_gnn_W2, L3_gnn_a_src2, L3_gnn_a_dst2, L3_gnn_b2)
    x = x + _L3_ffn_ref(_layernorm(x, axis=-1)[None], L3_ffn_router_w, L3_ffn_router_b, L3_ffn_expert_w, L3_ffn_expert_b)[0]
    return x

_drawn_inputs = setup_inputs


def setup_inputs(seed=0):
    import zlib

    import numpy as np

    out = dict(_drawn_inputs(seed))
    spreads = {'L0_gnn_b1s': (0.0, 0.1),
     'L0_gnn_b1d': (0.0, 0.546),
     'L0_gnn_ln1_w': (1.0, 0.2),
     'L0_gnn_ln1_b': (0.0, 0.1),
     'L0_gnn_bos': (0.0, 0.1),
     'L0_gnn_bod': (0.0, 0.1),
     'L0_gnn_lno_w': (1.0, 0.2),
     'L0_gnn_lno_b': (0.0, 0.1),
     'L0_ffn_router_b': (0.0, 0.1),
     'L0_ffn_b1': (0.0, 0.1),
     'L0_ffn_b2': (0.0, 0.1),
     'L1_gnn_b1': (0.0, 0.1),
     'L1_gnn_b2': (0.0, 0.1),
     'L1_ffn_g_in': (1.0, 0.6),
     'L1_ffn_g_out': (1.0, 0.6),
     'L2_gnn_b': (0.0, 0.1),
     'L3_gnn_b1': (0.0, 0.1),
     'L3_gnn_b2': (0.0, 0.1)}
    factors = {'L1_gnn_att_dst1': 4.15,
     'L1_gnn_att_src2': 4.409,
     'L1_gnn_att_dst2': 8.0,
     'L1_ffn_w_in': 3.625,
     'L1_ffn_w_out': 4.777,
     'L2_ffn_gate_b': 3.399,
     'L2_ffn_b1': 8.0,
     'L2_ffn_b2': 6.622,
     'L3_gnn_a_dst1': 3.915,
     'L3_gnn_a_src2': 4.807,
     'L3_gnn_a_dst2': 8.0,
     'L3_ffn_expert_b': 7.06}
    for name, (base, spread) in spreads.items():
        noise = np.random.default_rng([zlib.crc32(name.encode()), seed]).standard_normal(out[name].shape)
        drawn = base * np.exp(spread * noise) if base else spread * noise
        out[name] = jnp.asarray(drawn.astype(out[name].dtype))
    for name, factor in factors.items():
        out[name] = (out[name] * factor).astype(out[name].dtype)
    return out
```

```python
from contextlib import ExitStack

import numpy as np

import concourse.bass as bass
from concourse import mybir

F32 = mybir.dt.float32
BF16 = mybir.dt.bfloat16
I32 = mybir.dt.int32
U32 = mybir.dt.uint32
ACT = mybir.ActivationFunctionType
ALU = mybir.AluOpType
AX_X = mybir.AxisListType.X

P = 128
N = 625
R = 125
T = N // R
D = 768
KD = D // P
E = 20000
ET = -(-E // P)
ETP = 160
EU = 8
GW = D + 8
FF = 3072
FC = 4
NG = FF // (P * FC)
G1 = KD * FC * P + FC
G2 = FC * D
HALF = 313
HALVES = ((0, HALF), (HALF, N))
NEGBIG = -1.0e30
TINY = 1.0e-16
LN_EPS = 1.0e-5
ROUND = 12582912.0


def count_segments():
    out = []
    for c in range(T):
        a, end = c * N, (c + 1) * N
        while a < end:
            b = min(end, (a // 512 + 1) * 512)
            out.append((c, a, b, a % 512 == 0))
            a = b
    return out


HEADS = [
    dict(h=8, c=96, kind="table"),
    dict(h=1, c=768, kind="table"),
    dict(h=8, c=128, kind="gat"),
    dict(h=1, c=768, kind="gat"),
    dict(h=1, c=768, kind="average"),
    dict(h=4, c=192, kind="gat"),
    dict(h=4, c=192, kind="gat"),
]
LINEARS = [
    (6, 768, 0), (6, 768, 0), (6, 768, 1), (6, 768, 1),
    (6, 1024, 3), (8, 768, 4), (6, 768, 6),
    (6, 768, 8), (6, 768, 9),
]
LIN_HALF = [n // 2 for _, n, _ in LINEARS]
TR_CHUNKS = [6, 6, 6, 6, 8, 6, 6, 6, 6, 6, 6]


LINEARS_DONE = [2, 4, 5, 6, 7, 8, 9]
MG1 = 8 * NG * FC * 2
MB1 = 8 * NG * T
MB3 = MB1 + 6 * T
RS_COUNT = [0, 3, 4, 5, 8, 10, 11, 12, 13]


def unit_place(n):
    if n == 0:
        return lambda s: (s % 8, s // 8)
    return lambda s: (s // T, s % T)


def units_before(n, kinds):
    return sum(T * s["h"] for s in HEADS[:n] if s["kind"] in kinds)


def build(nc, ins, out, sections=8):
    ctx = ExitStack()
    with ctx:
        def sb(name, shape, dt=F32):
            return ctx.enter_context(nc.sbuf_tensor(name, shape, dt))

        def sem(name):
            return ctx.enter_context(nc.semaphore(name))

        def wait(eng, s, value):
            if isinstance(value, int) and value <= 0:
                return
            eng.wait_ge(s, value)

        src_rows = nc.dram_tensor("src_rows", [N, GW], F32, kind="Internal").ap()
        dst_rows = nc.dram_tensor("dst_rows", [N, GW], F32, kind="Internal").ap()
        logits8 = nc.dram_tensor("logits8", [N * N, 8], F32, kind="Internal").ap()
        logits1 = nc.dram_tensor("logits1", [N * N, 1], F32, kind="Internal").ap()
        tables = [logits8, logits1]

        X = sb("X", [R, T, D])
        XN = sb("XN", [R, T, D])
        XT = sb("XT", [P, 8, N])
        F = sb("F", [P, T, 1024])
        O = sb("O", [P, T, 1024])
        C = sb("C", [R, T, N])
        NEG = sb("NEG", [R, T, N])
        WB = sb("WB", [P, 2 * (G1 + G2)])
        PB = sb("PB", [P, 3840])
        W = sb("W", [P, 4, N])
        PT = sb("PT", [P, 2, T, R])
        idx = sb("idx", [P, ETP, 2], I32)
        key = sb("key", [P, ETP], I32)
        idf = sb("idf", [P, 2, ETP])
        ident = sb("ident", [P, P])
        AT = sb("AT", [8, T, R])
        attc = sb("attc", [P, 2, KD])
        hmask = sb("hmask", [P, 2, KD, 8])
        blk = sb("blk", [P, 2, KD, 8])
        iota8 = sb("iota8", [P, 8])
        stats = sb("stats", [R, T, 2, 6])
        mv = sb("mv", [R, T, 2])
        var = sb("var", [R, T])
        rstd = sb("rstd", [R, T])
        mhalf = sb("mhalf", [R, T])
        a_s = sb("a_s", [R, T, 8])
        a_d = sb("a_d", [R, T, 8])
        mx = sb("mx", [R, 4])
        nmx = sb("nmx", [R, 4])
        den = sb("den", [R, 4])
        rden = sb("rden", [R, 8])
        dinv = sb("dinv", [R, T])
        ixr = sb("ixr", [P, EU, 3], I32)
        lgr = sb("lgr", [P, EU, 8])
        rw = sb("rw", [P, KD, 8])
        rb = sb("rb", [R, 8])
        LG = sb("LG", [R, T, 8])
        top = sb("top", [R, T, 8])
        topi = sb("topi", [R, T, 8], U32)
        topf = sb("topf", [R, T, 8])
        gate = sb("gate", [R, 8, T])
        comb = sb("comb", [R, T, 8])
        comb2 = sb("comb2", [R, T, 8])
        mixb = sb("mixb", [8, D])
        ones = sb("ones", [P, P])
        bs = sb("bs", [P, 16, T])
        ws = sb("ws", [P, 8])

        Fz = F[:, :, :].rearrange("p t c -> p (t c)")
        Oz = O[:, :, :].rearrange("p t c -> p (t c)")
        iota = Fz[:, 0:626]
        oh = WB[:, 0:1252].bitcast(BF16).rearrange("p (u s n) -> p u s n", u=2, s=2)
        gs = WB[:, 0:4 * GW].rearrange("p (u c) -> p u c", u=4)
        gd = WB[:, 4 * GW:8 * GW].rearrange("p (u c) -> p u c", u=4)
        zr = WB[:, 8 * GW:8 * GW + 2 * D].rearrange("p (u k c) -> p u k c", u=2, k=KD)
        ltile = WB[0:R, 0:10000].rearrange("p (u n h) -> p u n h", u=2, h=8)
        ltile1 = WB[0:R, 0:T * N].rearrange("p (t n) -> p t n", t=T)
        wlin = [WB[:, 6144 * u:6144 * (u + 1)] for u in range(2)]
        TMP = W[:, :, :].rearrange("p a b -> p (a b)")[0:R, 0:1024]
        TMP2 = W[:, :, :].rearrange("p a b -> p (a b)")[0:R, 1024:2048]
        Cz = C[:, :, :].rearrange("p t n -> p (t n)")
        NEGz = NEG[:, :, :].rearrange("p t n -> p (t n)")

        hidT = WB[0:64, 3072:3072 + N].rearrange("p (t n) -> p t n", t=T)

        def par(slot, width, w=None):
            return PB[0:R, slot * width:slot * width + (w or width)]

        PS = ctx.enter_context(nc.psum_tensor("PS", [P, 8, 512], F32))
        PSz = PS[:, :, :].rearrange("p b n -> p (b n)")

        s_const = sem("consts_loaded")
        s_x = sem("x_loaded")
        s_idx = sem("edges_loaded")
        s_keys = sem("edge_keys_ready")
        s_zero = sem("zeros_ready")
        s_zeroed = sem("tables_zeroed")
        s_oh = sem("onehots_ready")
        s_ohu = sem("onehots_used")
        s_cnt = sem("counts_ready")
        s_link = sem("vector_link")
        s_mh = sem("minus_half_ready")
        s_var = sem("variances_ready")
        s_rstd = sem("rstds_ready")
        s_rows = sem("rows_ready")
        s_trp = sem("transposed_in_psum")
        s_trc = sem("transposed_copied")
        s_par = sem("params_loaded")
        s_pfree = sem("params_used")
        s_wl = [sem(f"linear_weights{u}") for u in range(2)]
        s_linp = sem("linear_in_psum")
        s_line = sem("linear_evacuated")
        s_frow = sem("table_rows_ready")
        s_tab = sem("tables_written")
        s_ends = sem("node_numbers_copied")
        s_kc = sem("pair_numbers_copied")
        s_gat = [sem(f"rows_gathered{u}") for u in range(4)]
        s_z = sem("edge_sums_ready")
        s_zt = sem("edge_sums_transposed")
        s_zr = sem("edge_relus_ready")
        s_dot = sem("edge_dots_ready")
        s_lg = sem("edge_logits_ready")
        s_sc = sem("edge_logits_scattered")
        s_lt = [sem(f"logit_tile_loaded{u}") for u in range(2)]
        s_att = sem("attention_terms_ready")
        s_astp = sem("terms_transposed")
        s_ast = sem("terms_copied")
        s_bc = sem("source_terms_broadcast")
        s_v = sem("edge_terms_ready")
        s_lm = sem("masked_logits_ready")
        s_e = sem("exps_ready")
        s_p = sem("weights_ready")
        s_tp = sem("weights_transposed")
        s_pt = sem("weights_copied")
        s_op = sem("sums_in_psum")
        s_out = sem("sums_evacuated")
        s_neg = sem("negative_parts_ready")
        s_elu = sem("elu_exps_ready")
        s_rw = sem("router_loaded")
        s_rtp = sem("router_in_psum")
        s_gap = sem("router_gaps_ready")
        s_gex = sem("router_exps_ready")
        s_comb = sem("mixture_weights_ready")
        s_mbt = sem("mixture_weights_transposed")
        s_mbc = sem("mixture_weights_copied")
        s_mixp = sem("bias_mix_in_psum")
        s_mixd = sem("bias_mix_added")
        s_mw = [sem(f"expert_weights{u}") for u in range(2)]
        s_ma = sem("hidden_in_psum")
        s_mg = sem("hidden_ready")
        s_mb = sem("expert_in_psum")
        s_md = sem("expert_added")
        s_m2w = sem("small_experts_loaded")
        s_m3w = [sem(f"square_expert_weights{u}") for u in range(2)]
        s_bw = sem("bit_weights_loaded")
        s_bclr = sem("bit_sums_cleared")
        s_babs = sem("bit_weight_sums_ready")
        s_bpe = sem("bit_products_ready")
        s_bwq = sem("bit_weights_rounded")
        s_by = sem("bit_rows_normalised")
        s_bya = sem("bit_rows_absolute")
        s_bh = sem("bit_hidden_ready")
        s_bsil = sem("bit_silu_ready")
        s_by2 = sem("bit_hidden_normalised")
        s_bq2 = sem("bit_hidden_rounded")
        s_bqt = sem("bit_hidden_transposed")
        s_bout = sem("bit_output_in_psum")
        s_badd = sem("bit_output_added")
        s_sec = sem("section_done")
        s_store = sem("output_stored")

        block = ctx.enter_context(nc.Block())

        PARAMS = [
            (768, ["L0_gnn_b1s", "L0_gnn_b1d", "L0_gnn_attn1", "L0_gnn_ln1_w", "L0_gnn_ln1_b"]),
            (768, ["L0_gnn_bos", "L0_gnn_bod", "L0_gnn_attno", "L0_gnn_lno_w", "L0_gnn_lno_b"]),
            (1024, ["L1_gnn_att_src1", "L1_gnn_att_dst1", "L1_gnn_b1"]),
            (768, ["L1_gnn_att_src2", "L1_gnn_att_dst2", "L1_gnn_b2"]),
            (768, ["L1_ffn_g_in", "L1_ffn_g_out"]),
            (768, ["L2_gnn_b"]),
            (768, ["L3_gnn_a_src1", "L3_gnn_a_dst1", "L3_gnn_b1"]),
            (768, ["L3_gnn_a_src2", "L3_gnn_a_dst2", "L3_gnn_b2"]),
        ]
        par_total = np.cumsum([0] + [len(p) for _, p in PARAMS]).tolist()
        LIN_W = ["L0_gnn_W1s", "L0_gnn_W1d", "L0_gnn_Wos", "L0_gnn_Wod", "L1_gnn_W1", "L1_gnn_W2",
                 "L2_gnn_W", "L3_gnn_W1", "L3_gnn_W2"]
        ROUTERS = [("L0_ffn_router_w", "L0_ffn_router_b"), ("L2_ffn_gate_w", "L2_ffn_gate_b"),
                   ("L3_ffn_router_w", "L3_ffn_router_b")]
        MIXB = ["L0_ffn_b2", "L2_ffn_b2", "L3_ffn_expert_b"]
        N_EXP = [8, 6, 8]

        @block.sync
        def _(sp):
            def params(g):
                wait(sp, s_pfree, g)
                width, names = PARAMS[g]
                for k, name in enumerate(names):
                    n = ins[name].shape[1]
                    sp.dma_start(PB[0:R, k * width:k * width + n], ins[name].to_broadcast([R, n]))\
                      .then_inc(s_par, 16)

            def linear_weights(n):
                k, width, _ = LINEARS[n]
                sp.dma_start(wlin[n % 2][:, 0:k * width], ins[LIN_W[n]]).then_inc(s_wl[n % 2], 16)

            def router(n):
                if n:
                    sp.wait_ge(s_mixp, T * n)
                    sp.wait_ge(s_comb, n)
                sp.dma_start(rw[:, :, 0:N_EXP[n]], ins[ROUTERS[n][0]]).then_inc(s_rw, 16)
                sp.dma_start(rb[:, 0:N_EXP[n]], ins[ROUTERS[n][1]].to_broadcast([R, N_EXP[n]])).then_inc(s_rw, 16)
                sp.dma_start(mixb[0:N_EXP[n], :], ins[MIXB[n]]).then_inc(s_rw, 16)

            sp.dma_start(iota, ins["iota"]).then_inc(s_const, 16)
            sp.dma_start(idx[:], ins["edges"]).then_inc(s_idx, 16)
            sp.dma_start(X[:], ins["x"].rearrange("(t p) d -> p t d", p=R)).then_inc(s_x, 16)
            for t, name in ((ident[:], "ident"), (iota8[:], "iota8"), (attc[:], "attc"), (hmask[:], "hmask")):
                sp.dma_start(t, ins[name]).then_inc(s_const, 16)
            sp.wait_ge(s_zero, 1)
            zeros = Oz[0:R, 0:5000]
            flat8 = logits8.rearrange("(a p b) h -> a p (b h)", p=R, a=5)
            for a in range(5):
                sp.dma_start(flat8[a], zeros).then_inc(s_zeroed, 16)
            sp.dma_start(logits1.rearrange("(p b) h -> p (b h)", p=R), zeros[:, 0:T * N]).then_inc(s_zeroed, 16)

            sp.wait_ge(s_ohu, ET)
            for g in range(2):
                params(g)
                for side in range(2):
                    n = 2 * g + side
                    if g:
                        sp.wait_ge(s_out, units_before(g, ("table",)))
                    linear_weights(n)
                for side, table in enumerate((src_rows, dst_rows)):
                    for t in range(T):
                        sp.wait_ge(s_frow, T * (2 * g + side) + t + 1)
                        rows = (F if side == 0 else O)[0:R, t, 0:GW]
                        sp.dma_start(table[t * R:(t + 1) * R, :], rows).then_inc(s_tab, 16)
                sp.wait_ge(s_sc, 16 * ETP * (g + 1))
                if g == 0:
                    for t in range(T):
                        if t >= 2:
                            sp.wait_ge(s_lm, 8 * (t - 1))
                        sp.dma_start(ltile[:, t % 2], logits8.rearrange("(t p n) h -> t p n h", t=T, p=R)[t])\
                          .then_inc(s_lt[t % 2], 16)
                else:
                    sp.dma_start(ltile1, logits1.rearrange("(t p n) h -> p t (n h)", t=T, p=R)).then_inc(s_lt[1], 16)
            if sections > 1:
                sp.wait_ge(s_sec, 1)
                router(0)
                for e in range(1):
                    for u in range(NG):
                        g = u
                        wait(sp, s_mb, T * (g - 1))
                        slot = u % 2
                        sp.dma_start(WB[:, G1 * slot:G1 * (slot + 1)], ins["L0_ffn_w1"][g])\
                          .then_inc(s_mw[slot], 16)
                        sp.dma_start(WB[:, 2 * G1 + G2 * slot:2 * G1 + G2 * (slot + 1)], ins["L0_ffn_w2"][g])\
                          .then_inc(s_mw[slot], 16)
                with sp.Fori(1, 8) as e:
                    for u in range(NG):
                        g = e * NG + u
                        sp.wait_ge(s_mb, e * (NG * T) + T * (u - 1))
                        slot = u % 2
                        sp.dma_start(WB[:, G1 * slot:G1 * (slot + 1)],
                                     ins["L0_ffn_w1"][bass.ds(g, 1)].rearrange("o p n -> p (o n)"))\
                          .then_inc(s_mw[slot], 16)
                        sp.dma_start(WB[:, 2 * G1 + G2 * slot:2 * G1 + G2 * (slot + 1)],
                                     ins["L0_ffn_w2"][bass.ds(g, 1)].rearrange("o p n -> p (o n)"))\
                          .then_inc(s_mw[slot], 16)
            if sections > 2:
                sp.wait_ge(s_sec, 2)
                params(2)
                linear_weights(4)
                linear_weights(5)
                params(3)
            if sections > 3:
                sp.wait_ge(s_sec, 3)
                params(4)
                sp.dma_start(WB[:, 0:768], ins["L1_ffn_w_in"]).then_inc(s_bw, 16)
                sp.dma_start(WB[0:64, 768:1536], ins["L1_ffn_w_out"]).then_inc(s_bw, 16)
            if sections > 4:
                sp.wait_ge(s_sec, 4)
                params(5)
                linear_weights(6)
            if sections > 5:
                sp.wait_ge(s_sec, 5)
                router(1)
                sp.dma_start(WB[:, 0:3456], ins["L2_ffn_w1"]).then_inc(s_m2w, 16)
                sp.dma_start(WB[0:96, 3456:3456 + 4608], ins["L2_ffn_w2"]).then_inc(s_m2w, 16)
                sp.dma_start(WB[0:96, 8064:8070], ins["L2_ffn_b1"]).then_inc(s_m2w, 16)
            if sections > 6:
                sp.wait_ge(s_sec, 6)
                params(6)
                linear_weights(7)
                linear_weights(8)
                params(7)
            if sections > 7:
                sp.wait_ge(s_sec, 7)
                router(2)
                for e in range(2):
                    sp.dma_start(WB[:, 4608 * e:4608 * (e + 1)], ins["L3_ffn_expert_w"][e]).then_inc(s_m3w[e], 16)
                with sp.Fori(1, 4) as j:
                    for u in range(2):
                        sp.wait_ge(s_mb, MB3 + j * (2 * T) + T * (u - 1))
                        sp.dma_start(WB[:, 4608 * u:4608 * (u + 1)],
                                     ins["L3_ffn_expert_w"][bass.ds(j * 2 + u, 1)].rearrange("o p n -> p (o n)"))\
                          .then_inc(s_m3w[u], 16)
            sp.wait_ge(s_sec, sections)
            sp.dma_start(out.rearrange("(t p) d -> p t d", p=R), X[:]).then_inc(s_store, 16)
            sp.wait_ge(s_store, 16)

        @block.gpsimd
        def _(pool):
            def rsqrt(n):
                pool.wait_ge(s_var, n + 1)
                pool.tensor_tensor(rstd[:], var[:], mhalf[:], ALU.pow).then_inc(s_rstd, 1)

            def edge_step(i, u, g, gather=True, scatter=True):
                base = ETP * g
                h = HEADS[g]["h"]
                if not gather:
                    pool.wait_ge(s_lg, base + i - LAG + 1)
                    pool.wait_ge(s_ends, ETP * (g + 1))
                    pool.wait_ge(s_kc, base + i - LAG + 1)
                    wait(pool, s_sc, 16 * (base + i - LAG))
                else:
                    wait(pool, s_lg, base + i - LAG + 1)
                    wait(pool, s_kc, base + i - LAG + 1)
                    wait(pool, s_sc, 16 * (base + i - LAG))
                    pool.tensor_copy(ixr[:, u, 0:2], idx[:, bass.ds(i, 1), :].rearrange("p o k -> p (o k)"))\
                        .then_inc(s_ends, 1)
                    pool.wait_ge(s_ends, base + i + 1)
                    pool.tensor_copy(ixr[:, u, 2:3], key[:, bass.ds(i, 1)]).then_inc(s_kc, 1)
                    pool.indirect_dma_start(
                        out=gs[:, u % 4, :], out_offset=None, in_=src_rows,
                        in_offset=bass.IndirectOffsetOnAxis(ap=ixr[:, u, 0:1], axis=0)).then_inc(s_gat[u % 4], 16)
                    pool.indirect_dma_start(
                        out=gd[:, u % 4, :], out_offset=None, in_=dst_rows,
                        in_offset=bass.IndirectOffsetOnAxis(ap=ixr[:, u, 1:2], axis=0)).then_inc(s_gat[u % 4], 16)
                if scatter:
                    v = (u - LAG) % EU
                    pool.indirect_dma_start(
                        out=tables[g], out_offset=bass.IndirectOffsetOnAxis(ap=ixr[:, v, 2:3], axis=0),
                        in_=lgr[:, v, 0:h], in_offset=None).then_inc(s_sc, 16)

            LAG = 4

            def edges(g):
                pool.wait_ge(s_tab, 16 * 2 * T * (g + 1))
                if g == 0:
                    pool.wait_ge(s_keys, 1)
                    pool.wait_ge(s_zeroed, 96)
                for i in range(EU):
                    edge_step(i, i, g, scatter=i >= LAG)
                with pool.Fori(1, ETP // EU) as j:
                    for u in range(EU):
                        edge_step(j * EU + u, u, g)
                for i in range(ETP, ETP + LAG):
                    edge_step(i, i % EU, g, gather=False)

            pool.wait_ge(s_mh, 1)
            rsqrt(0)
            edges(0)
            rsqrt(1)
            edges(1)
            rsqrt(2)
            for n in range(3, RS_COUNT[sections]):
                rsqrt(n)

        @block.tensor
        def _(pe):
            def counts():
                segs = count_segments()

                def tile_counts(i, slot, first, last, k):
                    pe.wait_ge(s_oh, i + 1)
                    for c, a, b, fresh in segs:
                        mm = pe.matmul(PSz[0:R, a:b], oh[0:k, slot, 1, c * R:(c + 1) * R],
                                       oh[0:k, slot, 0, a - c * N:b - c * N],
                                       start=(first and fresh), stop=last, skip_group_check=True)
                    mm.then_inc(s_ohu, 1)

                tile_counts(0, 0, True, False, P)
                tile_counts(1, 1, False, False, P)
                with pe.Fori(1, ET // 2) as j:
                    for u in range(2):
                        tile_counts(j * 2 + u, u, False, False, P)
                tile_counts(ET - 1, 0, False, True, E - (ET - 1) * P)

            def transpose_rows(n, src):
                per = TR_CHUNKS[n] // 2
                for t in range(T):
                    pe.wait_ge(s_rows, T * n + t + 1)
                    for half in range(2):
                        g = 2 * T * n + 2 * t + half
                        wait(pe, s_trc, g - 3)
                        for k in range(per):
                            kk = half * per + k
                            tr = pe.transpose(PS[:, g % 4, k * R:(k + 1) * R],
                                              src[0:R, t, kk * P:(kk + 1) * P], ident[0:R, 0:R])
                        tr.then_inc(s_trp, 1)

            def linear(n):
                kc, width, m = LINEARS[n]
                w = wlin[n % 2][:, 0:kc * width].rearrange("p (k c) -> p k c", k=kc)
                hw = width // 2
                pe.wait_ge(s_wl[n % 2], 16 * (n // 2 + 1))
                for t in range(T):
                    pe.wait_ge(s_trc, 2 * T * m + 2 * t + 2)
                    for half in range(2):
                        g = 2 * T * n + 2 * t + half
                        wait(pe, s_line, g - 3)
                        for k in range(kc):
                            mm = pe.matmul(PS[0:R, 4 + g % 4, 0:hw], XT[:, k, t * R:(t + 1) * R],
                                           w[:, k, half * hw:(half + 1) * hw], start=(k == 0), stop=(k == kc - 1))
                        mm.then_inc(s_linp, 1)

            def edge_turn(i, u, g):
                base = ETP * g
                pe.wait_ge(s_z, base + i + 1)
                wait(pe, s_zr, base + i - 1)
                for k in range(KD):
                    tr = pe.transpose(PSz[:, 1024 * (u % 2) + k * P:1024 * (u % 2) + (k + 1) * P],
                                      gs[:, u % 4, k * P:(k + 1) * P], ident[:])
                tr.then_inc(s_zt, 1)

            def edge_dot(i, u, g):
                base = ETP * g
                pe.wait_ge(s_zr, base + i + 1)
                wait(pe, s_lg, base + i - 1)
                for k in range(KD):
                    mm = pe.matmul(PS[:, 4 + u % 2, 0:8], zr[:, u % 2, k, :], blk[:, g, k, :],
                                   start=(k == 0), stop=(k == KD - 1))
                mm.then_inc(s_dot, 1)

            def edges(g):
                for i in range(EU):
                    edge_turn(i, i, g)
                    if i:
                        edge_dot(i - 1, i - 1, g)
                with pe.Fori(1, ETP // EU) as j:
                    for u in range(EU):
                        edge_turn(j * EU + u, u, g)
                        edge_dot(j * EU + (u - 1), (u - 1) % EU, g)
                edge_dot(ETP - 1, EU - 1, g)

            def attend(n):
                h, c, kind = HEADS[n]["h"], HEADS[n]["c"], HEADS[n]["kind"]
                soft = units_before(n, ("table", "gat"))
                gat = units_before(n, ("gat",))
                every = units_before(n, ("table", "gat", "average"))
                gats = sum(s["kind"] == "gat" for s in HEADS[:n])
                heads = sum(s["h"] for s in HEADS[:n] if s["kind"] == "gat")
                units = T * h
                place = unit_place(n)

                def broadcast(head):
                    wait(pe, s_v, gat + T * head)
                    for a, b in ((0, 512), (512, N)):
                        mm = pe.matmul(PSz[0:R, a:b], ident[0:h, head:head + 1].to_broadcast([h, R]),
                                       AT[0:h].rearrange("h t n -> h (t n)")[:, a:b], start=True, stop=True)
                    mm.then_inc(s_bc, 1)

                def turn(s):
                    t = place(s)[1]
                    if kind == "average":
                        src = C[:, t, :]
                    else:
                        pe.wait_ge(s_p, soft + s + 1)
                        src = W[0:R, s % 4, :]
                    wait(pe, s_pt, every + s - 1)
                    for b in range(T):
                        tr = pe.transpose(PSz[0:R, 1024 * (1 + s % 2) + b * P:1024 * (1 + s % 2) + b * P + R],
                                          src[:, b * R:(b + 1) * R], ident[0:R, 0:R])
                    tr.then_inc(s_tp, 1)

                def sum_up(s):
                    head, t = place(s)
                    pe.wait_ge(s_pt, every + s + 1)
                    wide = c > 512
                    wait(pe, s_out, every + s if wide else every + s - 1)
                    for half in range(2 if wide else 1):
                        cw = c // 2 if wide else c
                        col = head * c + half * cw
                        bank = 6 + (half if wide else s % 2)
                        for b in range(T):
                            mm = pe.matmul(PS[0:R, bank, 0:cw], PT[0:R, s % 2, b, :],
                                           F[0:R, b, col:col + cw], start=(b == 0), stop=(b == T - 1))
                    mm.then_inc(s_op, 1)

                pe.wait_ge(s_line, 2 * T * LINEARS_DONE[n])
                if kind == "gat":
                    pe.wait_ge(s_att, gats + 1)
                    for t in range(T):
                        tr = pe.transpose(PSz[0:h, t * P:t * P + R], a_s[:, t, 0:h], ident[0:R, 0:R])
                    tr.then_inc(s_astp, 1)
                    pe.wait_ge(s_ast, gats + 1)
                    broadcast(0)
                for s in range(units):
                    if kind == "gat" and place(s)[1] == T - 1 and place(s)[0] + 1 < h:
                        broadcast(place(s)[0] + 1)
                    turn(s)
                    if s:
                        sum_up(s - 1)
                sum_up(units - 1)

            def route(n, m):
                e = N_EXP[n]
                pe.wait_ge(s_rw, 48 * (n + 1))
                for t in range(T):
                    pe.wait_ge(s_trc, 2 * T * m + 2 * t + 2)
                    for k in range(KD):
                        mm = pe.matmul(PS[0:R, 4, t * 8:t * 8 + e], XT[:, k, t * R:(t + 1) * R], rw[:, k, 0:e],
                                       start=(k == 0), stop=(k == KD - 1))
                mm.then_inc(s_rtp, 1)

            def mix_bias(n):
                e = N_EXP[n]
                pe.wait_ge(s_comb, n + 1)
                for t in range(T):
                    tr = pe.transpose(PSz[0:8, t * P:t * P + R], comb[:, t, :], ident[0:R, 0:R])
                tr.then_inc(s_mbt, 1)
                pe.wait_ge(s_mbc, n + 1)
                for t in range(T):
                    g = T * n + t
                    wait(pe, s_mixd, g - 1)
                    for half in range(2):
                        mm = pe.matmul(PS[0:R, 4 + 2 * (g % 2) + half, 0:384], AT[0:e, t, :],
                                       mixb[0:e, half * 384:(half + 1) * 384], start=True, stop=True)
                    mm.then_inc(s_mixp, 1)

            def expert_out(done, t, u, lhs, rhs, last_u=None):
                wait(pe, s_md, done - 1)
                k_all = len(lhs)
                for half in range(2):
                    for k in range(k_all):
                        mm = pe.matmul(PS[0:R, 4 + 2 * (u % 2) + half, 0:384], lhs[k](t),
                                       rhs[k][:, half * 384:(half + 1) * 384], start=(k == 0), stop=(k == k_all - 1))
                mm.then_inc(s_mb, 1)

            def mixture0():
                hT = Oz[:, 0:2 * FC * N].rearrange("p (u c n) -> p u c n", u=2, c=FC)
                w1 = [WB[:, G1 * u:G1 * (u + 1) - FC].rearrange("p (k f) -> p k f", k=KD) for u in range(2)]
                w2 = WB[:, 2 * G1:].rearrange("p (u c d) -> p u c d", u=2, c=FC)

                def expert(e):
                    for u in range(NG):
                        slot = u % 2
                        pe.wait_ge(s_mw[slot], e * (32 * NG // 2) + 32 * (u // 2 + 1))
                        for c in range(FC):
                            for hf, (a, b) in enumerate(HALVES):
                                q = 2 * c + hf
                                if isinstance(e, int):
                                    wait(pe, s_mg, (e * NG + u) * 2 * FC + q - 3)
                                else:
                                    pe.wait_ge(s_mg, e * (NG * 2 * FC) + u * 2 * FC + q - 3)
                                for k in range(KD):
                                    mm = pe.matmul(PS[:, q % 4, 0:b - a], w1[slot][:, k, c * P:(c + 1) * P],
                                                   XT[:, k, a:b], start=(k == 0), stop=(k == KD - 1))
                                mm.then_inc(s_ma, 1)
                        pe.wait_ge(s_mg, e * (NG * 2 * FC) + (u + 1) * 2 * FC)
                        for t in range(T):
                            d = u * T + t
                            expert_out(e * (NG * T) + d, t, d,
                                       [lambda t, c=c: hT[:, slot, c, t * R:(t + 1) * R] for c in range(FC)],
                                       [w2[:, slot, c, :] for c in range(FC)])

                expert(0)
                with pe.Fori(1, 8) as e:
                    expert(e)

            def mixture1():
                w1 = WB[:, 0:3456].rearrange("p (e k f) -> p e k f", e=6, k=KD)
                w2 = WB[0:96, 3456:3456 + 4608].rearrange("p (e d) -> p e d", e=6)
                hT = Oz[0:96, 0:2 * N].rearrange("p (u n) -> p u n", u=2)
                pe.wait_ge(s_m2w, 48)
                for e in range(6):
                    for hf, (a, b) in enumerate(HALVES):
                        q = 2 * e + hf
                        pe.wait_ge(s_mg, MG1 + q - 3)
                        for k in range(KD):
                            mm = pe.matmul(PS[0:96, q % 4, 0:b - a], w1[:, e, k, :], XT[:, k, a:b],
                                           start=(k == 0), stop=(k == KD - 1))
                        mm.then_inc(s_ma, 1)
                    pe.wait_ge(s_mg, MG1 + 2 * e + 2)
                    for t in range(T):
                        d = MB1 + T * e + t
                        expert_out(d, t, d, [lambda t: hT[:, e % 2, t * R:(t + 1) * R]], [w2[:, e, :]])

            def mixture2():
                w = WB[:, 0:9216].rearrange("p (u k d) -> p u k d", u=2, k=KD)

                def two_experts(j):
                    for u in range(2):
                        pe.wait_ge(s_m3w[u], j * 16 + 16)
                        for t in range(T):
                            d = u * T + t
                            expert_out(MB3 + d + j * (2 * T), t, MB3 + d,
                                       [lambda t, k=k: XT[:, k, t * R:(t + 1) * R] for k in range(KD)],
                                       [w[:, u, k, :] for k in range(KD)])

                two_experts(0)
                with pe.Fori(1, 4) as j:
                    two_experts(j)

            def bit_layer():
                w1 = WB[:, 0:768].rearrange("p (k o) -> p k o", k=KD)
                pe.wait_ge(s_babs, 1)
                pe.matmul(PS[:, 4, 0:2], ones[:], ws[:, 0:2], start=True, stop=True).then_inc(s_bpe, 1)
                transpose_rows(5, O)
                pe.wait_ge(s_bwq, 1)
                for t in range(T):
                    pe.wait_ge(s_trc, 2 * T * 5 + 2 * t + 2)
                    for k in range(KD):
                        mm = pe.matmul(PS[0:R, 5 + t // 3, (t % 3) * P:(t % 3 + 1) * P],
                                       XT[:, k, t * R:(t + 1) * R], w1[:, k, :], start=(k == 0), stop=(k == KD - 1))
                mm.then_inc(s_bpe, 1)
                pe.wait_ge(s_bq2, 1)
                for t in range(T):
                    tr = pe.transpose(PSz[0:64, t * P:t * P + R], O[0:R, t, 0:64], ident[0:R, 0:R])
                tr.then_inc(s_bpe, 1)
                pe.wait_ge(s_bqt, 1)
                for t in range(T):
                    wait(pe, s_badd, t - 1)
                    for half in range(2):
                        mm = pe.matmul(PS[0:R, 4 * (t % 2) + 2 + half, 0:384], hidT[:, t, :],
                                       WB[0:64, 768 + half * 384:768 + (half + 1) * 384], start=True, stop=True)
                    mm.then_inc(s_bout, 1)

            pe.wait_ge(s_const, 80)
            counts()
            pe.wait_ge(s_cnt, 1)
            for g in range(2):
                transpose_rows(g, XN)
                linear(2 * g)
                linear(2 * g + 1)
                edges(g)
                attend(g)
            if sections > 1:
                transpose_rows(2, XN)
                route(0, 2)
                mix_bias(0)
                pe.wait_ge(s_mixd, T)
                mixture0()
            if sections > 2:
                transpose_rows(3, XN)
                linear(4)
                attend(2)
                transpose_rows(4, O)
                linear(5)
                attend(3)
            if sections > 3:
                bit_layer()
            if sections > 4:
                transpose_rows(6, XN)
                linear(6)
                attend(4)
            if sections > 5:
                transpose_rows(7, XN)
                route(1, 7)
                mix_bias(1)
                pe.wait_ge(s_mixd, 2 * T)
                mixture1()
            if sections > 6:
                transpose_rows(8, XN)
                linear(7)
                attend(5)
                transpose_rows(9, O)
                linear(8)
                attend(6)
            if sections > 7:
                transpose_rows(10, XN)
                route(2, 10)
                mix_bias(2)
                pe.wait_ge(s_mixd, 3 * T)
                mixture2()

        @block.scalar
        def _(act):
            def transpose_rows(n):
                per = TR_CHUNKS[n] // 2
                for t in range(T):
                    for half in range(2):
                        g = 2 * T * n + 2 * t + half
                        act.wait_ge(s_trp, g + 1)
                        act.copy(XT[:, half * per:(half + 1) * per, t * R:(t + 1) * R],
                                 PS[:, g % 4, 0:per * R].rearrange("p (k n) -> p k n", k=per)).then_inc(s_trc, 1)

            def edge_relu(i, u, g):
                base = ETP * g
                act.wait_ge(s_zt, base + i + 1)
                wait(act, s_dot, base + i - 1)
                act.activation(zr[:, u % 2, :, :].rearrange("p k c -> p (k c)"),
                               PSz[:, 1024 * (u % 2):1024 * (u % 2) + D], ACT.Relu).then_inc(s_zr, 1)

            def edges(g):
                for i in range(EU):
                    edge_relu(i, i, g)
                with act.Fori(1, ETP // EU) as j:
                    for u in range(EU):
                        edge_relu(j * EU + u, u, g)

            def attend(n):
                h, kind = HEADS[n]["h"], HEADS[n]["kind"]
                soft = units_before(n, ("table", "gat"))
                every = units_before(n, ("table", "gat", "average"))
                gats = sum(s["kind"] == "gat" for s in HEADS[:n])
                heads = sum(s["h"] for s in HEADS[:n] if s["kind"] == "gat")
                units = T * h
                place = unit_place(n)
                if kind == "gat":
                    act.wait_ge(s_astp, gats + 1)
                    act.copy(AT[0:h], PSz[0:h, 0:T * P].rearrange("h (t n) -> h t n", t=T)[:, :, 0:R])\
                       .then_inc(s_ast, 1)
                for s in range(units + 2):
                    if kind == "gat" and s < units:
                        head, t = place(s)
                        act.wait_ge(s_bc, heads + head + 1)
                        wait(act, s_tp, every + s - 3)
                        act.activation(W[0:R, s % 4, :], PSz[0:R, 0:N], ACT.Identity,
                                       bias=a_d[:, t, head:head + 1]).then_inc(s_v, 1)
                    if kind != "average" and 1 <= s <= units:
                        v = s - 1
                        act.wait_ge(s_lm, soft + v + 1)
                        act.activation(W[0:R, v % 4, :], W[0:R, v % 4, :], ACT.Exp, bias=nmx[:, v % 4:v % 4 + 1])\
                           .then_inc(s_e, 1)
                    if s >= 2:
                        v = s - 2
                        act.wait_ge(s_tp, every + v + 1)
                        wait(act, s_op, every + v - 1)
                        act.copy(PT[0:R, v % 2],
                                 PSz[0:R, 1024 * (1 + v % 2):1024 * (1 + v % 2) + T * P]
                                 .rearrange("p (b n) -> p b n", b=T)[:, :, 0:R]).then_inc(s_pt, 1)

            def elu_exp(g):
                for t in range(T):
                    act.wait_ge(s_neg, T * g + t + 1)
                    act.activation(F[0:R, t, 0:D], F[0:R, t, 0:D], ACT.Exp).then_inc(s_elu, 1)

            def route(n):
                act.wait_ge(s_gap, n + 1)
                act.activation(gate[:, 1, :], gate[:, 0, :], ACT.Exp)
                e = N_EXP[n]
                for t in range(T):
                    a = act.activation(comb2[:, t, 0:e], LG[:, t, 0:e], ACT.Exp, bias=gate[:, 2, t:t + 1],
                                       accum_out=gate[:, 3, t:t + 1])
                a.then_inc(s_gex, 1)

            def mix_bias(n):
                act.wait_ge(s_mbt, n + 1)
                act.copy(AT[0:8], PSz[0:8, 0:T * P].rearrange("h (t n) -> h t n", t=T)[:, :, 0:R])\
                   .then_inc(s_mbc, 1)

            def mixture0():
                hT = Oz[:, 0:2 * FC * N].rearrange("p (u c n) -> p u c n", u=2, c=FC)

                def expert(e):
                    for u in range(NG):
                        if isinstance(e, int):
                            wait(act, s_mb, T * (e * NG + u - 1))
                        else:
                            act.wait_ge(s_mb, e * (NG * T) + T * (u - 1))
                        for c in range(FC):
                            for hf, (a, b) in enumerate(HALVES):
                                q = 2 * c + hf
                                act.wait_ge(s_ma, e * (NG * 2 * FC) + u * 2 * FC + q + 1)
                                b1 = G1 * (u % 2 + 1) - FC + c
                                act.activation(hT[:, u % 2, c, a:b], PS[:, q % 4, 0:b - a], ACT.Gelu,
                                               bias=WB[:, b1:b1 + 1]).then_inc(s_mg, 1)

                expert(0)
                with act.Fori(1, 8) as e:
                    expert(e)

            def mixture1():
                hT = Oz[0:96, 0:2 * N].rearrange("p (u n) -> p u n", u=2)
                act.wait_ge(s_m2w, 48)
                for e in range(6):
                    act.wait_ge(s_mb, MB1 + T * (e - 1))
                    for hf, (a, b) in enumerate(HALVES):
                        q = 2 * e + hf
                        act.wait_ge(s_ma, MG1 + q + 1)
                        act.activation(hT[:, e % 2, a:b], PS[0:96, q % 4, 0:b - a], ACT.Gelu,
                                       bias=WB[0:96, 8064 + e:8065 + e]).then_inc(s_mg, 1)

            def bit_layer():
                act.wait_ge(s_bw, 32)
                act.wait_ge(s_bclr, 1)
                act.activation(WB[:, 1536:2304], WB[:, 0:768], ACT.Abs, accum_out=ws[:, 0:1])
                act.activation(WB[0:64, 2304:3072], WB[0:64, 768:1536], ACT.Abs, accum_out=ws[0:64, 1:2])\
                   .then_inc(s_babs, 1)
                for t in range(T):
                    act.wait_ge(s_by, t + 1)
                    act.activation(F[0:R, t, 0:D], O[0:R, t, 0:D], ACT.Abs).then_inc(s_bya, 1)
                transpose_rows(5)
                act.wait_ge(s_bh, 1)
                act.activation(F[0:R, 0:T, 0:64], O[0:R, 0:T, 192:256], ACT.Silu).then_inc(s_bsil, 1)
                act.wait_ge(s_by2, 1)
                act.activation(F[0:R, 0:T, 512:576], O[0:R, 0:T, 64:128], ACT.Abs).then_inc(s_bya, 1)
                act.wait_ge(s_bpe, 3)
                act.copy(hidT, PSz[0:64, 0:T * P].rearrange("h (t n) -> h t n", t=T)[:, :, 0:R]).then_inc(s_bqt, 1)

            for g in range(2):
                transpose_rows(g)
                edges(g)
                attend(g)
                elu_exp(g)
            if sections > 1:
                transpose_rows(2)
                route(0)
                mix_bias(0)
                mixture0()
            if sections > 2:
                transpose_rows(3)
                attend(2)
                transpose_rows(4)
                attend(3)
            if sections > 3:
                bit_layer()
            if sections > 4:
                transpose_rows(6)
                attend(4)
            if sections > 5:
                transpose_rows(7)
                route(1)
                mix_bias(1)
                mixture1()
            if sections > 6:
                transpose_rows(8)
                attend(5)
                transpose_rows(9)
                attend(6)
            if sections > 7:
                transpose_rows(10)
                route(2)
                mix_bias(2)

        @block.vector
        def _(dve):
            linked = [0]

            def link(ins):
                linked[0] += 1
                ins.then_inc(s_link, 1)
                dve.wait_ge(s_link, linked[0])

            def params(g):
                dve.wait_ge(s_par, 16 * par_total[g + 1])
                return PARAMS[g][0]

            def rows(t, buf, width=D):
                return buf[0:R, t, 0:width]

            def layer_norm(n, src, dst, tr=None, w=None, b=None, width=D):
                for t in range(T):
                    for half in range(2):
                        ins = dve.bn_stats(stats[:, t, half, :], src[0:R, t, half * 384:(half + 1) * 384])
                link(ins)
                for t in range(T):
                    ins = dve.bn_aggr(mv[:, t, :], stats[:, t].rearrange("p h s -> p (h s)"))
                link(ins)
                dve.tensor_scalar(var[:], mv[:, :, 1], LN_EPS, None, ALU.add).then_inc(s_var, 1)
                dve.wait_ge(s_rstd, n + 1)
                for t in range(T):
                    if w is None:
                        ins = dve.tensor_scalar(rows(t, dst), rows(t, src), mv[:, t, 0:1], rstd[:, t:t + 1],
                                                ALU.subtract, ALU.mult)
                    else:
                        link(dve.scalar_tensor_tensor(out=rows(t, dst), in0=rows(t, src), scalar=mv[:, t, 0:1],
                                                      in1=w, op0=ALU.subtract, op1=ALU.mult))
                        ins = dve.scalar_tensor_tensor(out=rows(t, dst), in0=rows(t, dst), scalar=rstd[:, t:t + 1],
                                                       in1=b, op0=ALU.mult, op1=ALU.add)
                    if tr is not None:
                        ins.then_inc(s_rows, 1)
                if tr is None:
                    link(ins)

            def counts():
                def onehots(i, slot):
                    wait(dve, s_ohu, i - 1)
                    for side in range(2):
                        ins = dve.tensor_scalar(oh[:, slot, side, :], iota, idf[:, side, bass.ds(i, 1)], None,
                                                ALU.is_equal)
                    ins.then_inc(s_oh, 1)

                onehots(0, 0)
                onehots(1, 1)
                with dve.Fori(1, ET // 2) as j:
                    for u in range(2):
                        onehots(j * 2 + u, u)
                onehots(ET - 1, 0)
                dve.wait_ge(s_ohu, ET)
                ins = dve.tensor_copy(Cz, PSz[0:R, 0:T * N])
                ins.then_inc(s_cnt, 1)
                dve.wait_ge(s_cnt, 1)
                link(dve.tensor_scalar(NEGz, Cz, 0.5, NEGBIG, ALU.is_lt, ALU.mult))

            def edge_rows(n, g, side):
                buf = (F, O)[side]
                for t in range(T):
                    for half in range(2):
                        q = 2 * T * n + 2 * t + half
                        dve.wait_ge(s_linp, q + 1)
                        dve.tensor_tensor(buf[0:R, t, half * 384:(half + 1) * 384], PS[0:R, 4 + q % 4, 0:384],
                                          PB[0:R, side * D + half * 384:side * D + (half + 1) * 384], ALU.add)\
                           .then_inc(s_line, 1)
                    if g:
                        link(dve.memset(buf[0:R, t, D:GW], 0.0))
                    dve.wait_ge(s_line, q + 1)
                    link(dve.scalar_tensor_tensor(out=TMP[:, 0:D], in0=rows(t, buf), scalar=0.2,
                                                  in1=par(2, D), op0=ALU.mult, op1=ALU.mult))
                    h = HEADS[g]["h"]
                    dve.tensor_reduce(buf[0:R, t, D:D + h], TMP[:, 0:D].rearrange("p (h c) -> p h c", h=h),
                                      AX_X, ALU.add).then_inc(s_frow, 1)

            def edges(g):
                base = ETP * g

                def add(i, u, rounds):
                    dve.wait_ge(s_gat[u % 4], rounds + 32 * (u // 4) + 32 * (ETP // 4) * g + 32)
                    dve.tensor_tensor(gs[:, u % 4, :], gs[:, u % 4, :], gd[:, u % 4, :], ALU.add).then_inc(s_z, 1)

                def finish(i, u):
                    dve.wait_ge(s_dot, base + i + 1)
                    wait(dve, s_sc, 16 * (base + i - 7))
                    dve.wait_ge(s_z, base + i + 1)
                    dve.tensor_tensor(lgr[:, u, :], PS[:, 4 + u % 2, 0:8], gs[:, u % 4, D:GW], ALU.add)\
                       .then_inc(s_lg, 1)

                for i in range(2 * EU):
                    add(i, i % EU, 32 * EU // 4 * (i // EU))
                    if i >= 2:
                        finish(i - 2, (i - 2) % EU)
                with dve.Fori(2, ETP // EU) as j:
                    for u in range(EU):
                        add(j * EU + u, u, j * (32 * EU // 4))
                        finish(j * EU + (u - 2), (u - 2) % EU)
                for i in (ETP - 2, ETP - 1):
                    finish(i, i % EU)

            def attend(n):
                h, c, kind = HEADS[n]["h"], HEADS[n]["c"], HEADS[n]["kind"]
                soft = units_before(n, ("table", "gat"))
                gat = units_before(n, ("gat",))
                every = units_before(n, ("table", "gat", "average"))
                units = T * h
                place = unit_place(n)

                def front(s):
                    head, t = place(s)
                    r = s % 4
                    w = W[0:R, r, :]
                    if kind == "gat":
                        dve.wait_ge(s_v, gat + s + 1)
                        link(dve.scalar_tensor_tensor(out=w, in0=w, scalar=0.2, in1=w, op0=ALU.mult, op1=ALU.max))
                        src = w
                    else:
                        wait(dve, s_tp, every + s - 3)
                        if n == 0:
                            dve.wait_ge(s_lt[t % 2], 16 * (t // 2 + 1))
                            src = ltile[:, t % 2, :, head]
                        else:
                            dve.wait_ge(s_lt[1], 16 * 3)
                            src = ltile1[:, t, :]
                    link(dve.tensor_tensor_reduce(out=w, in0=src, in1=NEG[:, t, :], scale=1.0, scalar=-3.0e38,
                                                  op0=ALU.add, op1=ALU.max, accum_out=mx[:, r:r + 1]))
                    dve.tensor_scalar(nmx[:, r:r + 1], mx[:, r:r + 1], -1.0, None, ALU.mult).then_inc(s_lm, 1)

                def back(s):
                    head, t = place(s)
                    r = s % 4
                    dve.wait_ge(s_e, soft + s + 1)
                    link(dve.tensor_tensor_reduce(out=W[0:R, r, :], in0=W[0:R, r, :], in1=C[:, t, :], scale=1.0,
                                                  scalar=TINY, op0=ALU.mult, op1=ALU.add, accum_out=den[:, r:r + 1]))
                    dve.reciprocal(rden[:, s % 8:s % 8 + 1], den[:, r:r + 1]).then_inc(s_p, 1)

                def evacuate(s):
                    head, t = place(s)
                    dve.wait_ge(s_op, every + s + 1)
                    if kind == "average":
                        scale = dinv[:, t:t + 1]
                    else:
                        dve.wait_ge(s_p, soft + s + 1)
                        scale = rden[:, s % 8:s % 8 + 1]
                    if c > 512:
                        o, i = O[0:R, t, 0:c].rearrange("p (a c) -> p a c", a=2), PS[0:R, 6:8, 0:c // 2]
                    else:
                        o, i = O[0:R, t, head * c:(head + 1) * c], PS[0:R, 6 + s % 2, 0:c]
                    dve.tensor_scalar(o, i, scale, None, ALU.mult).then_inc(s_out, 1)

                for s in range(units + 3):
                    if kind != "average" and s < units:
                        front(s)
                    if kind != "average" and 1 <= s <= units:
                        back(s - 1)
                    if s >= 3:
                        evacuate(s - 3)
                dve.wait_ge(s_out, every + units)

            def elu(g):
                for t in range(T):
                    dve.tensor_scalar(rows(t, F), rows(t, O), 0.0, None, ALU.min).then_inc(s_neg, 1)
                for t in range(T):
                    dve.wait_ge(s_elu, T * g + t + 1)
                    link(dve.scalar_tensor_tensor(out=rows(t, O), in0=rows(t, O), scalar=0.0, in1=rows(t, F),
                                                  op0=ALU.max, op1=ALU.add))
                    if g == 0:
                        ins = dve.scalar_tensor_tensor(out=rows(t, O), in0=rows(t, O), scalar=-1.0, in1=rows(t, XN),
                                                       op0=ALU.add, op1=ALU.add)
                    else:
                        ins = dve.tensor_scalar(rows(t, O), rows(t, O), -1.0, None, ALU.add)
                link(ins)

            def attention_terms(n, width, h):
                for t in range(T):
                    hw = width // 2
                    for half in range(2):
                        q = 2 * T * n + 2 * t + half
                        dve.wait_ge(s_linp, q + 1)
                        dve.tensor_copy(F[0:R, t, half * hw:(half + 1) * hw], PS[0:R, 4 + q % 4, 0:hw])\
                           .then_inc(s_line, 1)
                    dve.wait_ge(s_line, q + 1)
                    for side, (tmp, a) in enumerate(((TMP, a_s), (TMP2, a_d))):
                        link(dve.tensor_tensor(tmp[:, 0:width], rows(t, F, width), par(side, width), ALU.mult))
                        ins = dve.tensor_reduce(a[:, t, 0:h], tmp[:, 0:width].rearrange("p (h c) -> p h c", h=h),
                                                AX_X, ALU.add)
                        if side == 0 or t < T - 1:
                            link(ins)
                ins.then_inc(s_att, 1)

            def scaled_rows(n):
                for t in range(T):
                    for half in range(2):
                        q = 2 * T * n + 2 * t + half
                        dve.wait_ge(s_linp, q + 1)
                        dve.tensor_scalar(F[0:R, t, half * 384:(half + 1) * 384], PS[0:R, 4 + q % 4, 0:384],
                                          dinv[:, t:t + 1], None, ALU.mult).then_inc(s_line, 1)

            def bias_relu(width, slot):
                for t in range(T):
                    link(dve.tensor_tensor(rows(t, O, width), rows(t, O, width), par(slot, width), ALU.add))
                    ins = dve.tensor_scalar(rows(t, O, width), rows(t, O, width), 0.0, None, ALU.max)
                    ins.then_inc(s_rows, 1)

            def add_to_x(slot, last=True):
                for t in range(T):
                    if slot is not None:
                        link(dve.tensor_tensor(rows(t, O), rows(t, O), par(slot, D), ALU.add))
                    ins = dve.tensor_tensor(X[:, t, :], X[:, t, :], rows(t, O), ALU.add)
                link(ins)

            def route(n):
                e = N_EXP[n]
                dve.wait_ge(s_rtp, n + 1)
                dve.wait_ge(s_rw, 48 * (n + 1))
                if e < 8:
                    dve.memset(LG[:, :, e:8], NEGBIG)
                for t in range(T):
                    ins = dve.tensor_tensor(LG[:, t, 0:e], PS[0:R, 4, t * 8:t * 8 + e], rb[:, 0:e], ALU.add)
                link(ins)
                for t in range(T):
                    ins = dve.max(top[:, t, :], LG[:, t, :])
                link(ins)
                for t in range(T):
                    ins = dve.max_index(topi[:, t, :], top[:, t, :], LG[:, t, :])
                dve.tensor_tensor(gate[:, 0, :], top[:, :, 1], top[:, :, 0], ALU.subtract)
                dve.tensor_scalar(gate[:, 2, :], top[:, :, 0], -1.0, None, ALU.mult).then_inc(s_gap, 1)
                dve.wait_ge(s_gap, n + 1)
                link(dve.tensor_copy(topf[:], topi[:]))
                dve.wait_ge(s_gex, n + 1)
                link(dve.tensor_scalar(gate[:, 4, :], gate[:, 1, :], 1.0, None, ALU.add))
                if n == 2:
                    link(dve.scalar_tensor_tensor(out=gate[:, 4, :], in0=gate[:, 3, :], scalar=1.0e-9,
                                                  in1=gate[:, 4, :], op0=ALU.mult, op1=ALU.add))
                link(dve.reciprocal(gate[:, 5, :], gate[:, 4, :]))
                link(dve.tensor_tensor(gate[:, 6, :], gate[:, 5, :], gate[:, 1, :], ALU.mult))
                for t in range(T):
                    dve.tensor_scalar(comb[:, t, :], iota8[0:R], topf[:, t, 0:1], gate[:, 5, t:t + 1],
                                      ALU.is_equal, ALU.mult)
                    ins = dve.tensor_scalar(comb2[:, t, :], iota8[0:R], topf[:, t, 1:2], gate[:, 6, t:t + 1],
                                            ALU.is_equal, ALU.mult)
                link(ins)
                dve.tensor_tensor(comb[:], comb[:], comb2[:], ALU.add).then_inc(s_comb, 1)
                dve.wait_ge(s_comb, n + 1)

            def in_halves(ap):
                return ap.rearrange("p (a c) -> p a c", a=2)

            def mix_bias(n):
                for t in range(T):
                    g = T * n + t
                    dve.wait_ge(s_mixp, g + 1)
                    bank = 4 + 2 * (g % 2)
                    dve.tensor_tensor(in_halves(X[:, t, :]), PS[0:R, bank:bank + 2, 0:384], in_halves(X[:, t, :]),
                                      ALU.add).then_inc(s_mixd, 1)
                dve.wait_ge(s_mixd, T * (n + 1))

            def add_expert(done, t, parity, e):
                dve.wait_ge(s_mb, done + 1)
                wait(dve, s_md, done)
                bank = 4 + 2 * (parity % 2)
                dve.scalar_tensor_tensor(out=in_halves(X[:, t, :]), in0=PS[0:R, bank:bank + 2, 0:384],
                                         scalar=comb[:, t, bass.ds(e, 1)] if not isinstance(e, int) else comb[:, t, e:e + 1],
                                         in1=in_halves(X[:, t, :]), op0=ALU.mult, op1=ALU.add).then_inc(s_md, 1)

            def mixture0():
                def expert(e):
                    for d in range(NG * T):
                        add_expert(e * (NG * T) + d, d % T, d, e)

                expert(0)
                with dve.Fori(1, 8) as e:
                    expert(e)

            def mixture1():
                for e in range(6):
                    for t in range(T):
                        add_expert(MB1 + T * e + t, t, MB1 + T * e + t, e)

            def mixture2():
                def two_experts(j):
                    for d in range(2 * T):
                        add_expert(j * (2 * T) + MB3 + d, d % T, MB3 + d, j * 2 + d // T)

                two_experts(0)
                with dve.Fori(1, 4) as j:
                    two_experts(j)

            def bit_layer():
                dve.memset(ws[:], 0.0).then_inc(s_bclr, 1)
                params(4)
                for t in range(T):
                    ins = dve.tensor_tensor_reduce(out=rows(t, O), in0=XN[:, t, :], in1=XN[:, t, :], scale=1.0,
                                                   scalar=0.0, op0=ALU.mult, op1=ALU.add, accum_out=bs[0:R, 0, t:t + 1])
                link(ins)
                dve.tensor_scalar(var[:], bs[0:R, 0, :], 1.0 / D, 1.0e-6, ALU.mult, ALU.add).then_inc(s_var, 1)
                dve.wait_ge(s_rstd, 7)
                for t in range(T):
                    dve.scalar_tensor_tensor(out=rows(t, O), in0=XN[:, t, :], scalar=rstd[:, t:t + 1], in1=par(0, D),
                                             op0=ALU.mult, op1=ALU.mult).then_inc(s_by, 1)
                dve.wait_ge(s_bpe, 1)
                dve.tensor_scalar(ws[:, 2:3], PS[:, 4, 0:1], 1.0 / (P * D), 1.0e-5, ALU.mult, ALU.max)
                link(dve.tensor_scalar(ws[:, 3:4], PS[:, 4, 1:2], 1.0 / (64 * D), 1.0e-5, ALU.mult, ALU.max))
                link(dve.reciprocal(ws[:, 4:6], ws[:, 2:4]))
                for w, k in ((WB[:, 0:768], 4), (WB[0:64, 768:1536], 5)):
                    np_ = w.shape[0]
                    link(dve.tensor_scalar(w, w, ws[0:np_, k:k + 1], -1.0, ALU.mult, ALU.max))
                    link(dve.tensor_scalar(w, w, ROUND, ROUND + 1.0, ALU.add, ALU.min))
                    ins = dve.tensor_scalar(w, w, ROUND, None, ALU.subtract)
                ins.then_inc(s_bwq, 1)

                def quantise(width, src_abs, at, k):
                    for t in range(T):
                        dve.wait_ge(s_bya, (t + 1) if k == 0 else (T + 1))
                        ins = dve.tensor_reduce(bs[0:R, 1 + k, t:t + 1], src_abs(t), AX_X, ALU.max)
                    link(ins)
                    link(dve.tensor_scalar(bs[0:R, 1 + k, :], bs[0:R, 1 + k, :], 1.0e-5, None, ALU.max))
                    link(dve.reciprocal(bs[0:R, 3 + k, :], bs[0:R, 1 + k, :]))
                    link(dve.tensor_scalar(bs[0:R, 3 + k, :], bs[0:R, 3 + k, :], 127.0, None, ALU.mult))
                    link(dve.tensor_scalar(bs[0:R, 5 + k, :], bs[0:R, 1 + k, :], 1.0 / 127.0, ws[0:R, 2 + k:3 + k],
                                           ALU.mult, ALU.mult))
                    for t in range(T):
                        y, q = at(t)
                        link(dve.tensor_scalar(q, y, bs[0:R, 3 + k, t:t + 1], -128.0, ALU.mult, ALU.max))
                        link(dve.tensor_scalar(q, q, ROUND, ROUND + 127.0, ALU.add, ALU.min))
                        ins = dve.tensor_scalar(q, q, ROUND, None, ALU.subtract)
                        if k == 0:
                            ins.then_inc(s_rows, 1)
                    if k == 1:
                        ins.then_inc(s_bq2, 1)

                quantise(D, lambda t: rows(t, F), lambda t: (rows(t, O), rows(t, O)), 0)
                dve.wait_ge(s_bpe, 2)
                for t in range(T):
                    ins = dve.tensor_scalar(O[0:R, t, 128:256], PS[0:R, 5 + t // 3, (t % 3) * P:(t % 3 + 1) * P],
                                            bs[0:R, 5, t:t + 1], None, ALU.mult)
                ins.then_inc(s_bh, 1)
                dve.wait_ge(s_bh, 1)
                dve.wait_ge(s_bsil, 1)
                link(dve.tensor_tensor(O[0:R, 0:T, 0:64], F[0:R, 0:T, 0:64], O[0:R, 0:T, 128:192], ALU.mult))
                for t in range(T):
                    ins = dve.tensor_tensor_reduce(out=O[0:R, t, 64:128], in0=O[0:R, t, 0:64], in1=O[0:R, t, 0:64],
                                                   scale=1.0, scalar=0.0, op0=ALU.mult, op1=ALU.add,
                                                   accum_out=bs[0:R, 7, t:t + 1])
                link(ins)
                dve.tensor_scalar(var[:], bs[0:R, 7, :], 1.0 / 64, 1.0e-6, ALU.mult, ALU.add).then_inc(s_var, 1)
                dve.wait_ge(s_rstd, 8)
                for t in range(T):
                    ins = dve.scalar_tensor_tensor(out=O[0:R, t, 64:128], in0=O[0:R, t, 0:64],
                                                   scalar=rstd[:, t:t + 1], in1=PB[0:R, D:D + 64],
                                                   op0=ALU.mult, op1=ALU.mult)
                ins.then_inc(s_by2, 1)
                dve.wait_ge(s_by2, 1)
                quantise(64, lambda t: F[0:R, t, 512:576], lambda t: (O[0:R, t, 64:128], O[0:R, t, 0:64]), 1)
                for t in range(T):
                    dve.wait_ge(s_bout, t + 1)
                    bank = 4 * (t % 2) + 2
                    dve.scalar_tensor_tensor(out=in_halves(X[:, t, :]), in0=PS[0:R, bank:bank + 2, 0:384],
                                             scalar=bs[0:R, 6, t:t + 1], in1=in_halves(X[:, t, :]),
                                             op0=ALU.mult, op1=ALU.add).then_inc(s_badd, 1)
                dve.wait_ge(s_badd, T)

            def announce(s):
                dve.nop().then_inc(s, 1)

            def section_end():
                announce(s_sec)

            dve.memset(mhalf[:], -0.5).then_inc(s_mh, 1)
            dve.memset(Oz[0:R, 0:5000], 0.0).then_inc(s_zero, 1)
            dve.memset(ones[:], 1.0)
            dve.wait_ge(s_idx, 16)
            dve.tensor_copy(idf[:, 0, :], idx[:, :, 0])
            link(dve.tensor_copy(idf[:, 1, :], idx[:, :, 1]))
            keyf = W[:, 0, 0:ETP]
            link(dve.scalar_tensor_tensor(out=keyf, in0=idf[:, 1, :], scalar=float(N), in1=idf[:, 0, :],
                                          op0=ALU.mult, op1=ALU.add))
            dve.tensor_copy(key[:], keyf).then_inc(s_keys, 1)
            dve.wait_ge(s_const, 80)
            for a in range(2):
                for k in range(KD):
                    ins = dve.tensor_scalar(blk[:, a, k, :], hmask[:, a, k, :], attc[:, a, k:k + 1], 0.8,
                                            ALU.mult, ALU.mult)
            link(ins)
            dve.wait_ge(s_x, 16)
            layer_norm(0, X, XN, tr=0)
            counts()

            for g in range(2):
                params(g)
                if g == 0:
                    dve.wait_ge(s_zeroed, 96)
                edge_rows(2 * g, g, 0)
                edge_rows(2 * g + 1, g, 1)
                edges(g)
                attend(g)
                elu(g)
                layer_norm(1 + g, O, XN if g == 0 else O, tr=1 if g == 0 else None, w=par(3, D), b=par(4, D))
                if g == 0:
                    dve.wait_ge(s_rows, 2 * T)
                else:
                    add_to_x(None)
                announce(s_pfree)
            section_end()
            if sections > 1:
                layer_norm(3, X, XN, tr=2)
                route(0)
                mix_bias(0)
                mixture0()
                dve.wait_ge(s_md, MB1)
                section_end()
            if sections > 2:
                layer_norm(4, X, XN, tr=3)
                params(2)
                attention_terms(4, 1024, 8)
                attend(2)
                bias_relu(1024, 2)
                dve.wait_ge(s_rows, 5 * T)
                announce(s_pfree)
                params(3)
                attention_terms(5, 768, 1)
                attend(3)
                add_to_x(2)
                announce(s_pfree)
                section_end()
            if sections > 3:
                layer_norm(5, X, XN)
                bit_layer()
                announce(s_pfree)
                section_end()
            if sections > 4:
                for t in range(T):
                    ins = dve.tensor_tensor(C[:, t, t * R:(t + 1) * R], C[:, t, t * R:(t + 1) * R],
                                            ident[0:R, 0:R], ALU.add)
                link(ins)
                dve.tensor_scalar(NEGz, Cz, 0.5, NEGBIG, ALU.is_lt, ALU.mult)
                link(dve.tensor_reduce(bs[0:R, 8, :], C[:], AX_X, ALU.add))
                layer_norm(8, X, XN, tr=6)
                dve.tensor_copy(var[:], bs[0:R, 8, :]).then_inc(s_var, 1)
                dve.wait_ge(s_rstd, 10)
                link(dve.tensor_copy(dinv[:], rstd[:]))
                params(5)
                scaled_rows(6)
                attend(4)
                add_to_x(0)
                announce(s_pfree)
                section_end()
            if sections > 5:
                layer_norm(10, X, XN, tr=7)
                route(1)
                mix_bias(1)
                mixture1()
                dve.wait_ge(s_md, MB3)
                section_end()
            if sections > 6:
                layer_norm(11, X, XN, tr=8)
                params(6)
                attention_terms(7, 768, 4)
                attend(5)
                bias_relu(768, 2)
                dve.wait_ge(s_rows, 10 * T)
                announce(s_pfree)
                params(7)
                attention_terms(8, 768, 4)
                attend(6)
                add_to_x(2)
                announce(s_pfree)
                section_end()
            if sections > 7:
                layer_norm(12, X, XN, tr=10)
                route(2)
                mix_bias(2)
                mixture2()
                dve.wait_ge(s_md, MB3 + 8 * T)
                section_end()
    return nc


def _layout(inputs):
    a = {k: np.ascontiguousarray(v) for k, v in inputs.items()}

    def cols(w):
        k = w.shape[0] // P
        return np.ascontiguousarray(w.reshape(k, P, w.shape[1]).transpose(1, 0, 2).reshape(P, -1))

    out = {"x": a["x"]}
    ends = np.stack([a["src"], a["dst"]], -1)
    ends = np.concatenate([ends, ends[:ETP * P - E]])
    out["edges"] = np.ascontiguousarray(ends.reshape(ETP, P, 2).transpose(1, 0, 2).astype(np.int32))
    out["iota"] = np.ascontiguousarray(np.broadcast_to(np.arange(626, dtype=np.float32), (P, 626)))
    out["iota8"] = np.ascontiguousarray(np.broadcast_to(np.arange(8, dtype=np.float32), (P, 8)))
    out["ident"] = np.eye(P, dtype=np.float32)
    out["attc"] = np.ascontiguousarray(np.stack([a["L0_gnn_attn1"].reshape(KD, P).T,
                                                 a["L0_gnn_attno"].reshape(KD, P).T], 1))
    feature = np.arange(D).reshape(KD, P).T
    hm = np.zeros((P, 2, KD, 8), np.float32)
    for h in range(8):
        hm[:, 0, :, h] = feature // 96 == h
    hm[:, 1, :, 0] = 1.0
    out["hmask"] = hm
    for n in ("L0_gnn_W1s", "L0_gnn_W1d", "L0_gnn_Wos", "L0_gnn_Wod", "L2_gnn_W", "L3_gnn_W1", "L3_gnn_W2"):
        out[n] = cols(a[n])
    for n in ("L1_gnn_W1", "L1_gnn_W2", "L1_ffn_w_in"):
        out[n] = cols(a[n].T)
    out["L1_ffn_w_out"] = np.ascontiguousarray(a["L1_ffn_w_out"].T)
    for n in ("L0_ffn_router_w", "L2_ffn_gate_w"):
        out[n] = cols(a[n]).reshape(P, KD, -1)
    out["L3_ffn_router_w"] = cols(a["L3_ffn_router_w"].T).reshape(P, KD, -1)
    for n in ("L0_ffn_b2", "L2_ffn_b2", "L3_ffn_expert_b"):
        out[n] = a[n]
    w1 = a["L0_ffn_w1"].reshape(8, KD, P, NG, FC * P).transpose(0, 3, 2, 1, 4).reshape(8 * NG, P, -1)
    b1 = a["L0_ffn_b1"].reshape(8 * NG, FC, P).transpose(0, 2, 1)
    out["L0_ffn_w1"] = np.ascontiguousarray(np.concatenate([w1, b1], 2))
    out["L0_ffn_w2"] = np.ascontiguousarray(
        a["L0_ffn_w2"].reshape(8, NG, FC, P, D).transpose(0, 1, 3, 2, 4).reshape(8 * NG, P, -1))
    out["L2_ffn_w1"] = np.ascontiguousarray(a["L2_ffn_w1"].reshape(6, KD, P, 96).transpose(2, 0, 1, 3).reshape(P, -1))
    out["L2_ffn_w2"] = np.ascontiguousarray(a["L2_ffn_w2"].transpose(1, 0, 2).reshape(96, -1))
    out["L2_ffn_b1"] = np.ascontiguousarray(a["L2_ffn_b1"].T)
    out["L3_ffn_expert_w"] = np.ascontiguousarray(
        a["L3_ffn_expert_w"].transpose(0, 2, 1).reshape(8, KD, P, D).transpose(0, 2, 1, 3).reshape(8, P, -1))
    for n, v in a.items():
        if n not in out and n not in ("src", "dst", "L0_ffn_b1"):
            out[n] = v.reshape(1, -1)
    return out


def kernel(**inputs):
    import concourse.bacc as bacc
    from concourse.bass_utils import run_bass_kernel_spmd

    nc = bacc.Bacc("TRN2", target_bir_lowering=False, num_devices=1)
    arrays, aps = {}, {}
    for name, v in _layout(inputs).items():
        arrays["in_" + name] = v
        aps[name] = nc.dram_tensor("in_" + name, v.shape, mybir.dt.from_np(v.dtype), kind="ExternalInput").ap()
    out = nc.dram_tensor("out_0", (N, D), F32, kind="ExternalOutput").ap()
    build(nc, aps, out)
    r = run_bass_kernel_spmd(nc, [arrays], core_ids=[0])
    return r.results[0]["out_0"]
```

```python
from contextlib import ExitStack

import numpy as np

import concourse.bass as bass
from concourse import mybir

F32 = mybir.dt.float32
BF16 = mybir.dt.bfloat16
F32R = mybir.dt.float32r
I32 = mybir.dt.int32
U32 = mybir.dt.uint32
ACT = mybir.ActivationFunctionType
ALU = mybir.AluOpType
AX_X = mybir.AxisListType.X

P = 128
N = 625
R = 125
T = N // R
D = 768
KD = D // P
E = 20000
ET = -(-E // P)
ETP = 160
EU = 8
GW = D + 8
FF = 3072
FC = 2
NG = FF // (P * FC)
G1 = KD * FC * P + FC
G2 = FC * D
TU = 256
NU = 8 + (2 * N - 8) // TU
ZEROED = 16 * (6 + NU + 1 + NU)
SU = TU // P
HALF = 313
HALVES = ((0, HALF), (HALF, N))
NEGBIG = -1.0e30
TINY = 1.0e-16
LN_EPS = 1.0e-5
ROUND = 12582912.0


def count_segments():
    out = []
    for c in range(T):
        a, end = c * N, (c + 1) * N
        while a < end:
            b = min(end, (a // 512 + 1) * 512)
            out.append((c, a, b, a % 512 == 0))
            a = b
    return out


HEADS = [
    dict(h=8, c=96, kind="table"),
    dict(h=1, c=768, kind="table"),
    dict(h=8, c=128, kind="gat"),
    dict(h=1, c=768, kind="gat"),
    dict(h=1, c=768, kind="average"),
    dict(h=4, c=192, kind="gat"),
    dict(h=4, c=192, kind="gat"),
]
LINEARS = [
    (6, 768, 0), (6, 768, 0), (6, 768, 1), (6, 768, 1),
    (6, 1024, 3), (8, 768, 4), (6, 768, 6),
    (6, 768, 8), (6, 768, 9),
]
LIN_HALF = [n // 2 for _, n, _ in LINEARS]
TR_CHUNKS = [6, 6, 6, 6, 8, 6, 6, 6, 6, 6, 6]


LINEARS_DONE = [2, 4, 5, 6, 7, 8, 9]
MG1 = 0
MB1 = 0
MB3 = MB1 + 6 * T
RS_COUNT = [0, 3, 4, 5, 8, 10, 11, 12, 13]


def unit_place(n):
    if n == 0:
        return lambda s: (s % 8, s // 8)
    return lambda s: (s // T, s % T)


def units_before(n, kinds):
    return sum(T * s["h"] for s in HEADS[:n] if s["kind"] in kinds)


def build(nc, ins, out, sections=8):
    ctx = ExitStack()
    with ctx:
        def sb(name, shape, dt=F32):
            return ctx.enter_context(nc.sbuf_tensor(name, shape, dt))

        def sem(name):
            return ctx.enter_context(nc.semaphore(name))

        def wait(eng, s, value):
            if isinstance(value, int) and value <= 0:
                return
            eng.wait_ge(s, value)

        src_rows = nc.dram_tensor("src_rows", [N, GW], F32, kind="Internal").ap()
        dst_rows = nc.dram_tensor("dst_rows", [N, GW], F32, kind="Internal").ap()
        logits8 = nc.dram_tensor("logits8", [N * N, 8], F32, kind="Internal").ap()
        logits1 = nc.dram_tensor("logits1", [N * N, 1], F32, kind="Internal").ap()
        tables = [logits8, logits1]
        slot_rows = nc.dram_tensor("slot_rows", [(NU + 1) * TU, D], F32, kind="Internal").ap()
        slot_outs = nc.dram_tensor("slot_outs", [NU * TU, D], F32, kind="Internal").ap()

        with ExitStack() as early:
            w1s = early.enter_context(nc.sbuf_tensor("w1s", [P, 2, 2, G2], F32R))
            w2s = early.enter_context(nc.sbuf_tensor("w2s", [P, 2, 2, G2], F32R))
            hid2 = early.enter_context(nc.sbuf_tensor("hid2", [P, 2, 2, FC * TU], F32R))
            urowsT2 = early.enter_context(nc.sbuf_tensor("urowsT2", [P, 2, KD * TU], F32R))
        WB = sb("WB", [P, 2 * 6144])
        O = sb("O", [P, T, 1024])
        X = sb("X", [R, T, D])
        XN = sb("XN", [P, T, D])
        XT = sb("XT", [P, 8, N])
        F = sb("F", [P, T, 1024])
        C = sb("C", [R, T, N])
        NEG = sb("NEG", [R, T, N])
        PB = sb("PB", [P, 3840])
        W = sb("W", [P, 4, N])
        PT = sb("PT", [P, 2, T, R])
        idx = sb("idx", [P, ETP, 2], I32)
        key = sb("key", [P, ETP], I32)
        idf = sb("idf", [P, 2, ETP])
        ident = sb("ident", [P, P])
        AT = sb("AT", [8, T, R])
        attc = sb("attc", [P, 2, KD])
        hmask = sb("hmask", [P, 2, KD, 8])
        blk = sb("blk", [P, 2, KD, 8])
        iota8 = sb("iota8", [P, 8])
        stats = sb("stats", [R, T, 2, 6])
        mv = sb("mv", [R, T, 2])
        var = sb("var", [R, T])
        rstd = sb("rstd", [R, T])
        mhalf = sb("mhalf", [R, T])
        a_s = sb("a_s", [R, T, 8])
        a_d = sb("a_d", [R, T, 8])
        mx = sb("mx", [R, 4])
        nmx = sb("nmx", [R, 4])
        den = sb("den", [R, 4])
        rden = sb("rden", [R, 8])
        dinv = sb("dinv", [R, T])
        ixr = sb("ixr", [P, EU, 3], I32)
        lgr = sb("lgr", [P, EU, 8])
        rw = sb("rw", [P, KD, 8])
        rb = sb("rb", [R, 8])
        LG = sb("LG", [R, T, 8])
        top = sb("top", [R, T, 8])
        topi = sb("topi", [R, T, 8], U32)
        topf = sb("topf", [R, T, 8])
        gate = sb("gate", [R, 8, T])
        comb = sb("comb", [R, T, 8])
        comb2 = sb("comb2", [R, T, 8])
        mixb = sb("mixb", [8, D])
        ones = sb("ones", [P, P])
        bs = sb("bs", [P, 16, T])
        ws = sb("ws", [P, 8])

        iotaU = sb("iotaU", [P, NU + 1])
        before = sb("before", [R, R])
        pick = sb("pick", [R, 3, T, 8])
        place_of = sb("place_of", [R, T, 8])
        slotf = sb("slotf", [R, 2, T])
        slots = sb("slots", [R, 2, T], I32)
        plan = sb("plan", [P, 4, 8])
        uexpf = sb("uexpf", [P, NU + 1])
        uexp = sb("uexp", [P, NU + 1], I32)
        nunits = sb("nunits", [P, 1], I32)
        b1c = sb("b1c", [P, 2, FC])

        Fz = F[:, :, :].rearrange("p t c -> p (t c)")
        Oz = O[:, :, :].rearrange("p t c -> p (t c)")
        iota = Fz[:, 0:626]
        oh = WB[:, 0:1252].bitcast(BF16).rearrange("p (u s n) -> p u s n", u=2, s=2)
        XTz = XT[:, :, :].rearrange("p k n -> p (k n)")
        gs = [WB[:, u * GW:(u + 1) * GW] for u in range(EU)]
        gd = [WB[:, (EU + u) * GW:(EU + u + 1) * GW] for u in range(EU - 1)] + [XTz[:, 0:GW]]
        zr = XTz[:, GW:GW + 2 * D].rearrange("p (u k c) -> p u k c", u=2, k=KD)
        ltile = WB[0:R, 0:10000].rearrange("p (u n h) -> p u n h", u=2, h=8)
        ltile1 = WB[0:R, 0:T * N].rearrange("p (t n) -> p t n", t=T)
        wlin = [WB[:, 6144 * u:6144 * (u + 1)] for u in range(2)]
        TMP = W[:, :, :].rearrange("p a b -> p (a b)")[0:R, 0:1024]
        TMP2 = W[:, :, :].rearrange("p a b -> p (a b)")[0:R, 1024:2048]
        Cz = C[:, :, :].rearrange("p t n -> p (t n)")
        NEGz = NEG[:, :, :].rearrange("p t n -> p (t n)")

        hidT = WB[0:64, 3072:3072 + N].rearrange("p (t n) -> p t n", t=T)

        uout = Fz[:, 0:SU * D].rearrange("p (s d) -> p s d", s=SU)
        urows = Fz[:, SU * D:2 * SU * D].rearrange("p (s d) -> p s d", s=SU)
        hid = Fz[:, 2 * SU * D:2 * SU * D + 2 * FC * TU].rearrange("p (u n) -> p u n", u=2)
        uw1 = [XN[:, :, :].rearrange("p t d -> p (t d)")[:, G1 * u:G1 * (u + 1)] for u in range(2)]
        uw2 = [PB[:, G2 * u:G2 * (u + 1)] for u in range(2)]
        picked = WB[0:R, 0:2 * T * D].rearrange("p (k t d) -> p k t d", k=2, t=T)

        def par(slot, width, w=None):
            return PB[0:R, slot * width:slot * width + (w or width)]

        PS = ctx.enter_context(nc.psum_tensor("PS", [P, 8, 512], F32))
        PSz = PS[:, :, :].rearrange("p b n -> p (b n)")

        s_const = sem("consts_loaded")
        s_x = sem("x_loaded")
        s_idx = sem("edges_loaded")
        s_keys = sem("edge_keys_ready")
        s_zero = sem("zeros_ready")
        s_zeroed = sem("tables_zeroed")
        s_oh = sem("onehots_ready")
        s_ohu = sem("onehots_used")
        s_cnt = sem("counts_ready")
        s_link = sem("vector_link")
        s_mh = sem("minus_half_ready")
        s_var = sem("variances_ready")
        s_rstd = sem("rstds_ready")
        s_rows = sem("rows_ready")
        s_trp = sem("transposed_in_psum")
        s_trc = sem("transposed_copied")
        s_par = sem("params_loaded")
        s_pfree = sem("params_used")
        s_wl = [sem(f"linear_weights{u}") for u in range(2)]
        s_linp = sem("linear_in_psum")
        s_line = sem("linear_evacuated")
        s_frow = sem("table_rows_ready")
        s_tab = sem("tables_written")
        s_ends = sem("node_numbers_copied")
        s_kc = sem("pair_numbers_copied")
        s_gat = [sem(f"rows_gathered{u}") for u in range(EU)]
        s_z = sem("edge_sums_ready")
        s_zt = sem("edge_sums_transposed")
        s_zr = sem("edge_relus_ready")
        s_dot = sem("edge_dots_ready")
        s_lg = sem("edge_logits_ready")
        s_sc = sem("edge_logits_scattered")
        s_lt = [sem(f"logit_tile_loaded{u}") for u in range(2)]
        s_att = sem("attention_terms_ready")
        s_astp = sem("terms_transposed")
        s_ast = sem("terms_copied")
        s_bc = sem("source_terms_broadcast")
        s_v = sem("edge_terms_ready")
        s_lm = sem("masked_logits_ready")
        s_e = sem("exps_ready")
        s_p = sem("weights_ready")
        s_tp = sem("weights_transposed")
        s_pt = sem("weights_copied")
        s_op = sem("sums_in_psum")
        s_out = sem("sums_evacuated")
        s_neg = sem("negative_parts_ready")
        s_elu = sem("elu_exps_ready")
        s_rw = sem("router_loaded")
        s_rtp = sem("router_in_psum")
        s_gap = sem("router_gaps_ready")
        s_gex = sem("router_exps_ready")
        s_comb = sem("mixture_weights_ready")
        s_mbt = sem("mixture_weights_transposed")
        s_mbc = sem("mixture_weights_copied")
        s_mixp = sem("bias_mix_in_psum")
        s_mixd = sem("bias_mix_added")
        s_pick = sem("choices_ready")
        s_rank = sem("ranks_in_psum")
        s_slots = sem("slots_ready")
        s_plan = sem("unit_experts_ready")
        s_scr = sem("token_rows_scattered")
        s_w1 = [sem(f"first_weights{u}") for u in range(2)]
        s_w2 = [sem(f"second_weights{u}") for u in range(2)]
        s_ux = sem("unit_rows_loaded")
        s_ut = sem("unit_rows_transposed")
        s_uc = sem("unit_rows_copied")
        s_ua = sem("unit_hidden_in_psum")
        s_ug = sem("unit_hidden_ready")
        s_ub = sem("unit_group_summed")
        s_uy = sem("unit_output_evacuated")
        s_us = sem("unit_output_stored")
        s_left = sem("units_left")
        s_hi1 = sem("first_weights_rounded")
        s_lo1 = sem("first_weights_split")
        s_hi2 = sem("second_weights_rounded")
        s_lo2 = sem("second_weights_split")
        s_hh = sem("unit_hidden_rounded")
        s_hl = sem("unit_hidden_split")
        s_ul = sem("unit_rows_split")
        s_yg = sem("token_outputs_gathered")
        s_ma = sem("hidden_in_psum")
        s_mg = sem("hidden_ready")
        s_mb = sem("expert_in_psum")
        s_md = sem("expert_added")
        s_m2w = sem("small_experts_loaded")
        s_m3w = [sem(f"square_expert_weights{u}") for u in range(2)]
        s_bw = sem("bit_weights_loaded")
        s_bclr = sem("bit_sums_cleared")
        s_babs = sem("bit_weight_sums_ready")
        s_bpe = sem("bit_products_ready")
        s_bwq = sem("bit_weights_rounded")
        s_by = sem("bit_rows_normalised")
        s_bya = sem("bit_rows_absolute")
        s_bh = sem("bit_hidden_ready")
        s_bsil = sem("bit_silu_ready")
        s_by2 = sem("bit_hidden_normalised")
        s_bq2 = sem("bit_hidden_rounded")
        s_bqt = sem("bit_hidden_transposed")
        s_bout = sem("bit_output_in_psum")
        s_badd = sem("bit_output_added")
        s_sec = sem("section_done")
        s_store = sem("output_stored")

        block = ctx.enter_context(nc.Block())

        PARAMS = [
            (768, ["L0_gnn_b1s", "L0_gnn_b1d", "L0_gnn_attn1", "L0_gnn_ln1_w", "L0_gnn_ln1_b"]),
            (768, ["L0_gnn_bos", "L0_gnn_bod", "L0_gnn_attno", "L0_gnn_lno_w", "L0_gnn_lno_b"]),
            (1024, ["L1_gnn_att_src1", "L1_gnn_att_dst1", "L1_gnn_b1"]),
            (768, ["L1_gnn_att_src2", "L1_gnn_att_dst2", "L1_gnn_b2"]),
            (768, ["L1_ffn_g_in", "L1_ffn_g_out"]),
            (768, ["L2_gnn_b"]),
            (768, ["L3_gnn_a_src1", "L3_gnn_a_dst1", "L3_gnn_b1"]),
            (768, ["L3_gnn_a_src2", "L3_gnn_a_dst2", "L3_gnn_b2"]),
        ]
        par_total = np.cumsum([0] + [len(p) for _, p in PARAMS]).tolist()
        LIN_W = ["L0_gnn_W1s", "L0_gnn_W1d", "L0_gnn_Wos", "L0_gnn_Wod", "L1_gnn_W1", "L1_gnn_W2",
                 "L2_gnn_W", "L3_gnn_W1", "L3_gnn_W2"]
        ROUTERS = [("L0_ffn_router_w", "L0_ffn_router_b"), ("L2_ffn_gate_w", "L2_ffn_gate_b"),
                   ("L3_ffn_router_w", "L3_ffn_router_b")]
        MIXB = ["L0_ffn_b2", "L2_ffn_b2", "L3_ffn_expert_b"]
        N_EXP = [8, 6, 8]

        @block.sync
        def _(sp):
            def params(g):
                wait(sp, s_pfree, g)
                width, names = PARAMS[g]
                for k, name in enumerate(names):
                    n = ins[name].shape[1]
                    sp.dma_start(PB[0:R, k * width:k * width + n], ins[name].to_broadcast([R, n]))\
                      .then_inc(s_par, 16)

            def linear_weights(n):
                k, width, _ = LINEARS[n]
                sp.dma_start(wlin[n % 2][:, 0:k * width], ins[LIN_W[n]]).then_inc(s_wl[n % 2], 16)

            def router(n):
                if n:
                    sp.wait_ge(s_mixp, T * n)
                    sp.wait_ge(s_comb, n)
                sp.dma_start(rw[:, :, 0:N_EXP[n]], ins[ROUTERS[n][0]]).then_inc(s_rw, 16)
                sp.dma_start(rb[:, 0:N_EXP[n]], ins[ROUTERS[n][1]].to_broadcast([R, N_EXP[n]])).then_inc(s_rw, 16)
                sp.dma_start(mixb[0:N_EXP[n], :], ins[MIXB[n]]).then_inc(s_rw, 16)

            sp.dma_start(iota, ins["iota"]).then_inc(s_const, 16)
            sp.dma_start(idx[:], ins["edges"]).then_inc(s_idx, 16)
            sp.dma_start(X[:], ins["x"].rearrange("(t p) d -> p t d", p=R)).then_inc(s_x, 16)
            for t, name in ((ident[:], "ident"), (iota8[:], "iota8"), (attc[:], "attc"), (hmask[:], "hmask"),
                            (iotaU[:], "iotaU"), (before[:], "before")):
                sp.dma_start(t, ins[name]).then_inc(s_const, 16)
            sp.wait_ge(s_zero, 1)
            zeros = Oz[0:R, 0:5000]
            flat8 = logits8.rearrange("(a p b) h -> a p (b h)", p=R, a=5)
            for a in range(5):
                sp.dma_start(flat8[a], zeros).then_inc(s_zeroed, 16)
            sp.dma_start(logits1.rearrange("(p b) h -> p (b h)", p=R), zeros[:, 0:T * N]).then_inc(s_zeroed, 16)
            flat_slots = slot_rows.rearrange("(a p b) d -> a p (b d)", a=NU + 1, p=P)
            for a in range(NU + 1):
                sp.dma_start(flat_slots[a], Oz[:, 0:SU * D]).then_inc(s_zeroed, 16)
            flat_outs = slot_outs.rearrange("(a p b) d -> a p (b d)", a=NU, p=P)
            for a in range(NU):
                sp.dma_start(flat_outs[a], Oz[:, 0:SU * D]).then_inc(s_zeroed, 16)

            sp.wait_ge(s_ohu, ET)
            for g in range(2):
                params(g)
                for side in range(2):
                    n = 2 * g + side
                    if g:
                        sp.wait_ge(s_out, units_before(g, ("table",)))
                    linear_weights(n)
                for side, table in enumerate((src_rows, dst_rows)):
                    for t in range(T):
                        sp.wait_ge(s_frow, T * (2 * g + side) + t + 1)
                        rows = (F if side == 0 else O)[0:R, t, 0:GW]
                        sp.dma_start(table[t * R:(t + 1) * R, :], rows).then_inc(s_tab, 16)
                sp.wait_ge(s_sc, 16 * ETP * (g + 1))
                if g == 0:
                    for t in range(T):
                        if t >= 2:
                            sp.wait_ge(s_lm, 8 * (t - 1))
                        sp.dma_start(ltile[:, t % 2], logits8.rearrange("(t p n) h -> t p n h", t=T, p=R)[t])\
                          .then_inc(s_lt[t % 2], 16)
                else:
                    sp.dma_start(ltile1, logits1.rearrange("(t p n) h -> p t (n h)", t=T, p=R)).then_inc(s_lt[1], 16)
            if sections > 1:
                sp.wait_ge(s_sec, 1)
                router(0)
                def first_weights(u, g, expert):
                    sp.wait_ge(s_lo1, u * NG + g - 1)
                    first_load(g, expert)

                def first_load(g, expert):
                    sp.dma_start(uw1[g % 2], ins["L0_ffn_w1"][bass.ds(expert * NG + g, 1)]
                                 .rearrange("o p n -> p (o n)")).then_inc(s_w1[g % 2], 16)

                def second_weights(u, g, expert):
                    wait(sp, s_lo2, u * NG + g - 1)
                    sp.dma_start(uw2[g % 2], ins["L0_ffn_w2"][bass.ds(expert * NG + g, 1)]
                                 .rearrange("o p n -> p (o n)")).then_inc(s_w2[g % 2], 16)

                def unit_loads(u):
                    sp.wait_ge(s_ut, u * (KD // 2) + KD // 2)
                    sp.dma_start(urows, slot_rows.rearrange("(u s p) d -> u p s d", s=SU, p=P)[bass.ds(u + 1, 1)]
                                 .rearrange("o p s d -> p (o s) d")).then_inc(s_ux, 16)
                    this = sp.value_load(uexp[0:1, bass.ds(u, 1)], min_val=0, max_val=7)
                    then = sp.value_load(uexp[0:1, bass.ds(u + 1, 1)], min_val=0, max_val=7)
                    for g in range(NG):
                        if g + 2 < NG:
                            first_weights(u, g + 2, this)
                        else:
                            first_weights(u + 1, g + 2 - NG, then)
                        if g + 1 < NG:
                            second_weights(u, g + 1, this)
                        else:
                            second_weights(u + 1, 0, then)

                sp.wait_ge(s_plan, 2)
                sp.wait_ge(s_scr, 16 * 2 * T)
                sp.dma_start(urows, slot_rows[0:TU].rearrange("(s p) d -> p s d", s=SU)).then_inc(s_ux, 16)
                units = sp.value_load(nunits[0:1, 0:1], min_val=1, max_val=NU)
                expert = sp.value_load(uexp[0:1, 0:1], min_val=0, max_val=7)
                first_load(0, expert)
                second_weights(0, 0, expert)
                first_load(1, expert)
                unit_loads(0)
                with sp.Fori(1, NU) as u:
                    with sp.If(u < units):
                        unit_loads(u)
            if sections > 2:
                sp.wait_ge(s_sec, 2)
                params(2)
                linear_weights(4)
                linear_weights(5)
                params(3)
            if sections > 3:
                sp.wait_ge(s_sec, 3)
                params(4)
                sp.dma_start(WB[:, 0:768], ins["L1_ffn_w_in"]).then_inc(s_bw, 16)
                sp.dma_start(WB[0:64, 768:1536], ins["L1_ffn_w_out"]).then_inc(s_bw, 16)
            if sections > 4:
                sp.wait_ge(s_sec, 4)
                params(5)
                linear_weights(6)
            if sections > 5:
                sp.wait_ge(s_sec, 5)
                router(1)
                sp.dma_start(WB[:, 0:3456], ins["L2_ffn_w1"]).then_inc(s_m2w, 16)
                sp.dma_start(WB[0:96, 3456:3456 + 4608], ins["L2_ffn_w2"]).then_inc(s_m2w, 16)
                sp.dma_start(WB[0:96, 8064:8070], ins["L2_ffn_b1"]).then_inc(s_m2w, 16)
            if sections > 6:
                sp.wait_ge(s_sec, 6)
                params(6)
                linear_weights(7)
                linear_weights(8)
                params(7)
            if sections > 7:
                sp.wait_ge(s_sec, 7)
                router(2)
                for e in range(2):
                    sp.dma_start(WB[:, 4608 * e:4608 * (e + 1)], ins["L3_ffn_expert_w"][e]).then_inc(s_m3w[e], 16)
                with sp.Fori(1, 4) as j:
                    for u in range(2):
                        sp.wait_ge(s_mb, MB3 + j * (2 * T) + T * (u - 1))
                        sp.dma_start(WB[:, 4608 * u:4608 * (u + 1)],
                                     ins["L3_ffn_expert_w"][bass.ds(j * 2 + u, 1)].rearrange("o p n -> p (o n)"))\
                          .then_inc(s_m3w[u], 16)
            sp.wait_ge(s_sec, sections)
            sp.dma_start(out.rearrange("(t p) d -> p t d", p=R), X[:]).then_inc(s_store, 16)
            sp.wait_ge(s_store, 16)

        @block.gpsimd
        def _(pool):
            def rsqrt(n):
                pool.wait_ge(s_var, n + 1)
                pool.tensor_tensor(rstd[:], var[:], mhalf[:], ALU.pow).then_inc(s_rstd, 1)

            LAG = 6

            def node_numbers(i, u):
                pool.tensor_copy(ixr[:, u % EU, 0:2], idx[:, bass.ds(i, 1), :].rearrange("p o k -> p (o k)"))\
                    .then_inc(s_ends, 1)

            def edge_step(i, u, g, gather=True, scatter=True, more=True):
                base = ETP * g
                if gather:
                    wait(pool, s_kc, base + i)
                    pool.wait_ge(s_ends, base + i + 1)
                    pool.tensor_copy(ixr[:, u, 2:3], key[:, bass.ds(i, 1)]).then_inc(s_kc, 1)
                    pool.indirect_dma_start(
                        out=gs[u], out_offset=None, in_=src_rows,
                        in_offset=bass.IndirectOffsetOnAxis(ap=ixr[:, u, 0:1], axis=0)).then_inc(s_gat[u], 16)
                    pool.indirect_dma_start(
                        out=gd[u], out_offset=None, in_=dst_rows,
                        in_offset=bass.IndirectOffsetOnAxis(ap=ixr[:, u, 1:2], axis=0)).then_inc(s_gat[u], 16)
                else:
                    pool.wait_ge(s_kc, ETP * (g + 1))
                wait(pool, s_lg, base + i - LAG + 1)
                wait(pool, s_sc, 16 * (base + i - LAG))
                if gather and more:
                    node_numbers(i + 1, u + 1)
                if scatter:
                    v = (u - LAG) % EU
                    pool.indirect_dma_start(
                        out=tables[g], out_offset=bass.IndirectOffsetOnAxis(ap=ixr[:, v, 2:3], axis=0),
                        in_=lgr[:, v, 0:HEADS[g]["h"]], in_offset=None).then_inc(s_sc, 16)

            def edges(g):
                pool.wait_ge(s_tab, 16 * 2 * T * (g + 1))
                if g == 0:
                    pool.wait_ge(s_keys, 1)
                    pool.wait_ge(s_zeroed, ZEROED)
                node_numbers(0, 0)
                for i in range(EU):
                    edge_step(i, i, g, scatter=i >= LAG)
                with pool.Fori(1, ETP // EU - 1) as j:
                    for u in range(EU):
                        edge_step(j * EU + u, u, g)
                for i in range(ETP - EU, ETP):
                    edge_step(i, i % EU, g, more=i + 1 < ETP)
                for i in range(ETP, ETP + LAG):
                    edge_step(i, i % EU, g, gather=False)

            pool.wait_ge(s_mh, 1)
            rsqrt(0)
            edges(0)
            rsqrt(1)
            edges(1)
            rsqrt(2)
            if sections > 1:
                rsqrt(3)
                pool.wait_ge(s_slots, 1)
                for k in range(2):
                    for t in range(T):
                        wait(pool, s_scr, 16 * (k * T + t))
                        pool.indirect_dma_start(
                            out=slot_rows, out_offset=bass.IndirectOffsetOnAxis(ap=slots[:, k, t:t + 1], axis=0),
                            in_=XN[0:R, t, :], in_offset=None).then_inc(s_scr, 16)
                pool.wait_ge(s_plan, 2)
                units = pool.value_load(nunits[0:1, 0:1], min_val=1, max_val=NU)

                def unit_store(u):
                    pool.wait_ge(s_uy, u * SU + SU)
                    pool.dma_start(slot_outs.rearrange("(u s p) d -> u p s d", s=SU, p=P)[bass.ds(u, 1)]
                                   .rearrange("o p s d -> p (o s) d"), uout).then_inc(s_us, 16)
                    pool.wait_ge(s_us, u * 16 + 16)

                unit_store(0)
                with pool.Fori(1, NU) as u:
                    with pool.If(u < units):
                        unit_store(u)
                pool.wait_ge(s_left, 1)
                for k in range(2):
                    for t in range(T):
                        pool.indirect_dma_start(
                            out=picked[:, k, t, :], out_offset=None, in_=slot_outs,
                            in_offset=bass.IndirectOffsetOnAxis(ap=slots[:, k, t:t + 1], axis=0)).then_inc(s_yg, 16)
            for n in range(4, RS_COUNT[sections]):
                rsqrt(n)

        @block.tensor
        def _(pe):
            def counts():
                segs = count_segments()

                def tile_counts(i, slot, first, last, k):
                    pe.wait_ge(s_oh, i + 1)
                    for c, a, b, fresh in segs:
                        mm = pe.matmul(PSz[0:R, a:b], oh[0:k, slot, 1, c * R:(c + 1) * R],
                                       oh[0:k, slot, 0, a - c * N:b - c * N],
                                       start=(first and fresh), stop=last, skip_group_check=True)
                    mm.then_inc(s_ohu, 1)

                tile_counts(0, 0, True, False, P)
                tile_counts(1, 1, False, False, P)
                with pe.Fori(1, ET // 2) as j:
                    for u in range(2):
                        tile_counts(j * 2 + u, u, False, False, P)
                tile_counts(ET - 1, 0, False, True, E - (ET - 1) * P)

            def transpose_rows(n, src):
                per = TR_CHUNKS[n] // 2
                for t in range(T):
                    pe.wait_ge(s_rows, T * n + t + 1)
                    for half in range(2):
                        g = 2 * T * n + 2 * t + half
                        wait(pe, s_trc, g - 3)
                        for k in range(per):
                            kk = half * per + k
                            tr = pe.transpose(PS[:, g % 4, k * R:(k + 1) * R],
                                              src[0:R, t, kk * P:(kk + 1) * P], ident[0:R, 0:R])
                        tr.then_inc(s_trp, 1)

            def linear(n):
                kc, width, m = LINEARS[n]
                w = wlin[n % 2][:, 0:kc * width].rearrange("p (k c) -> p k c", k=kc)
                hw = width // 2
                pe.wait_ge(s_wl[n % 2], 16 * (n // 2 + 1))
                for t in range(T):
                    pe.wait_ge(s_trc, 2 * T * m + 2 * t + 2)
                    for half in range(2):
                        g = 2 * T * n + 2 * t + half
                        wait(pe, s_line, g - 3)
                        for k in range(kc):
                            mm = pe.matmul(PS[0:R, 4 + g % 4, 0:hw], XT[:, k, t * R:(t + 1) * R],
                                           w[:, k, half * hw:(half + 1) * hw], start=(k == 0), stop=(k == kc - 1))
                        mm.then_inc(s_linp, 1)

            def edge_turn(i, u, g):
                base = ETP * g
                pe.wait_ge(s_z, base + i + 1)
                wait(pe, s_zr, base + i - 1)
                for k in range(KD):
                    tr = pe.transpose(PSz[:, 1024 * (u % 2) + k * P:1024 * (u % 2) + (k + 1) * P],
                                      gs[u][:, k * P:(k + 1) * P], ident[:])
                tr.then_inc(s_zt, 1)

            def edge_dot(i, u, g):
                base = ETP * g
                pe.wait_ge(s_zr, base + i + 1)
                wait(pe, s_lg, base + i - 1)
                for k in range(KD):
                    mm = pe.matmul(PS[:, 4 + u % 2, 0:8], zr[:, u % 2, k, :], blk[:, g, k, :],
                                   start=(k == 0), stop=(k == KD - 1))
                mm.then_inc(s_dot, 1)

            def edges(g):
                for i in range(EU):
                    edge_turn(i, i, g)
                    if i:
                        edge_dot(i - 1, i - 1, g)
                with pe.Fori(1, ETP // EU) as j:
                    for u in range(EU):
                        edge_turn(j * EU + u, u, g)
                        edge_dot(j * EU + (u - 1), (u - 1) % EU, g)
                edge_dot(ETP - 1, EU - 1, g)

            def attend(n):
                h, c, kind = HEADS[n]["h"], HEADS[n]["c"], HEADS[n]["kind"]
                soft = units_before(n, ("table", "gat"))
                gat = units_before(n, ("gat",))
                every = units_before(n, ("table", "gat", "average"))
                gats = sum(s["kind"] == "gat" for s in HEADS[:n])
                heads = sum(s["h"] for s in HEADS[:n] if s["kind"] == "gat")
                units = T * h
                place = unit_place(n)

                def broadcast(head):
                    wait(pe, s_v, gat + T * head)
                    for a, b in ((0, 512), (512, N)):
                        mm = pe.matmul(PSz[0:R, a:b], ident[0:h, head:head + 1].to_broadcast([h, R]),
                                       AT[0:h].rearrange("h t n -> h (t n)")[:, a:b], start=True, stop=True)
                    mm.then_inc(s_bc, 1)

                def turn(s):
                    t = place(s)[1]
                    if kind == "average":
                        src = C[:, t, :]
                    else:
                        pe.wait_ge(s_p, soft + s + 1)
                        src = W[0:R, s % 4, :]
                    wait(pe, s_pt, every + s - 1)
                    for b in range(T):
                        tr = pe.transpose(PSz[0:R, 1024 * (1 + s % 2) + b * P:1024 * (1 + s % 2) + b * P + R],
                                          src[:, b * R:(b + 1) * R], ident[0:R, 0:R])
                    tr.then_inc(s_tp, 1)

                def sum_up(s):
                    head, t = place(s)
                    pe.wait_ge(s_pt, every + s + 1)
                    wide = c > 512
                    wait(pe, s_out, every + s if wide else every + s - 1)
                    for half in range(2 if wide else 1):
                        cw = c // 2 if wide else c
                        col = head * c + half * cw
                        bank = 6 + (half if wide else s % 2)
                        for b in range(T):
                            mm = pe.matmul(PS[0:R, bank, 0:cw], PT[0:R, s % 2, b, :],
                                           F[0:R, b, col:col + cw], start=(b == 0), stop=(b == T - 1))
                    mm.then_inc(s_op, 1)

                pe.wait_ge(s_line, 2 * T * LINEARS_DONE[n])
                if kind == "gat":
                    pe.wait_ge(s_att, gats + 1)
                    for t in range(T):
                        tr = pe.transpose(PSz[0:h, t * P:t * P + R], a_s[:, t, 0:h], ident[0:R, 0:R])
                    tr.then_inc(s_astp, 1)
                    pe.wait_ge(s_ast, gats + 1)
                    broadcast(0)
                for s in range(units):
                    if kind == "gat" and place(s)[1] == T - 1 and place(s)[0] + 1 < h:
                        broadcast(place(s)[0] + 1)
                    turn(s)
                    if s:
                        sum_up(s - 1)
                sum_up(units - 1)

            def route(n, m):
                e = N_EXP[n]
                pe.wait_ge(s_rw, 48 * (n + 1))
                for t in range(T):
                    pe.wait_ge(s_trc, 2 * T * m + 2 * t + 2)
                    for k in range(KD):
                        mm = pe.matmul(PS[0:R, 4, t * 8:t * 8 + e], XT[:, k, t * R:(t + 1) * R], rw[:, k, 0:e],
                                       start=(k == 0), stop=(k == KD - 1))
                mm.then_inc(s_rtp, 1)

            def mix_bias(n):
                e = N_EXP[n]
                pe.wait_ge(s_comb, n + 1)
                for t in range(T):
                    tr = pe.transpose(PSz[0:8, t * P:t * P + R], comb[:, t, :], ident[0:R, 0:R])
                tr.then_inc(s_mbt, 1)
                pe.wait_ge(s_mbc, n + 1)
                for t in range(T):
                    g = T * n + t
                    wait(pe, s_mixd, g - 1)
                    for half in range(2):
                        mm = pe.matmul(PS[0:R, 4 + 2 * (g % 2) + half, 0:384], AT[0:e, t, :],
                                       mixb[0:e, half * 384:(half + 1) * 384], start=True, stop=True)
                    mm.then_inc(s_mixp, 1)

            def expert_out(done, t, u, lhs, rhs, last_u=None):
                wait(pe, s_md, done - 1)
                k_all = len(lhs)
                for half in range(2):
                    for k in range(k_all):
                        mm = pe.matmul(PS[0:R, 4 + 2 * (u % 2) + half, 0:384], lhs[k](t),
                                       rhs[k][:, half * 384:(half + 1) * 384], start=(k == 0), stop=(k == k_all - 1))
                mm.then_inc(s_mb, 1)

            def ranks():
                pe.wait_ge(s_pick, 1)
                for t in range(T):
                    for b in range(t + 1):
                        pe.matmul(PS[0:R, 5, t * 8:(t + 1) * 8], before[:] if b == t else ones[0:R, 0:R],
                                  pick[:, 2, b, :], start=(b == 0), stop=(b == t))
                for t in range(T):
                    mm = pe.matmul(PS[:, 6, 0:8], ones[0:R, :], pick[:, 2, t, :], start=(t == 0), stop=(t == T - 1))
                mm.then_inc(s_rank, 1)

            def mixture0():
                def turn(u):
                    pe.wait_ge(s_ux, u * 16 + 16)
                    wait(pe, s_ug, u * (NG * FC))
                    for b in range(KD // 2):
                        for k in range(2):
                            for s in range(SU):
                                tr = pe.transpose(PS[:, b, k * TU + s * P:k * TU + (s + 1) * P],
                                                  urows[:, s, (2 * b + k) * P:(2 * b + k + 1) * P], ident[:])
                        tr.then_inc(s_ut, 1)

                def three(out, w, x, first, last):
                    for n, (i, j) in enumerate(((0, 0), (0, 1), (1, 0))):
                        mm = pe.matmul(out, w(i), x(j), start=first and n == 0, stop=last and n == 2)
                    return mm

                def first(u, g):
                    pe.wait_ge(s_lo1, u * NG + g + 1)
                    if g == 0:
                        pe.wait_ge(s_ul, u * (KD // 2) + KD // 2)
                    for c in range(FC):
                        q = g * FC + c
                        wait(pe, s_ug, u * (NG * FC) + q - 3)
                        for k in range(KD):
                            mm = three(PS[:, q % 4, 0:TU],
                                       lambda i: w1s[:, g % 2, i, (k * FC + c) * P:(k * FC + c + 1) * P],
                                       lambda j: urowsT2[:, j, k * TU:(k + 1) * TU], k == 0, k == KD - 1)
                        mm.then_inc(s_ua, 1)

                def second(u, g):
                    pe.wait_ge(s_lo2, u * NG + g + 1)
                    if g == 0:
                        wait(pe, s_uy, u * SU)
                    pe.wait_ge(s_hl, u * NG + g + 1)
                    for s in range(SU):
                        for half in range(2):
                            for c in range(FC):
                                mm = three(PS[:, 4 + 2 * s + half, 0:384],
                                           lambda i: hid2[:, g % 2, i, c * TU + s * P:c * TU + (s + 1) * P],
                                           lambda j: w2s[:, g % 2, j, c * D + half * 384:c * D + (half + 1) * 384],
                                           g == 0 and c == 0, g == NG - 1 and c == FC - 1)
                    mm.then_inc(s_ub, 1)

                def unit(u):
                    for g in range(NG - 1):
                        first(u, g + 1)
                        second(u, g)
                    turn(u + 1)
                    second(u, NG - 1)
                    first(u + 1, 0)

                pe.wait_ge(s_plan, 2)
                units = pe.value_load(nunits[0:1, 0:1], min_val=1, max_val=NU)
                turn(0)
                first(0, 0)
                unit(0)
                with pe.Fori(1, NU) as u:
                    with pe.If(u < units):
                        unit(u)

            def mixture1():
                w1 = WB[:, 0:3456].rearrange("p (e k f) -> p e k f", e=6, k=KD)
                w2 = WB[0:96, 3456:3456 + 4608].rearrange("p (e d) -> p e d", e=6)
                hT = Oz[0:96, 0:2 * N].rearrange("p (u n) -> p u n", u=2)
                pe.wait_ge(s_m2w, 48)
                for e in range(6):
                    for hf, (a, b) in enumerate(HALVES):
                        q = 2 * e + hf
                        wait(pe, s_mg, MG1 + q - 3)
                        for k in range(KD):
                            mm = pe.matmul(PS[0:96, q % 4, 0:b - a], w1[:, e, k, :], XT[:, k, a:b],
                                           start=(k == 0), stop=(k == KD - 1))
                        mm.then_inc(s_ma, 1)
                    pe.wait_ge(s_mg, MG1 + 2 * e + 2)
                    for t in range(T):
                        d = MB1 + T * e + t
                        expert_out(d, t, d, [lambda t: hT[:, e % 2, t * R:(t + 1) * R]], [w2[:, e, :]])

            def mixture2():
                w = WB[:, 0:9216].rearrange("p (u k d) -> p u k d", u=2, k=KD)

                def two_experts(j):
                    for u in range(2):
                        pe.wait_ge(s_m3w[u], j * 16 + 16)
                        for t in range(T):
                            d = u * T + t
                            expert_out(MB3 + d + j * (2 * T), t, MB3 + d,
                                       [lambda t, k=k: XT[:, k, t * R:(t + 1) * R] for k in range(KD)],
                                       [w[:, u, k, :] for k in range(KD)])

                two_experts(0)
                with pe.Fori(1, 4) as j:
                    two_experts(j)

            def bit_layer():
                w1 = WB[:, 0:768].rearrange("p (k o) -> p k o", k=KD)
                pe.wait_ge(s_babs, 1)
                pe.matmul(PS[:, 4, 0:2], ones[:], ws[:, 0:2], start=True, stop=True).then_inc(s_bpe, 1)
                transpose_rows(5, O)
                pe.wait_ge(s_bwq, 1)
                for t in range(T):
                    pe.wait_ge(s_trc, 2 * T * 5 + 2 * t + 2)
                    for k in range(KD):
                        mm = pe.matmul(PS[0:R, 5 + t // 3, (t % 3) * P:(t % 3 + 1) * P],
                                       XT[:, k, t * R:(t + 1) * R], w1[:, k, :], start=(k == 0), stop=(k == KD - 1))
                mm.then_inc(s_bpe, 1)
                pe.wait_ge(s_bq2, 1)
                for t in range(T):
                    tr = pe.transpose(PSz[0:64, t * P:t * P + R], O[0:R, t, 0:64], ident[0:R, 0:R])
                tr.then_inc(s_bpe, 1)
                pe.wait_ge(s_bqt, 1)
                for t in range(T):
                    wait(pe, s_badd, t - 1)
                    for half in range(2):
                        mm = pe.matmul(PS[0:R, 4 * (t % 2) + 2 + half, 0:384], hidT[:, t, :],
                                       WB[0:64, 768 + half * 384:768 + (half + 1) * 384], start=True, stop=True)
                    mm.then_inc(s_bout, 1)

            pe.wait_ge(s_const, 112)
            counts()
            pe.wait_ge(s_cnt, 1)
            for g in range(2):
                transpose_rows(g, XN)
                linear(2 * g)
                linear(2 * g + 1)
                edges(g)
                attend(g)
            if sections > 1:
                transpose_rows(2, XN)
                route(0, 2)
                mix_bias(0)
                pe.wait_ge(s_mixd, T)
                ranks()
                mixture0()
            if sections > 2:
                transpose_rows(3, XN)
                linear(4)
                attend(2)
                transpose_rows(4, O)
                linear(5)
                attend(3)
            if sections > 3:
                bit_layer()
            if sections > 4:
                transpose_rows(6, XN)
                linear(6)
                attend(4)
            if sections > 5:
                transpose_rows(7, XN)
                route(1, 7)
                mix_bias(1)
                pe.wait_ge(s_mixd, 2 * T)
                mixture1()
            if sections > 6:
                transpose_rows(8, XN)
                linear(7)
                attend(5)
                transpose_rows(9, O)
                linear(8)
                attend(6)
            if sections > 7:
                transpose_rows(10, XN)
                route(2, 10)
                mix_bias(2)
                pe.wait_ge(s_mixd, 3 * T)
                mixture2()

        @block.scalar
        def _(act):
            def transpose_rows(n):
                per = TR_CHUNKS[n] // 2
                for t in range(T):
                    for half in range(2):
                        g = 2 * T * n + 2 * t + half
                        act.wait_ge(s_trp, g + 1)
                        act.copy(XT[:, half * per:(half + 1) * per, t * R:(t + 1) * R],
                                 PS[:, g % 4, 0:per * R].rearrange("p (k n) -> p k n", k=per)).then_inc(s_trc, 1)

            def edge_relu(i, u, g):
                base = ETP * g
                act.wait_ge(s_zt, base + i + 1)
                wait(act, s_dot, base + i - 1)
                act.activation(zr[:, u % 2, :, :].rearrange("p k c -> p (k c)"),
                               PSz[:, 1024 * (u % 2):1024 * (u % 2) + D], ACT.Relu).then_inc(s_zr, 1)

            def edges(g):
                for i in range(EU):
                    edge_relu(i, i, g)
                with act.Fori(1, ETP // EU) as j:
                    for u in range(EU):
                        edge_relu(j * EU + u, u, g)

            def attend(n):
                h, kind = HEADS[n]["h"], HEADS[n]["kind"]
                soft = units_before(n, ("table", "gat"))
                every = units_before(n, ("table", "gat", "average"))
                gats = sum(s["kind"] == "gat" for s in HEADS[:n])
                heads = sum(s["h"] for s in HEADS[:n] if s["kind"] == "gat")
                units = T * h
                place = unit_place(n)
                if kind == "gat":
                    act.wait_ge(s_astp, gats + 1)
                    act.copy(AT[0:h], PSz[0:h, 0:T * P].rearrange("h (t n) -> h t n", t=T)[:, :, 0:R])\
                       .then_inc(s_ast, 1)
                for s in range(units + 2):
                    if kind == "gat" and s < units:
                        head, t = place(s)
                        act.wait_ge(s_bc, heads + head + 1)
                        wait(act, s_tp, every + s - 3)
                        act.activation(W[0:R, s % 4, :], PSz[0:R, 0:N], ACT.Identity,
                                       bias=a_d[:, t, head:head + 1]).then_inc(s_v, 1)
                    if kind != "average" and 1 <= s <= units:
                        v = s - 1
                        act.wait_ge(s_lm, soft + v + 1)
                        act.activation(W[0:R, v % 4, :], W[0:R, v % 4, :], ACT.Exp, bias=nmx[:, v % 4:v % 4 + 1])\
                           .then_inc(s_e, 1)
                    if s >= 2:
                        v = s - 2
                        act.wait_ge(s_tp, every + v + 1)
                        wait(act, s_op, every + v - 1)
                        act.copy(PT[0:R, v % 2],
                                 PSz[0:R, 1024 * (1 + v % 2):1024 * (1 + v % 2) + T * P]
                                 .rearrange("p (b n) -> p b n", b=T)[:, :, 0:R]).then_inc(s_pt, 1)

            def elu_exp(g):
                for t in range(T):
                    act.wait_ge(s_neg, T * g + t + 1)
                    act.activation(F[0:R, t, 0:D], F[0:R, t, 0:D], ACT.Exp).then_inc(s_elu, 1)

            def route(n):
                act.wait_ge(s_gap, n + 1)
                act.activation(gate[:, 1, :], gate[:, 0, :], ACT.Exp)
                e = N_EXP[n]
                for t in range(T):
                    a = act.activation(comb2[:, t, 0:e], LG[:, t, 0:e], ACT.Exp, bias=gate[:, 2, t:t + 1],
                                       accum_out=gate[:, 3, t:t + 1])
                a.then_inc(s_gex, 1)

            def mix_bias(n):
                act.wait_ge(s_mbt, n + 1)
                act.copy(AT[0:8], PSz[0:8, 0:T * P].rearrange("h (t n) -> h t n", t=T)[:, :, 0:R])\
                   .then_inc(s_mbc, 1)

            def mixture0():
                def round_rows(u):
                    for b in range(KD // 2):
                        act.wait_ge(s_ut, u * (KD // 2) + b + 1)
                        act.copy(urowsT2[:, 0, 2 * b * TU:2 * (b + 1) * TU], PS[:, b, 0:2 * TU]).then_inc(s_uc, 1)

                def round_first(u, g):
                    act.wait_ge(s_w1[g % 2], u * (16 * NG // 2) + 16 * (g // 2 + 1))
                    wait(act, s_ua, u * (NG * FC) + (g - 1) * FC)
                    act.copy(w1s[:, g % 2, 0, :], uw1[g % 2][:, 0:G1 - FC]).then_inc(s_hi1, 1)

                def round_second(u, g):
                    act.wait_ge(s_w2[g % 2], u * (16 * NG // 2) + 16 * (g // 2 + 1))
                    wait(act, s_ub, u * NG + g - 1)
                    act.copy(w2s[:, g % 2, 0, :], uw2[g % 2]).then_inc(s_hi2, 1)

                def hidden(u, g):
                    wait(act, s_hl, u * NG + g - 1)
                    for c in range(FC):
                        q = g * FC + c
                        act.wait_ge(s_ua, u * (NG * FC) + q + 1)
                        act.activation(hid[:, g % 2, c * TU:(c + 1) * TU], PS[:, q % 4, 0:TU], ACT.Gelu,
                                       bias=b1c[:, g % 2, c:c + 1]).then_inc(s_ug, 1)

                def unit(u):
                    for g in range(NG):
                        hidden(u, g)
                        if g + 2 < NG:
                            round_first(u, g + 2)
                        else:
                            round_first(u + 1, g + 2 - NG)
                        if g + 1 < NG:
                            round_second(u, g + 1)
                    round_second(u + 1, 0)
                    round_rows(u + 1)

                act.wait_ge(s_plan, 2)
                units = act.value_load(nunits[0:1, 0:1], min_val=1, max_val=NU)
                round_rows(0)
                round_first(0, 0)
                round_second(0, 0)
                round_first(0, 1)
                unit(0)
                with act.Fori(1, NU) as u:
                    with act.If(u < units):
                        unit(u)

            def mixture1():
                hT = Oz[0:96, 0:2 * N].rearrange("p (u n) -> p u n", u=2)
                act.wait_ge(s_m2w, 48)
                for e in range(6):
                    wait(act, s_mb, MB1 + T * (e - 1))
                    for hf, (a, b) in enumerate(HALVES):
                        q = 2 * e + hf
                        act.wait_ge(s_ma, MG1 + q + 1)
                        act.activation(hT[:, e % 2, a:b], PS[0:96, q % 4, 0:b - a], ACT.Gelu,
                                       bias=WB[0:96, 8064 + e:8065 + e]).then_inc(s_mg, 1)

            def bit_layer():
                act.wait_ge(s_bw, 32)
                act.wait_ge(s_bclr, 1)
                act.activation(WB[:, 1536:2304], WB[:, 0:768], ACT.Abs, accum_out=ws[:, 0:1])
                act.activation(WB[0:64, 2304:3072], WB[0:64, 768:1536], ACT.Abs, accum_out=ws[0:64, 1:2])\
                   .then_inc(s_babs, 1)
                for t in range(T):
                    act.wait_ge(s_by, t + 1)
                    act.activation(F[0:R, t, 0:D], O[0:R, t, 0:D], ACT.Abs).then_inc(s_bya, 1)
                transpose_rows(5)
                act.wait_ge(s_bh, 1)
                act.activation(F[0:R, 0:T, 0:64], O[0:R, 0:T, 192:256], ACT.Silu).then_inc(s_bsil, 1)
                act.wait_ge(s_by2, 1)
                act.activation(F[0:R, 0:T, 512:576], O[0:R, 0:T, 64:128], ACT.Abs).then_inc(s_bya, 1)
                act.wait_ge(s_bpe, 3)
                act.copy(hidT, PSz[0:64, 0:T * P].rearrange("h (t n) -> h t n", t=T)[:, :, 0:R]).then_inc(s_bqt, 1)

            for g in range(2):
                transpose_rows(g)
                edges(g)
                attend(g)
                elu_exp(g)
            if sections > 1:
                transpose_rows(2)
                route(0)
                mix_bias(0)
                mixture0()
            if sections > 2:
                transpose_rows(3)
                attend(2)
                transpose_rows(4)
                attend(3)
            if sections > 3:
                bit_layer()
            if sections > 4:
                transpose_rows(6)
                attend(4)
            if sections > 5:
                transpose_rows(7)
                route(1)
                mix_bias(1)
                mixture1()
            if sections > 6:
                transpose_rows(8)
                attend(5)
                transpose_rows(9)
                attend(6)
            if sections > 7:
                transpose_rows(10)
                route(2)
                mix_bias(2)

        @block.vector
        def _(dve):
            linked = [0]

            def link(ins):
                linked[0] += 1
                ins.then_inc(s_link, 1)
                dve.wait_ge(s_link, linked[0])

            def params(g):
                dve.wait_ge(s_par, 16 * par_total[g + 1])
                return PARAMS[g][0]

            def rows(t, buf, width=D):
                return buf[0:R, t, 0:width]

            def layer_norm(n, src, dst, tr=None, w=None, b=None, width=D):
                for t in range(T):
                    for half in range(2):
                        ins = dve.bn_stats(stats[:, t, half, :], src[0:R, t, half * 384:(half + 1) * 384])
                link(ins)
                for t in range(T):
                    ins = dve.bn_aggr(mv[:, t, :], stats[:, t].rearrange("p h s -> p (h s)"))
                link(ins)
                dve.tensor_scalar(var[:], mv[:, :, 1], LN_EPS, None, ALU.add).then_inc(s_var, 1)
                dve.wait_ge(s_rstd, n + 1)
                for t in range(T):
                    if w is None:
                        ins = dve.tensor_scalar(rows(t, dst), rows(t, src), mv[:, t, 0:1], rstd[:, t:t + 1],
                                                ALU.subtract, ALU.mult)
                    else:
                        link(dve.scalar_tensor_tensor(out=rows(t, dst), in0=rows(t, src), scalar=mv[:, t, 0:1],
                                                      in1=w, op0=ALU.subtract, op1=ALU.mult))
                        ins = dve.scalar_tensor_tensor(out=rows(t, dst), in0=rows(t, dst), scalar=rstd[:, t:t + 1],
                                                       in1=b, op0=ALU.mult, op1=ALU.add)
                    if tr is not None:
                        ins.then_inc(s_rows, 1)
                if tr is None:
                    link(ins)

            def counts():
                def onehots(i, slot):
                    wait(dve, s_ohu, i - 1)
                    for side in range(2):
                        ins = dve.tensor_scalar(oh[:, slot, side, :], iota, idf[:, side, bass.ds(i, 1)], None,
                                                ALU.is_equal)
                    ins.then_inc(s_oh, 1)

                onehots(0, 0)
                onehots(1, 1)
                with dve.Fori(1, ET // 2) as j:
                    for u in range(2):
                        onehots(j * 2 + u, u)
                onehots(ET - 1, 0)
                dve.wait_ge(s_ohu, ET)
                ins = dve.tensor_copy(Cz, PSz[0:R, 0:T * N])
                ins.then_inc(s_cnt, 1)
                dve.wait_ge(s_cnt, 1)
                link(dve.tensor_scalar(NEGz, Cz, 0.5, NEGBIG, ALU.is_lt, ALU.mult))

            def edge_rows(n, g, side):
                buf = (F, O)[side]
                for t in range(T):
                    for half in range(2):
                        q = 2 * T * n + 2 * t + half
                        dve.wait_ge(s_linp, q + 1)
                        dve.tensor_tensor(buf[0:R, t, half * 384:(half + 1) * 384], PS[0:R, 4 + q % 4, 0:384],
                                          PB[0:R, side * D + half * 384:side * D + (half + 1) * 384], ALU.add)\
                           .then_inc(s_line, 1)
                    if g:
                        link(dve.memset(buf[0:R, t, D:GW], 0.0))
                    dve.wait_ge(s_line, q + 1)
                    link(dve.scalar_tensor_tensor(out=TMP[:, 0:D], in0=rows(t, buf), scalar=0.2,
                                                  in1=par(2, D), op0=ALU.mult, op1=ALU.mult))
                    h = HEADS[g]["h"]
                    dve.tensor_reduce(buf[0:R, t, D:D + h], TMP[:, 0:D].rearrange("p (h c) -> p h c", h=h),
                                      AX_X, ALU.add).then_inc(s_frow, 1)

            def edges(g):
                base = ETP * g

                def add(i, u, rounds):
                    dve.wait_ge(s_gat[u], rounds + 32 * (ETP // EU) * g + 32)
                    dve.tensor_tensor(gs[u], gs[u], gd[u], ALU.add).then_inc(s_z, 1)

                def finish(i, u):
                    dve.wait_ge(s_dot, base + i + 1)
                    wait(dve, s_sc, 16 * (base + i - 7))
                    dve.wait_ge(s_z, base + i + 1)
                    dve.tensor_tensor(lgr[:, u, :], PS[:, 4 + u % 2, 0:8], gs[u][:, D:GW], ALU.add)\
                       .then_inc(s_lg, 1)

                for i in range(2 * EU):
                    add(i, i % EU, 32 * (i // EU))
                    if i >= 2:
                        finish(i - 2, (i - 2) % EU)
                with dve.Fori(2, ETP // EU) as j:
                    for u in range(EU):
                        add(j * EU + u, u, j * 32)
                        finish(j * EU + (u - 2), (u - 2) % EU)
                for i in (ETP - 2, ETP - 1):
                    finish(i, i % EU)

            def attend(n):
                h, c, kind = HEADS[n]["h"], HEADS[n]["c"], HEADS[n]["kind"]
                soft = units_before(n, ("table", "gat"))
                gat = units_before(n, ("gat",))
                every = units_before(n, ("table", "gat", "average"))
                units = T * h
                place = unit_place(n)

                def front(s):
                    head, t = place(s)
                    r = s % 4
                    w = W[0:R, r, :]
                    if kind == "gat":
                        dve.wait_ge(s_v, gat + s + 1)
                        link(dve.scalar_tensor_tensor(out=w, in0=w, scalar=0.2, in1=w, op0=ALU.mult, op1=ALU.max))
                        src = w
                    else:
                        wait(dve, s_tp, every + s - 3)
                        if n == 0:
                            dve.wait_ge(s_lt[t % 2], 16 * (t // 2 + 1))
                            src = ltile[:, t % 2, :, head]
                        else:
                            dve.wait_ge(s_lt[1], 16 * 3)
                            src = ltile1[:, t, :]
                    link(dve.tensor_tensor_reduce(out=w, in0=src, in1=NEG[:, t, :], scale=1.0, scalar=-3.0e38,
                                                  op0=ALU.add, op1=ALU.max, accum_out=mx[:, r:r + 1]))
                    dve.tensor_scalar(nmx[:, r:r + 1], mx[:, r:r + 1], -1.0, None, ALU.mult).then_inc(s_lm, 1)

                def back(s):
                    head, t = place(s)
                    r = s % 4
                    dve.wait_ge(s_e, soft + s + 1)
                    link(dve.tensor_tensor_reduce(out=W[0:R, r, :], in0=W[0:R, r, :], in1=C[:, t, :], scale=1.0,
                                                  scalar=TINY, op0=ALU.mult, op1=ALU.add, accum_out=den[:, r:r + 1]))
                    dve.reciprocal(rden[:, s % 8:s % 8 + 1], den[:, r:r + 1]).then_inc(s_p, 1)

                def evacuate(s):
                    head, t = place(s)
                    dve.wait_ge(s_op, every + s + 1)
                    if kind == "average":
                        scale = dinv[:, t:t + 1]
                    else:
                        dve.wait_ge(s_p, soft + s + 1)
                        scale = rden[:, s % 8:s % 8 + 1]
                    if c > 512:
                        o, i = O[0:R, t, 0:c].rearrange("p (a c) -> p a c", a=2), PS[0:R, 6:8, 0:c // 2]
                    else:
                        o, i = O[0:R, t, head * c:(head + 1) * c], PS[0:R, 6 + s % 2, 0:c]
                    dve.tensor_scalar(o, i, scale, None, ALU.mult).then_inc(s_out, 1)

                for s in range(units + 3):
                    if kind != "average" and s < units:
                        front(s)
                    if kind != "average" and 1 <= s <= units:
                        back(s - 1)
                    if s >= 3:
                        evacuate(s - 3)
                dve.wait_ge(s_out, every + units)

            def elu(g):
                for t in range(T):
                    dve.tensor_scalar(rows(t, F), rows(t, O), 0.0, None, ALU.min).then_inc(s_neg, 1)
                for t in range(T):
                    dve.wait_ge(s_elu, T * g + t + 1)
                    link(dve.scalar_tensor_tensor(out=rows(t, O), in0=rows(t, O), scalar=0.0, in1=rows(t, F),
                                                  op0=ALU.max, op1=ALU.add))
                    if g == 0:
                        ins = dve.scalar_tensor_tensor(out=rows(t, O), in0=rows(t, O), scalar=-1.0, in1=rows(t, XN),
                                                       op0=ALU.add, op1=ALU.add)
                    else:
                        ins = dve.tensor_scalar(rows(t, O), rows(t, O), -1.0, None, ALU.add)
                link(ins)

            def attention_terms(n, width, h):
                for t in range(T):
                    hw = width // 2
                    for half in range(2):
                        q = 2 * T * n + 2 * t + half
                        dve.wait_ge(s_linp, q + 1)
                        dve.tensor_copy(F[0:R, t, half * hw:(half + 1) * hw], PS[0:R, 4 + q % 4, 0:hw])\
                           .then_inc(s_line, 1)
                    dve.wait_ge(s_line, q + 1)
                    for side, (tmp, a) in enumerate(((TMP, a_s), (TMP2, a_d))):
                        link(dve.tensor_tensor(tmp[:, 0:width], rows(t, F, width), par(side, width), ALU.mult))
                        ins = dve.tensor_reduce(a[:, t, 0:h], tmp[:, 0:width].rearrange("p (h c) -> p h c", h=h),
                                                AX_X, ALU.add)
                        if side == 0 or t < T - 1:
                            link(ins)
                ins.then_inc(s_att, 1)

            def scaled_rows(n):
                for t in range(T):
                    for half in range(2):
                        q = 2 * T * n + 2 * t + half
                        dve.wait_ge(s_linp, q + 1)
                        dve.tensor_scalar(F[0:R, t, half * 384:(half + 1) * 384], PS[0:R, 4 + q % 4, 0:384],
                                          dinv[:, t:t + 1], None, ALU.mult).then_inc(s_line, 1)

            def bias_relu(width, slot):
                for t in range(T):
                    link(dve.tensor_tensor(rows(t, O, width), rows(t, O, width), par(slot, width), ALU.add))
                    ins = dve.tensor_scalar(rows(t, O, width), rows(t, O, width), 0.0, None, ALU.max)
                    ins.then_inc(s_rows, 1)

            def add_to_x(slot, last=True):
                for t in range(T):
                    if slot is not None:
                        link(dve.tensor_tensor(rows(t, O), rows(t, O), par(slot, D), ALU.add))
                    ins = dve.tensor_tensor(X[:, t, :], X[:, t, :], rows(t, O), ALU.add)
                link(ins)

            def route(n):
                e = N_EXP[n]
                dve.wait_ge(s_rtp, n + 1)
                dve.wait_ge(s_rw, 48 * (n + 1))
                if e < 8:
                    dve.memset(LG[:, :, e:8], NEGBIG)
                for t in range(T):
                    ins = dve.tensor_tensor(LG[:, t, 0:e], PS[0:R, 4, t * 8:t * 8 + e], rb[:, 0:e], ALU.add)
                link(ins)
                for t in range(T):
                    ins = dve.max(top[:, t, :], LG[:, t, :])
                link(ins)
                for t in range(T):
                    ins = dve.max_index(topi[:, t, :], top[:, t, :], LG[:, t, :])
                dve.tensor_tensor(gate[:, 0, :], top[:, :, 1], top[:, :, 0], ALU.subtract)
                dve.tensor_scalar(gate[:, 2, :], top[:, :, 0], -1.0, None, ALU.mult).then_inc(s_gap, 1)
                dve.wait_ge(s_gap, n + 1)
                link(dve.tensor_copy(topf[:], topi[:]))
                dve.wait_ge(s_gex, n + 1)
                link(dve.tensor_scalar(gate[:, 4, :], gate[:, 1, :], 1.0, None, ALU.add))
                if n == 2:
                    link(dve.scalar_tensor_tensor(out=gate[:, 4, :], in0=gate[:, 3, :], scalar=1.0e-9,
                                                  in1=gate[:, 4, :], op0=ALU.mult, op1=ALU.add))
                link(dve.reciprocal(gate[:, 5, :], gate[:, 4, :]))
                link(dve.tensor_tensor(gate[:, 6, :], gate[:, 5, :], gate[:, 1, :], ALU.mult))
                for t in range(T):
                    dve.tensor_scalar(comb[:, t, :], iota8[0:R], topf[:, t, 0:1], gate[:, 5, t:t + 1],
                                      ALU.is_equal, ALU.mult)
                    ins = dve.tensor_scalar(comb2[:, t, :], iota8[0:R], topf[:, t, 1:2], gate[:, 6, t:t + 1],
                                            ALU.is_equal, ALU.mult)
                link(ins)
                dve.tensor_tensor(comb[:], comb[:], comb2[:], ALU.add).then_inc(s_comb, 1)
                dve.wait_ge(s_comb, n + 1)

            def in_halves(ap):
                return ap.rearrange("p (a c) -> p a c", a=2)

            def mix_bias(n):
                for t in range(T):
                    g = T * n + t
                    dve.wait_ge(s_mixp, g + 1)
                    bank = 4 + 2 * (g % 2)
                    dve.tensor_tensor(in_halves(X[:, t, :]), PS[0:R, bank:bank + 2, 0:384], in_halves(X[:, t, :]),
                                      ALU.add).then_inc(s_mixd, 1)
                dve.wait_ge(s_mixd, T * (n + 1))

            def add_expert(done, t, parity, e):
                dve.wait_ge(s_mb, done + 1)
                wait(dve, s_md, done)
                bank = 4 + 2 * (parity % 2)
                dve.scalar_tensor_tensor(out=in_halves(X[:, t, :]), in0=PS[0:R, bank:bank + 2, 0:384],
                                         scalar=comb[:, t, bass.ds(e, 1)] if not isinstance(e, int) else comb[:, t, e:e + 1],
                                         in1=in_halves(X[:, t, :]), op0=ALU.mult, op1=ALU.add).then_inc(s_md, 1)

            def make_plan():
                for t in range(T):
                    for k in range(2):
                        ins = dve.tensor_scalar(pick[:, k, t, :], iota8[0:R], topf[:, t, k:k + 1], None, ALU.is_equal)
                link(ins)
                dve.tensor_tensor(pick[:, 2], pick[:, 0], pick[:, 1], ALU.add).then_inc(s_pick, 1)
                dve.wait_ge(s_rank, 1)
                units, start, end = plan[:, 0, :], plan[:, 1, :], plan[:, 2, :]
                link(dve.tensor_scalar(units, PS[:, 6, 0:8], 0.5, None, ALU.is_gt))
                for full in range(TU, N, TU):
                    link(dve.scalar_tensor_tensor(out=units, in0=PS[:, 6, 0:8], scalar=full + 0.5, in1=units,
                                                  op0=ALU.is_gt, op1=ALU.add))
                link(dve.tensor_copy(plan[:, 2, 0:1], plan[:, 0, 0:1]))
                for e in range(1, 8):
                    link(dve.tensor_tensor(plan[:, 2, e:e + 1], plan[:, 2, e - 1:e], plan[:, 0, e:e + 1], ALU.add))
                link(dve.tensor_tensor(start, end, units, ALU.subtract))
                for t in range(T):
                    ins = dve.scalar_tensor_tensor(out=place_of[:, t, :], in0=start[0:R], scalar=float(TU),
                                                   in1=PS[0:R, 5, t * 8:(t + 1) * 8], op0=ALU.mult, op1=ALU.add)
                link(ins)
                for k in range(2):
                    ins = dve.tensor_tensor(pick[:, k], pick[:, k], place_of[:], ALU.mult)
                link(ins)
                for k in range(2):
                    ins = dve.tensor_reduce(slotf[:, k, :], pick[:, k], AX_X, ALU.add)
                link(ins)
                dve.wait_ge(s_rows, 3 * T)
                dve.tensor_copy(slots[:], slotf[:]).then_inc(s_slots, 1)
                link(dve.memset(uexpf[:], 0.0))
                for e in range(8):
                    link(dve.scalar_tensor_tensor(out=uexpf[:], in0=iotaU[:], scalar=plan[:, 2, e:e + 1], in1=uexpf[:],
                                                  op0=ALU.is_ge, op1=ALU.add))
                dve.tensor_scalar(uexp[:], uexpf[:], 7.0, None, ALU.min).then_inc(s_plan, 1)
                dve.tensor_copy(nunits[:], plan[:, 2, 7:8]).then_inc(s_plan, 1)

            def mixture0():
                def split_rows(u):
                    for b in range(KD // 2):
                        dve.wait_ge(s_uc, u * (KD // 2) + b + 1)
                        part = slice(2 * b * TU, 2 * (b + 1) * TU)
                        dve.tensor_tensor(urowsT2[:, 1, part], PS[:, b, 0:2 * TU], urowsT2[:, 0, part].bitcast(F32),
                                          ALU.subtract).then_inc(s_ul, 1)

                def split_first(u, g):
                    dve.wait_ge(s_hi1, u * NG + g + 1)
                    wait(dve, s_ug, u * (NG * FC) + (g - 1) * FC)
                    dve.tensor_copy(b1c[:, g % 2, :], uw1[g % 2][:, G1 - FC:G1])
                    dve.tensor_tensor(w1s[:, g % 2, 1, :], uw1[g % 2][:, 0:G1 - FC], w1s[:, g % 2, 0, :].bitcast(F32),
                                      ALU.subtract).then_inc(s_lo1, 1)

                def split_second(u, g):
                    dve.wait_ge(s_hi2, u * NG + g + 1)
                    dve.tensor_tensor(w2s[:, g % 2, 1, :], uw2[g % 2], w2s[:, g % 2, 0, :].bitcast(F32),
                                      ALU.subtract).then_inc(s_lo2, 1)

                def split_hidden(u, g):
                    dve.wait_ge(s_ug, u * (NG * FC) + (g + 1) * FC)
                    wait(dve, s_ub, u * NG + g - 1)
                    dve.tensor_copy(hid2[:, g % 2, 0, :], hid[:, g % 2, :]).then_inc(s_hh, 1)
                    dve.wait_ge(s_hh, u * NG + g + 1)
                    dve.tensor_tensor(hid2[:, g % 2, 1, :], hid[:, g % 2, :], hid2[:, g % 2, 0, :].bitcast(F32),
                                      ALU.subtract).then_inc(s_hl, 1)

                def unit(u):
                    for g in range(NG):
                        split_hidden(u, g)
                        if g + 2 < NG:
                            split_first(u, g + 2)
                        else:
                            split_first(u + 1, g + 2 - NG)
                        if g + 1 < NG:
                            split_second(u, g + 1)
                    split_second(u + 1, 0)
                    split_rows(u + 1)
                    dve.wait_ge(s_ub, u * NG + NG)
                    wait(dve, s_us, u * 16)
                    for s in range(SU):
                        dve.tensor_copy(in_halves(uout[:, s, :]), PS[:, 4 + 2 * s:6 + 2 * s, 0:384]).then_inc(s_uy, 1)

                dve.wait_ge(s_plan, 2)
                units = dve.value_load(nunits[0:1, 0:1], min_val=1, max_val=NU)
                split_rows(0)
                split_first(0, 0)
                split_second(0, 0)
                split_first(0, 1)
                unit(0)
                with dve.Fori(1, NU) as u:
                    with dve.If(u < units):
                        unit(u)
                dve.wait_ge(s_ua, units * (NG * FC) + FC)
                dve.nop().then_inc(s_left, 1)
                dve.wait_ge(s_yg, 16 * 2 * T)
                for k in range(2):
                    for t in range(T):
                        ins = dve.scalar_tensor_tensor(out=X[:, t, :], in0=picked[:, k, t, :],
                                                       scalar=gate[:, 5 + k, t:t + 1], in1=X[:, t, :],
                                                       op0=ALU.mult, op1=ALU.add)
                    link(ins)

            def mixture1():
                for e in range(6):
                    for t in range(T):
                        add_expert(MB1 + T * e + t, t, MB1 + T * e + t, e)

            def mixture2():
                def two_experts(j):
                    for d in range(2 * T):
                        add_expert(j * (2 * T) + MB3 + d, d % T, MB3 + d, j * 2 + d // T)

                two_experts(0)
                with dve.Fori(1, 4) as j:
                    two_experts(j)

            def bit_layer():
                dve.memset(ws[:], 0.0).then_inc(s_bclr, 1)
                params(4)
                for t in range(T):
                    ins = dve.tensor_tensor_reduce(out=rows(t, O), in0=rows(t, XN), in1=rows(t, XN), scale=1.0,
                                                   scalar=0.0, op0=ALU.mult, op1=ALU.add, accum_out=bs[0:R, 0, t:t + 1])
                link(ins)
                dve.tensor_scalar(var[:], bs[0:R, 0, :], 1.0 / D, 1.0e-6, ALU.mult, ALU.add).then_inc(s_var, 1)
                dve.wait_ge(s_rstd, 7)
                for t in range(T):
                    dve.scalar_tensor_tensor(out=rows(t, O), in0=rows(t, XN), scalar=rstd[:, t:t + 1], in1=par(0, D),
                                             op0=ALU.mult, op1=ALU.mult).then_inc(s_by, 1)
                dve.wait_ge(s_bpe, 1)
                dve.tensor_scalar(ws[:, 2:3], PS[:, 4, 0:1], 1.0 / (P * D), 1.0e-5, ALU.mult, ALU.max)
                link(dve.tensor_scalar(ws[:, 3:4], PS[:, 4, 1:2], 1.0 / (64 * D), 1.0e-5, ALU.mult, ALU.max))
                link(dve.reciprocal(ws[:, 4:6], ws[:, 2:4]))
                for w, k in ((WB[:, 0:768], 4), (WB[0:64, 768:1536], 5)):
                    np_ = w.shape[0]
                    link(dve.tensor_scalar(w, w, ws[0:np_, k:k + 1], -1.0, ALU.mult, ALU.max))
                    link(dve.tensor_scalar(w, w, ROUND, ROUND + 1.0, ALU.add, ALU.min))
                    ins = dve.tensor_scalar(w, w, ROUND, None, ALU.subtract)
                ins.then_inc(s_bwq, 1)

                def quantise(width, src_abs, at, k):
                    for t in range(T):
                        dve.wait_ge(s_bya, (t + 1) if k == 0 else (T + 1))
                        ins = dve.tensor_reduce(bs[0:R, 1 + k, t:t + 1], src_abs(t), AX_X, ALU.max)
                    link(ins)
                    link(dve.tensor_scalar(bs[0:R, 1 + k, :], bs[0:R, 1 + k, :], 1.0e-5, None, ALU.max))
                    link(dve.reciprocal(bs[0:R, 3 + k, :], bs[0:R, 1 + k, :]))
                    link(dve.tensor_scalar(bs[0:R, 3 + k, :], bs[0:R, 3 + k, :], 127.0, None, ALU.mult))
                    link(dve.tensor_scalar(bs[0:R, 5 + k, :], bs[0:R, 1 + k, :], 1.0 / 127.0, ws[0:R, 2 + k:3 + k],
                                           ALU.mult, ALU.mult))
                    for t in range(T):
                        y, q = at(t)
                        link(dve.tensor_scalar(q, y, bs[0:R, 3 + k, t:t + 1], -128.0, ALU.mult, ALU.max))
                        link(dve.tensor_scalar(q, q, ROUND, ROUND + 127.0, ALU.add, ALU.min))
                        ins = dve.tensor_scalar(q, q, ROUND, None, ALU.subtract)
                        if k == 0:
                            ins.then_inc(s_rows, 1)
                    if k == 1:
                        ins.then_inc(s_bq2, 1)

                quantise(D, lambda t: rows(t, F), lambda t: (rows(t, O), rows(t, O)), 0)
                dve.wait_ge(s_bpe, 2)
                for t in range(T):
                    ins = dve.tensor_scalar(O[0:R, t, 128:256], PS[0:R, 5 + t // 3, (t % 3) * P:(t % 3 + 1) * P],
                                            bs[0:R, 5, t:t + 1], None, ALU.mult)
                ins.then_inc(s_bh, 1)
                dve.wait_ge(s_bh, 1)
                dve.wait_ge(s_bsil, 1)
                link(dve.tensor_tensor(O[0:R, 0:T, 0:64], F[0:R, 0:T, 0:64], O[0:R, 0:T, 128:192], ALU.mult))
                for t in range(T):
                    ins = dve.tensor_tensor_reduce(out=O[0:R, t, 64:128], in0=O[0:R, t, 0:64], in1=O[0:R, t, 0:64],
                                                   scale=1.0, scalar=0.0, op0=ALU.mult, op1=ALU.add,
                                                   accum_out=bs[0:R, 7, t:t + 1])
                link(ins)
                dve.tensor_scalar(var[:], bs[0:R, 7, :], 1.0 / 64, 1.0e-6, ALU.mult, ALU.add).then_inc(s_var, 1)
                dve.wait_ge(s_rstd, 8)
                for t in range(T):
                    ins = dve.scalar_tensor_tensor(out=O[0:R, t, 64:128], in0=O[0:R, t, 0:64],
                                                   scalar=rstd[:, t:t + 1], in1=PB[0:R, D:D + 64],
                                                   op0=ALU.mult, op1=ALU.mult)
                ins.then_inc(s_by2, 1)
                dve.wait_ge(s_by2, 1)
                quantise(64, lambda t: F[0:R, t, 512:576], lambda t: (O[0:R, t, 64:128], O[0:R, t, 0:64]), 1)
                for t in range(T):
                    dve.wait_ge(s_bout, t + 1)
                    bank = 4 * (t % 2) + 2
                    dve.scalar_tensor_tensor(out=in_halves(X[:, t, :]), in0=PS[0:R, bank:bank + 2, 0:384],
                                             scalar=bs[0:R, 6, t:t + 1], in1=in_halves(X[:, t, :]),
                                             op0=ALU.mult, op1=ALU.add).then_inc(s_badd, 1)
                dve.wait_ge(s_badd, T)

            def announce(s):
                dve.nop().then_inc(s, 1)

            def section_end():
                announce(s_sec)

            dve.memset(mhalf[:], -0.5).then_inc(s_mh, 1)
            dve.memset(Oz[:, 0:5000], 0.0).then_inc(s_zero, 1)
            dve.memset(ones[:], 1.0)
            dve.wait_ge(s_idx, 16)
            dve.tensor_copy(idf[:, 0, :], idx[:, :, 0])
            link(dve.tensor_copy(idf[:, 1, :], idx[:, :, 1]))
            keyf = W[:, 0, 0:ETP]
            link(dve.scalar_tensor_tensor(out=keyf, in0=idf[:, 1, :], scalar=float(N), in1=idf[:, 0, :],
                                          op0=ALU.mult, op1=ALU.add))
            dve.tensor_copy(key[:], keyf).then_inc(s_keys, 1)
            dve.wait_ge(s_const, 112)
            for a in range(2):
                for k in range(KD):
                    ins = dve.tensor_scalar(blk[:, a, k, :], hmask[:, a, k, :], attc[:, a, k:k + 1], 0.8,
                                            ALU.mult, ALU.mult)
            link(ins)
            dve.wait_ge(s_x, 16)
            layer_norm(0, X, XN, tr=0)
            counts()

            for g in range(2):
                params(g)
                if g == 0:
                    dve.wait_ge(s_zeroed, ZEROED)
                edge_rows(2 * g, g, 0)
                edge_rows(2 * g + 1, g, 1)
                edges(g)
                attend(g)
                elu(g)
                layer_norm(1 + g, O, XN if g == 0 else O, tr=1 if g == 0 else None, w=par(3, D), b=par(4, D))
                if g == 0:
                    dve.wait_ge(s_rows, 2 * T)
                else:
                    add_to_x(None)
                announce(s_pfree)
            section_end()
            if sections > 1:
                layer_norm(3, X, XN, tr=2)
                route(0)
                mix_bias(0)
                make_plan()
                mixture0()
                section_end()
            if sections > 2:
                layer_norm(4, X, XN, tr=3)
                params(2)
                attention_terms(4, 1024, 8)
                attend(2)
                bias_relu(1024, 2)
                dve.wait_ge(s_rows, 5 * T)
                announce(s_pfree)
                params(3)
                attention_terms(5, 768, 1)
                attend(3)
                add_to_x(2)
                announce(s_pfree)
                section_end()
            if sections > 3:
                layer_norm(5, X, XN)
                bit_layer()
                announce(s_pfree)
                section_end()
            if sections > 4:
                for t in range(T):
                    ins = dve.tensor_tensor(C[:, t, t * R:(t + 1) * R], C[:, t, t * R:(t + 1) * R],
                                            ident[0:R, 0:R], ALU.add)
                link(ins)
                dve.tensor_scalar(NEGz, Cz, 0.5, NEGBIG, ALU.is_lt, ALU.mult)
                link(dve.tensor_reduce(bs[0:R, 8, :], C[:], AX_X, ALU.add))
                layer_norm(8, X, XN, tr=6)
                dve.tensor_copy(var[:], bs[0:R, 8, :]).then_inc(s_var, 1)
                dve.wait_ge(s_rstd, 10)
                link(dve.tensor_copy(dinv[:], rstd[:]))
                params(5)
                scaled_rows(6)
                attend(4)
                add_to_x(0)
                announce(s_pfree)
                section_end()
            if sections > 5:
                layer_norm(10, X, XN, tr=7)
                route(1)
                mix_bias(1)
                mixture1()
                dve.wait_ge(s_md, MB3)
                section_end()
            if sections > 6:
                layer_norm(11, X, XN, tr=8)
                params(6)
                attention_terms(7, 768, 4)
                attend(5)
                bias_relu(768, 2)
                dve.wait_ge(s_rows, 10 * T)
                announce(s_pfree)
                params(7)
                attention_terms(8, 768, 4)
                attend(6)
                add_to_x(2)
                announce(s_pfree)
                section_end()
            if sections > 7:
                layer_norm(12, X, XN, tr=10)
                route(2)
                mix_bias(2)
                mixture2()
                dve.wait_ge(s_md, MB3 + 8 * T)
                section_end()
    return nc


def _layout(inputs):
    a = {k: np.ascontiguousarray(v) for k, v in inputs.items()}

    def cols(w):
        k = w.shape[0] // P
        return np.ascontiguousarray(w.reshape(k, P, w.shape[1]).transpose(1, 0, 2).reshape(P, -1))

    out = {"x": a["x"]}
    ends = np.stack([a["src"], a["dst"]], -1)
    ends = np.concatenate([ends, ends[:ETP * P - E]])
    out["edges"] = np.ascontiguousarray(ends.reshape(ETP, P, 2).transpose(1, 0, 2))
    out["iota"] = np.ascontiguousarray(np.broadcast_to(np.arange(626, dtype=np.float32), (P, 626)))
    out["iota8"] = np.ascontiguousarray(np.broadcast_to(np.arange(8, dtype=np.float32), (P, 8)))
    out["iotaU"] = np.ascontiguousarray(np.broadcast_to(np.arange(NU + 1, dtype=np.float32), (P, NU + 1)))
    out["before"] = np.triu(np.ones((R, R), np.float32), 1)
    out["ident"] = np.eye(P, dtype=np.float32)
    out["attc"] = np.ascontiguousarray(np.stack([a["L0_gnn_attn1"].reshape(KD, P).T,
                                                 a["L0_gnn_attno"].reshape(KD, P).T], 1))
    feature = np.arange(D).reshape(KD, P).T
    hm = np.zeros((P, 2, KD, 8), np.float32)
    for h in range(8):
        hm[:, 0, :, h] = feature // 96 == h
    hm[:, 1, :, 0] = 1.0
    out["hmask"] = hm
    for n in ("L0_gnn_W1s", "L0_gnn_W1d", "L0_gnn_Wos", "L0_gnn_Wod", "L2_gnn_W", "L3_gnn_W1", "L3_gnn_W2"):
        out[n] = cols(a[n])
    for n in ("L1_gnn_W1", "L1_gnn_W2", "L1_ffn_w_in"):
        out[n] = cols(a[n].T)
    out["L1_ffn_w_out"] = np.ascontiguousarray(a["L1_ffn_w_out"].T)
    for n in ("L0_ffn_router_w", "L2_ffn_gate_w"):
        out[n] = cols(a[n]).reshape(P, KD, -1)
    out["L3_ffn_router_w"] = cols(a["L3_ffn_router_w"].T).reshape(P, KD, -1)
    for n in ("L0_ffn_b2", "L2_ffn_b2", "L3_ffn_expert_b"):
        out[n] = a[n]
    w1 = a["L0_ffn_w1"].reshape(8, KD, P, NG, FC * P).transpose(0, 3, 2, 1, 4).reshape(8 * NG, P, -1)
    b1 = a["L0_ffn_b1"].reshape(8 * NG, FC, P).transpose(0, 2, 1)
    out["L0_ffn_w1"] = np.ascontiguousarray(np.concatenate([w1, b1], 2))
    out["L0_ffn_w2"] = np.ascontiguousarray(
        a["L0_ffn_w2"].reshape(8, NG, FC, P, D).transpose(0, 1, 3, 2, 4).reshape(8 * NG, P, -1))
    out["L2_ffn_w1"] = np.ascontiguousarray(a["L2_ffn_w1"].reshape(6, KD, P, 96).transpose(2, 0, 1, 3).reshape(P, -1))
    out["L2_ffn_w2"] = np.ascontiguousarray(a["L2_ffn_w2"].transpose(1, 0, 2).reshape(96, -1))
    out["L2_ffn_b1"] = np.ascontiguousarray(a["L2_ffn_b1"].T)
    out["L3_ffn_expert_w"] = np.ascontiguousarray(
        a["L3_ffn_expert_w"].transpose(0, 2, 1).reshape(8, KD, P, D).transpose(0, 2, 1, 3).reshape(8, P, -1))
    for n, v in a.items():
        if n not in out and n not in ("src", "dst", "L0_ffn_b1"):
            out[n] = v.reshape(1, -1)
    return out


def kernel(**inputs):
    import concourse.bacc as bacc
    from concourse.bass_utils import run_bass_kernel_spmd

    nc = bacc.Bacc("TRN2", target_bir_lowering=False, num_devices=1)
    arrays, aps = {}, {}
    for name, v in _layout(inputs).items():
        arrays["in_" + name] = v
        aps[name] = nc.dram_tensor("in_" + name, v.shape, mybir.dt.from_np(v.dtype), kind="ExternalInput").ap()
    out = nc.dram_tensor("out_0", (N, D), F32, kind="ExternalOutput").ap()
    build(nc, aps, out)
    r = run_bass_kernel_spmd(nc, [arrays], core_ids=[0])
    return r.results[0]["out_0"]
```

```python
from contextlib import ExitStack

import numpy as np

import concourse.bass as bass
from concourse import mybir

F32 = mybir.dt.float32
BF16 = mybir.dt.bfloat16
F32R = mybir.dt.float32r
I32 = mybir.dt.int32
U32 = mybir.dt.uint32
ACT = mybir.ActivationFunctionType
ALU = mybir.AluOpType
AX_X = mybir.AxisListType.X

P = 128
N = 625
R = 125
T = N // R
D = 768
KD = D // P
E = 20000
ET = -(-E // P)
EU = 8
ER = ET // EU
GW = D + 8
FF = 3072
FC = 2
NG = FF // (P * FC)
G1 = KD * FC * P + FC
G2 = FC * D
TU = 256
NU = 8 + (2 * N - 8) // TU
LOGITS0 = 16 * 9
SLOTS0 = 16 * (2 * NU + 1)
SU = TU // P
NP = (T - 1) * R + P
G3 = KD // 2 * D
HALF = 313
HALVES = ((0, HALF), (HALF, N))
NEGBIG = -1.0e30
TINY = 1.0e-16
LN_EPS = 1.0e-5
ROUND = 12582912.0


PASSES = ((0, 3), (3, T))
TURN = -(-(ET + 1) // (2 * EU)) * EU
CT = 2 * TURN
MASK_PARTS = PASSES + ((0, T),)


def count_segments(p):
    out = []
    base = PASSES[p][0] * N
    for c in range(*PASSES[p]):
        a, end = c * N, (c + 1) * N
        while a < end:
            b = min(end, base + ((a - base) // 512 + 1) * 512)
            out.append((c, a, b, 2048 + a - base, (a - base) % 512 == 0))
            a = b
    return out


HEADS = [
    dict(h=8, c=96, kind="table"),
    dict(h=1, c=768, kind="table"),
    dict(h=8, c=128, kind="gat"),
    dict(h=1, c=768, kind="gat"),
    dict(h=1, c=768, kind="average"),
    dict(h=4, c=192, kind="gat"),
    dict(h=4, c=192, kind="gat"),
]
LINEARS = [
    (6, 768, 0), (6, 768, 0), (6, 768, 1), (6, 768, 1),
    (6, 1024, 3), (8, 768, 4), (6, 768, 6),
    (6, 768, 8), (6, 768, 9),
]
TR_CHUNKS = [6, 6, 6, 6, 8, 6, 6, 6, 6, 6, 6]


LINEARS_DONE = [2, 4, 5, 6, 7, 8, 9]
MB3 = 6 * T
ROOTS = 13


def unit_place(n):
    if n == 0:
        return lambda s: (s % 8, s // 8)
    return lambda s: (s // T, s % T)


def units_before(n, kinds):
    return sum(T * s["h"] for s in HEADS[:n] if s["kind"] in kinds)


def build(nc, ins, out):
    ctx = ExitStack()
    with ctx:
        def sb(name, shape, dt=F32):
            return ctx.enter_context(nc.sbuf_tensor(name, shape, dt))

        def sem(name):
            return ctx.enter_context(nc.semaphore(name))

        def wait(eng, s, value):
            if isinstance(value, int) and value <= 0:
                return
            eng.wait_ge(s, value)

        src_rows = nc.dram_tensor("src_rows", [N, GW], F32, kind="Internal").ap()
        dst_rows = nc.dram_tensor("dst_rows", [N, GW], F32, kind="Internal").ap()
        logits8 = nc.dram_tensor("logits8", [N * N, 8], F32, kind="Internal").ap()
        logits1 = nc.dram_tensor("logits1", [N * N, 1], F32, kind="Internal").ap()
        tables = [logits8, logits1]
        slot_rows = nc.dram_tensor("slot_rows", [(NU + 1) * TU, D], F32, kind="Internal").ap()
        slot_outs = nc.dram_tensor("slot_outs", [NU * TU, D], F32, kind="Internal").ap()

        with ExitStack() as early:
            w1s = early.enter_context(nc.sbuf_tensor("w1s", [P, 2, 2, G2], F32R))
            w2s = early.enter_context(nc.sbuf_tensor("w2s", [P, 2, 2, G2], F32R))
            hid2 = early.enter_context(nc.sbuf_tensor("hid2", [P, 2, 2, FC * TU], F32R))
            urowsT2 = early.enter_context(nc.sbuf_tensor("urowsT2", [P, 2, KD * TU], F32R))
        with ExitStack() as early:
            XT2 = early.enter_context(nc.sbuf_tensor("XT2", [P, 2, KD, NP], F32R))
            w3s = early.enter_context(nc.sbuf_tensor("w3s", [P, 4, 2, G3], F32R))
        WB = sb("WB", [P, 2 * 6144])
        O = sb("O", [P, T, 1024])
        F = sb("F", [P, T, 1024])
        PB = sb("PB", [P, 3840])
        X = sb("X", [R, T, D])
        XN = sb("XN", [P, T, D])
        XT = sb("XT", [P, 8, N])
        C = sb("C", [P, T, N])
        NEG = sb("NEG", [P, T, N])
        W = sb("W", [P, 4, N])
        PT = sb("PT", [P, 2, T, R])
        idx = sb("idx", [P, ET, 2], I32)
        key = sb("key", [P, ET], I32)
        idf = sb("idf", [P, 2, CT])
        ident = sb("ident", [P, P])
        AT = sb("AT", [8, T, R])
        attc = sb("attc", [P, 2, KD])
        hmask = sb("hmask", [P, 2, KD, 8])
        blk = sb("blk", [P, 2, KD, 8])
        iota8 = sb("iota8", [P, 8])
        stats = sb("stats", [R, T, 2, 6])
        mv = sb("mv", [R, T, 2])
        var = sb("var", [R, T])
        rstd = sb("rstd", [R, T])
        mhalf = sb("mhalf", [R, T])
        a_s = sb("a_s", [R, T, 8])
        a_d = sb("a_d", [R, T, 8])
        mx = sb("mx", [R, 4])
        nmx = sb("nmx", [R, 4])
        den = sb("den", [R, 4])
        rden = sb("rden", [R, 8])
        dinv = sb("dinv", [R, T])
        ixr = sb("ixr", [P, EU, 3], I32)
        lgr = sb("lgr", [P, EU, 8])
        rw = sb("rw", [P, KD, 8])
        rb = sb("rb", [R, 8])
        LG = sb("LG", [R, T, 8])
        top = sb("top", [R, T, 8])
        topi = sb("topi", [R, T, 8], U32)
        topf = sb("topf", [R, T, 8])
        gate = sb("gate", [R, 8, T])
        comb = sb("comb", [R, T, 8])
        comb2 = sb("comb2", [R, T, 8])
        mixb = sb("mixb", [8, D])
        ones = sb("ones", [P, P])
        bs = sb("bs", [P, 16, T])
        ws = sb("ws", [P, 8])
        iotaU = sb("iotaU", [P, NU + 1])
        before = sb("before", [R, R])
        pick = sb("pick", [R, 3, T, 8])
        place_of = sb("place_of", [R, T, 8])
        slotf = sb("slotf", [R, 2, T])
        slots = sb("slots", [R, 2, T], I32)
        plan = sb("plan", [P, 5, 8])
        emptyf = sb("emptyf", [P, NU])
        empty = sb("empty", [P, NU], I32)
        uexpf = sb("uexpf", [P, NU + 1])
        uexp = sb("uexp", [P, NU + 1], I32)
        nunits = sb("nunits", [P, 1], I32)
        b1c = sb("b1c", [P, 2, FC])

        Fz = F[:, :, :].rearrange("p t c -> p (t c)")
        Oz = O[:, :, :].rearrange("p t c -> p (t c)")
        XTz = XT[:, :, :].rearrange("p k n -> p (k n)")
        iota = XTz[:, 6 * N:7 * N]
        oh = Oz[:, 0:2 * (N + 1)].bitcast(BF16).rearrange("p (u s n) -> p u s n", u=2, s=2)
        gs = [WB[:, u * GW:(u + 1) * GW] for u in range(EU)]
        gd = [WB[:, (EU + u) * GW:(EU + u + 1) * GW] for u in range(EU - 1)] + [XTz[:, 0:GW]]
        zr = XTz[:, GW:GW + 2 * D].rearrange("p (u k c) -> p u k c", u=2, k=KD)
        ltile = WB[0:R, 0:10000].rearrange("p (u n h) -> p u n h", u=2, h=8)
        ltile1 = WB[0:R, 0:T * N].rearrange("p (t n) -> p t n", t=T)
        wlin = [WB[:, 6144 * u:6144 * (u + 1)] for u in range(2)]
        TMP = W[:, :, :].rearrange("p a b -> p (a b)")[0:R, 0:1024]
        TMP2 = W[:, :, :].rearrange("p a b -> p (a b)")[0:R, 1024:2048]

        uw3 = [C[:, :, :].rearrange("p t n -> p (t n)")[:, 0:G3], NEG[:, :, :].rearrange("p t n -> p (t n)")[:, 0:G3]]

        hidT = WB[0:64, 3072:3072 + N].rearrange("p (t n) -> p t n", t=T)

        uout = Fz[:, 0:SU * D].rearrange("p (s d) -> p s d", s=SU)
        urows = Fz[:, SU * D:2 * SU * D].rearrange("p (s d) -> p s d", s=SU)
        hid = Fz[:, 2 * SU * D:2 * SU * D + 2 * FC * TU].rearrange("p (u n) -> p u n", u=2)
        uw1 = [XN[:, :, :].rearrange("p t d -> p (t d)")[:, G1 * u:G1 * (u + 1)] for u in range(2)]
        uw2 = [PB[:, G2 * u:G2 * (u + 1)] for u in range(2)]
        picked = WB[0:R, 0:2 * T * D].rearrange("p (k t d) -> p k t d", k=2, t=T)

        def mask(n, of=None):
            a, b = MASK_PARTS[n]
            return (of or NEG)[0:R, a:b, :].rearrange("p t n -> p (t n)")

        def par(slot, width, w=None):
            return PB[0:R, slot * width:slot * width + (w or width)]

        PS = ctx.enter_context(nc.psum_tensor("PS", [P, 8, 512], F32))
        PSz = PS[:, :, :].rearrange("p b n -> p (b n)")

        s_const = sem("consts_loaded")
        s_x = sem("x_loaded")
        s_idx = sem("edges_loaded")
        s_keys = sem("edge_keys_ready")
        s_zero = sem("zeros_ready")
        s_zeroed = sem("logit_tables_zeroed")
        s_zslots = sem("slot_tables_zeroed")
        s_oh = sem("onehots_ready")
        s_ohu = sem("onehots_used")
        s_cnt = sem("counts_ready")
        s_link = sem("vector_link")
        s_mh = sem("minus_half_ready")
        s_var = sem("variances_ready")
        s_rstd = sem("rstds_ready")
        s_rows = sem("rows_ready")
        s_trp = sem("transposed_in_psum")
        s_trc = sem("transposed_copied")
        s_par = sem("params_loaded")
        s_pfree = sem("params_used")
        s_wl = [sem(f"linear_weights{u}") for u in range(2)]
        s_linp = sem("linear_in_psum")
        s_line = sem("linear_evacuated")
        s_frow = sem("table_rows_ready")
        s_tab = sem("tables_written")
        s_ends = sem("node_numbers_copied")
        s_kc = sem("pair_numbers_copied")
        s_gat = [sem(f"rows_gathered{u}") for u in range(EU)]
        s_z = sem("edge_sums_ready")
        s_zt = sem("edge_sums_transposed")
        s_zr = sem("edge_relus_ready")
        s_dot = sem("edge_dots_ready")
        s_lg = sem("edge_logits_ready")
        s_sc = sem("edge_logits_scattered")
        s_lt = [sem(f"logit_tile_loaded{u}") for u in range(2)]
        s_att = sem("attention_terms_ready")
        s_astp = sem("terms_transposed")
        s_ast = sem("terms_copied")
        s_bc = sem("source_terms_broadcast")
        s_many = sem("counts_above_zero_ready")
        s_ln = sem("logarithms_ready")
        s_v = sem("edge_terms_ready")
        s_lm = sem("masked_logits_ready")
        s_e = sem("exps_ready")
        s_p = sem("weights_ready")
        s_tp = sem("weights_transposed")
        s_pt = sem("weights_copied")
        s_op = sem("sums_in_psum")
        s_out = sem("sums_evacuated")
        s_neg = sem("negative_parts_ready")
        s_elu = sem("elu_exps_ready")
        s_rw = sem("router_loaded")
        s_rtp = sem("router_in_psum")
        s_gap = sem("router_gaps_ready")
        s_gex = sem("router_exps_ready")
        s_comb = sem("mixture_weights_ready")
        s_mbt = sem("mixture_weights_transposed")
        s_mbc = sem("mixture_weights_copied")
        s_mixp = sem("bias_mix_in_psum")
        s_mixd = sem("bias_mix_added")
        s_pick = sem("choices_ready")
        s_rank = sem("ranks_in_psum")
        s_slots = sem("slots_ready")
        s_plan = sem("unit_experts_ready")
        s_scr = sem("token_rows_scattered")
        s_w1 = [sem(f"first_weights{u}") for u in range(2)]
        s_w2 = [sem(f"second_weights{u}") for u in range(2)]
        s_ux = sem("unit_rows_loaded")
        s_ut = sem("unit_rows_transposed")
        s_uc = sem("unit_rows_copied")
        s_ua = sem("unit_hidden_in_psum")
        s_ug = sem("unit_hidden_ready")
        s_ub = sem("unit_group_summed")
        s_uy = sem("unit_output_evacuated")
        s_us = sem("unit_output_stored")
        s_left = sem("units_left")
        s_hi1 = sem("first_weights_rounded")
        s_lo1 = sem("first_weights_split")
        s_hi2 = sem("second_weights_rounded")
        s_lo2 = sem("second_weights_split")
        s_hh = sem("unit_hidden_rounded")
        s_hl = sem("unit_hidden_split")
        s_ul = sem("unit_rows_split")
        s_yg = [sem(f"choice{k}_outputs_gathered") for k in range(2)]
        s_ma = sem("hidden_in_psum")
        s_mg = sem("hidden_ready")
        s_mb = sem("expert_in_psum")
        s_md = sem("expert_added")
        s_m2w = sem("small_experts_loaded")
        s_m3w = [sem(f"square_expert_weights{u}") for u in range(2)]
        s_h3 = sem("square_weights_rounded")
        s_l3 = sem("square_weights_split")
        s_xh = sem("features_rounded")
        s_xl = sem("features_split")
        s_bw = sem("bit_weights_loaded")
        s_bclr = sem("bit_sums_cleared")
        s_babs = sem("bit_weight_sums_ready")
        s_bpe = sem("bit_products_ready")
        s_bwq = sem("bit_weights_rounded")
        s_by = sem("bit_rows_normalised")
        s_bya = sem("bit_rows_absolute")
        s_bh = sem("bit_hidden_ready")
        s_bsil = sem("bit_silu_ready")
        s_by2 = sem("bit_hidden_normalised")
        s_bq2 = sem("bit_hidden_rounded")
        s_bqt = sem("bit_hidden_transposed")
        s_bout = sem("bit_output_in_psum")
        s_badd = sem("bit_output_added")
        s_sec = sem("section_done")
        s_store = sem("output_stored")

        block = ctx.enter_context(nc.Block())

        PARAMS = [
            (768, ["L0_gnn_b1s", "L0_gnn_b1d", "L0_gnn_attn1", "L0_gnn_ln1_w", "L0_gnn_ln1_b"]),
            (768, ["L0_gnn_bos", "L0_gnn_bod", "L0_gnn_attno", "L0_gnn_lno_w", "L0_gnn_lno_b"]),
            (1024, ["L1_gnn_att_src1", "L1_gnn_att_dst1", "L1_gnn_b1"]),
            (768, ["L1_gnn_att_src2", "L1_gnn_att_dst2", "L1_gnn_b2"]),
            (768, ["L1_ffn_g_in", "L1_ffn_g_out"]),
            (768, ["L2_gnn_b"]),
            (768, ["L3_gnn_a_src1", "L3_gnn_a_dst1", "L3_gnn_b1"]),
            (768, ["L3_gnn_a_src2", "L3_gnn_a_dst2", "L3_gnn_b2"]),
        ]
        par_total = np.cumsum([0] + [len(p) for _, p in PARAMS]).tolist()
        LIN_W = ["L0_gnn_W1s", "L0_gnn_W1d", "L0_gnn_Wos", "L0_gnn_Wod", "L1_gnn_W1", "L1_gnn_W2",
                 "L2_gnn_W", "L3_gnn_W1", "L3_gnn_W2"]
        ROUTERS = [("L0_ffn_router_w", "L0_ffn_router_b"), ("L2_ffn_gate_w", "L2_ffn_gate_b"),
                   ("L3_ffn_router_w", "L3_ffn_router_b")]
        MIXB = ["L0_ffn_b2", "L2_ffn_b2", "L3_ffn_expert_b"]
        N_EXP = [8, 6, 8]

        @block.sync
        def _(sp):
            def params(g):
                wait(sp, s_pfree, g)
                width, names = PARAMS[g]
                for k, name in enumerate(names):
                    n = ins[name].shape[1]
                    sp.dma_start(PB[0:R, k * width:k * width + n], ins[name].to_broadcast([R, n]))\
                      .then_inc(s_par, 16)

            def linear_weights(n):
                k, width, _ = LINEARS[n]
                sp.dma_start(wlin[n % 2][:, 0:k * width], ins[LIN_W[n]]).then_inc(s_wl[n % 2], 16)

            def router(n):
                if n:
                    sp.wait_ge(s_mixp, T * n)
                    sp.wait_ge(s_comb, n)
                sp.dma_start(rw[:, :, 0:N_EXP[n]], ins[ROUTERS[n][0]]).then_inc(s_rw, 16)
                sp.dma_start(rb[:, 0:N_EXP[n]], ins[ROUTERS[n][1]].to_broadcast([R, N_EXP[n]])).then_inc(s_rw, 16)
                sp.dma_start(mixb[0:N_EXP[n], :], ins[MIXB[n]]).then_inc(s_rw, 16)

            sp.dma_start(iota, ins["iota"]).then_inc(s_const, 16)
            sp.dma_start(idx[:], ins["edges"]).then_inc(s_idx, 16)
            sp.dma_start(X[:], ins["x"].rearrange("(t p) d -> p t d", p=R)).then_inc(s_x, 16)
            for t, name in ((ident[:], "ident"), (iota8[:], "iota8"), (attc[:], "attc"), (hmask[:], "hmask"),
                            (iotaU[:], "iotaU"), (before[:], "before")):
                sp.dma_start(t, ins[name]).then_inc(s_const, 16)
            for g in range(2):
                params(g)
                for side in range(2):
                    n = 2 * g + side
                    if g:
                        sp.wait_ge(s_out, units_before(g, ("table",)))
                    linear_weights(n)
                if g == 0:
                    sp.wait_ge(s_zero, 1)
                    zeros = NEG[:, :, :].rearrange("p t n -> p (t n)")
                    flat8 = logits8.rearrange("n h -> (n h)").rearrange("(a p c) -> a p c", a=8, p=R)
                    for a in range(8):
                        sp.dma_start(flat8[a], zeros[0:R]).then_inc(s_zeroed, 16)
                    sp.dma_start(logits1.rearrange("(p b) h -> p (b h)", p=R), zeros[0:R]).then_inc(s_zeroed, 16)
                for side, table in enumerate((src_rows, dst_rows)):
                    for t in range(T):
                        sp.wait_ge(s_frow, T * (2 * g + side) + t + 1)
                        rows = (F if side == 0 else O)[0:R, t, 0:GW]
                        sp.dma_start(table[t * R:(t + 1) * R, :], rows).then_inc(s_tab, 16)
                if g == 0:
                    zeroed = 0
                    for table, units in ((slot_rows, NU + 1), (slot_outs, NU)):
                        flat = table.rearrange("(a p b) d -> a p (b d)", a=units, p=P)
                        for a in range(units):
                            zeroed += 1
                            sp.wait_ge(s_sc, 16 * 3 * zeroed)
                            sp.dma_start(flat[a], zeros[:, 0:SU * D]).then_inc(s_zslots, 16)
                sp.wait_ge(s_sc, 16 * ET * (g + 1))
                if g == 0:
                    for t in range(T):
                        if t >= 2:
                            sp.wait_ge(s_lm, 8 * (t - 1))
                        sp.dma_start(ltile[:, t % 2], logits8.rearrange("(t p n) h -> t p n h", t=T, p=R)[t])\
                          .then_inc(s_lt[t % 2], 16)
                else:
                    sp.dma_start(ltile1, logits1.rearrange("(t p n) h -> p t (n h)", t=T, p=R)).then_inc(s_lt[1], 16)
            sp.wait_ge(s_sec, 1)
            router(0)
            def first_weights(u, g, expert):
                sp.wait_ge(s_lo1, u * NG + g - 1)
                first_load(g, expert)

            def first_load(g, expert):
                sp.dma_start(uw1[g % 2], ins["L0_ffn_w1"][bass.ds(expert * NG + g, 1)]
                             .rearrange("o p n -> p (o n)")).then_inc(s_w1[g % 2], 16)

            def second_weights(u, g, expert):
                wait(sp, s_lo2, u * NG + g - 1)
                sp.dma_start(uw2[g % 2], ins["L0_ffn_w2"][bass.ds(expert * NG + g, 1)]
                             .rearrange("o p n -> p (o n)")).then_inc(s_w2[g % 2], 16)

            def unit_loads(u):
                sp.wait_ge(s_ut, u * (KD // 2) + KD // 2)
                sp.dma_start(urows, slot_rows.rearrange("(u s p) d -> u p s d", s=SU, p=P)[bass.ds(u + 1, 1)]
                             .rearrange("o p s d -> p (o s) d")).then_inc(s_ux, 16)
                this = sp.value_load(uexp[0:1, bass.ds(u, 1)], min_val=0, max_val=7)
                then = sp.value_load(uexp[0:1, bass.ds(u + 1, 1)], min_val=0, max_val=7)
                for g in range(NG):
                    if g + 2 < NG:
                        first_weights(u, g + 2, this)
                    else:
                        first_weights(u + 1, g + 2 - NG, then)
                    if g + 1 < NG:
                        second_weights(u, g + 1, this)
                    else:
                        second_weights(u + 1, 0, then)

            sp.wait_ge(s_plan, 2)
            units = sp.value_load(nunits[0:1, 0:1], min_val=1, max_val=NU)
            expert = sp.value_load(uexp[0:1, 0:1], min_val=0, max_val=7)
            sp.wait_ge(s_scr, 16 * 2 * T)
            sp.dma_start(urows, slot_rows[0:TU].rearrange("(s p) d -> p s d", s=SU)).then_inc(s_ux, 16)
            first_load(0, expert)
            second_weights(0, 0, expert)
            first_load(1, expert)
            unit_loads(0)
            with sp.Fori(1, NU) as u:
                with sp.If(u < units):
                    unit_loads(u)
            sp.wait_ge(s_sec, 2)
            params(2)
            linear_weights(4)
            linear_weights(5)
            params(3)
            sp.wait_ge(s_sec, 3)
            params(4)
            sp.dma_start(WB[:, 0:768], ins["L1_ffn_w_in"]).then_inc(s_bw, 16)
            sp.dma_start(WB[0:64, 768:1536], ins["L1_ffn_w_out"]).then_inc(s_bw, 16)
            sp.wait_ge(s_sec, 4)
            params(5)
            linear_weights(6)
            sp.wait_ge(s_sec, 5)
            router(1)
            sp.dma_start(WB[:, 0:3456], ins["L2_ffn_w1"]).then_inc(s_m2w, 16)
            sp.dma_start(WB[0:96, 3456:3456 + 4608], ins["L2_ffn_w2"]).then_inc(s_m2w, 16)
            sp.dma_start(WB[0:96, 8064:8070], ins["L2_ffn_b1"]).then_inc(s_m2w, 16)
            sp.wait_ge(s_sec, 6)
            params(6)
            linear_weights(7)
            linear_weights(8)
            params(7)
            sp.wait_ge(s_sec, 7)
            router(2)
            def halves_of(e, expert):
                for u in range(2):
                    wait(sp, s_l3, e * 2 + u - 1)
                    sp.dma_start(uw3[u], expert[:, u * G3:(u + 1) * G3]).then_inc(s_m3w[u], 16)

            halves_of(0, ins["L3_ffn_expert_w"][0])
            with sp.Fori(1, 8) as e:
                halves_of(e, ins["L3_ffn_expert_w"][bass.ds(e, 1)].rearrange("o p n -> p (o n)"))
            sp.wait_ge(s_sec, 8)
            sp.dma_start(out.rearrange("(t p) d -> p t d", p=R), X[:]).then_inc(s_store, 16)
            sp.wait_ge(s_store, 16)

        @block.gpsimd
        def _(pool):
            def rsqrt(n):
                pool.wait_ge(s_var, n + 1)
                pool.tensor_tensor(rstd[:], var[:], mhalf[:], ALU.pow).then_inc(s_rstd, 1)

            LAG = 6

            def node_numbers(i, u):
                pool.tensor_copy(ixr[:, u % EU, 0:2], idx[:, bass.ds(i, 1), :].rearrange("p o k -> p (o k)"))\
                    .then_inc(s_ends, 1)

            def edge_step(i, u, g, gather=True, scatter=True, more=True):
                base = ET * g
                if gather:
                    wait(pool, s_kc, base + i)
                    pool.wait_ge(s_ends, base + i + 1)
                    pool.tensor_copy(ixr[:, u, 2:3], key[:, bass.ds(i, 1)]).then_inc(s_kc, 1)
                    pool.indirect_dma_start(
                        out=gs[u], out_offset=None, in_=src_rows,
                        in_offset=bass.IndirectOffsetOnAxis(ap=ixr[:, u, 0:1], axis=0)).then_inc(s_gat[u], 16)
                    pool.indirect_dma_start(
                        out=gd[u], out_offset=None, in_=dst_rows,
                        in_offset=bass.IndirectOffsetOnAxis(ap=ixr[:, u, 1:2], axis=0)).then_inc(s_gat[u], 16)
                else:
                    pool.wait_ge(s_kc, ET * (g + 1))
                wait(pool, s_lg, base + i - LAG + 1)
                wait(pool, s_sc, 16 * (base + i - LAG))
                if gather and more:
                    node_numbers(i + 1, u + 1)
                if scatter:
                    v = (u - LAG) % EU
                    pool.indirect_dma_start(
                        out=tables[g], out_offset=bass.IndirectOffsetOnAxis(ap=ixr[:, v, 2:3], axis=0),
                        in_=lgr[:, v, 0:HEADS[g]["h"]], in_offset=None).then_inc(s_sc, 16)

            def edges(g):
                pool.wait_ge(s_tab, 16 * 2 * T * (g + 1))
                if g == 0:
                    pool.wait_ge(s_keys, 1)
                    pool.wait_ge(s_zeroed, LOGITS0)
                node_numbers(0, 0)
                for i in range(EU):
                    edge_step(i, i, g, scatter=i >= LAG)
                with pool.Fori(1, ER) as j:
                    for u in range(EU):
                        edge_step(j * EU + u, u, g)
                for i in range(ER * EU, ET):
                    edge_step(i, i % EU, g, more=i + 1 < ET)
                for i in range(ET, ET + LAG):
                    edge_step(i, i % EU, g, gather=False)

            pool.wait_ge(s_mh, 1)
            rsqrt(0)
            edges(0)
            rsqrt(1)
            edges(1)
            rsqrt(2)
            rsqrt(3)
            pool.wait_ge(s_zslots, SLOTS0)
            pool.wait_ge(s_slots, 1)
            for k in range(2):
                for t in range(T):
                    pool.indirect_dma_start(
                        out=slot_rows, out_offset=bass.IndirectOffsetOnAxis(ap=slots[:, k, t:t + 1], axis=0),
                        in_=XN[0:R, t, :], in_offset=None).then_inc(s_scr, 16)
            pool.wait_ge(s_plan, 2)
            units = pool.value_load(nunits[0:1, 0:1], min_val=1, max_val=NU)

            def unit_store(u):
                pool.wait_ge(s_uy, u * SU + SU)
                pool.dma_start(slot_outs.rearrange("(u s p) d -> u p s d", s=SU, p=P)[bass.ds(u, 1)]
                               .rearrange("o p s d -> p (o s) d"), uout).then_inc(s_us, 16)
                pool.wait_ge(s_us, u * 16 + 16)

            unit_store(0)
            with pool.Fori(1, NU) as u:
                with pool.If(u < units):
                    unit_store(u)
            pool.wait_ge(s_left, 1)
            for k in range(2):
                for t in range(T):
                    pool.indirect_dma_start(
                        out=picked[:, k, t, :], out_offset=None, in_=slot_outs,
                        in_offset=bass.IndirectOffsetOnAxis(ap=slots[:, k, t:t + 1], axis=0)).then_inc(s_yg[k], 16)
            for n in range(4, ROOTS):
                rsqrt(n)

        @block.tensor
        def _(pe):
            def count(n, slot, p, first=False, last=False):
                pe.wait_ge(s_oh, n + 1)
                for c, a, b, at, fresh in count_segments(p):
                    mm = pe.matmul(PSz[0:R, at:at + b - a], oh[:, slot, 1, c * R:(c + 1) * R],
                                   oh[:, slot, 0, a - c * N:b - c * N],
                                   start=(first and fresh), stop=last, skip_group_check=True)
                mm.then_inc(s_ohu, 1)

            def transpose_rows(n, src):
                per = TR_CHUNKS[n] // 2
                for t in range(T):
                    pe.wait_ge(s_rows, T * n + t + 1)
                    for half in range(2):
                        g = 2 * T * n + 2 * t + half
                        wait(pe, s_trc, g - 3)
                        for k in range(per):
                            kk = half * per + k
                            tr = pe.transpose(PS[:, g % 4, k * R:(k + 1) * R],
                                              src[0:R, t, kk * P:(kk + 1) * P], ident[0:R, 0:R])
                        tr.then_inc(s_trp, 1)

            def linear(n):
                kc, width, m = LINEARS[n]
                w = wlin[n % 2][:, 0:kc * width].rearrange("p (k c) -> p k c", k=kc)
                hw = width // 2
                pe.wait_ge(s_wl[n % 2], 16 * (n // 2 + 1))
                for t in range(T):
                    pe.wait_ge(s_trc, 2 * T * m + 2 * t + 2)
                    for half in range(2):
                        g = 2 * T * n + 2 * t + half
                        wait(pe, s_line, g - 3)
                        for k in range(kc):
                            mm = pe.matmul(PS[0:R, 4 + g % 4, 0:hw], XT[:, k, t * R:(t + 1) * R],
                                           w[:, k, half * hw:(half + 1) * hw], start=(k == 0), stop=(k == kc - 1))
                        mm.then_inc(s_linp, 1)

            def edge_turn(i, u, g):
                base = ET * g
                pe.wait_ge(s_z, base + i + 1)
                wait(pe, s_zr, base + i)
                for k in range(KD):
                    tr = pe.transpose(PSz[:, k * P:(k + 1) * P],
                                      gs[u][:, k * P:(k + 1) * P], ident[:])
                tr.then_inc(s_zt, 1)

            def edge_dot(i, u, g):
                base = ET * g
                pe.wait_ge(s_zr, base + i + 1)
                wait(pe, s_lg, base + i - 1)
                for k in range(KD):
                    mm = pe.matmul(PS[:, 2 + u % 2, 0:8], zr[:, u % 2, k, :], blk[:, g, k, :],
                                   start=(k == 0), stop=(k == KD - 1))
                mm.then_inc(s_dot, 1)

            def edges(g):
                def step(i, u, p):
                    edge_turn(i, u, g)
                    if not isinstance(i, int) or i:
                        edge_dot(i - 1, (u - 1) % EU, g)
                    if g == 0:
                        for v in range(2):
                            if isinstance(i, int) and i == TURN and v == 0:
                                pe.wait_ge(s_cnt, 1)
                            count(i * 2 + v, v, p, first=isinstance(i, int) and i in (0, TURN) and v == 0,
                                  last=isinstance(i, int) and i == TURN - 1 and v == 1)

                turn = TURN // EU
                for i in range(EU):
                    step(i, i, 0)
                with pe.Fori(1, turn - 1) as j:
                    for u in range(EU):
                        step(j * EU + u, u, 0)
                for i in range(TURN - EU, TURN):
                    step(i, i % EU, 0)
                for i in range(TURN, TURN + EU):
                    step(i, i % EU, 1)
                with pe.Fori(turn + 1, ER) as j:
                    for u in range(EU):
                        step(j * EU + u, u, 1)
                for i in range(ER * EU, ET):
                    step(i, i % EU, 1)
                edge_dot(ET - 1, (ET - 1) % EU, g)
                if g == 0:
                    for n in range(2 * ET, CT + ET):
                        count(n, n % 2, 1, last=n == CT + ET - 1)
                    pe.wait_ge(s_cnt, 2)

            def attend(n):
                h, c, kind = HEADS[n]["h"], HEADS[n]["c"], HEADS[n]["kind"]
                soft = units_before(n, ("table", "gat"))
                gat = units_before(n, ("gat",))
                every = units_before(n, ("table", "gat", "average"))
                gats = sum(s["kind"] == "gat" for s in HEADS[:n])
                heads = sum(s["h"] for s in HEADS[:n] if s["kind"] == "gat")
                units = T * h
                place = unit_place(n)

                def broadcast(head):
                    wait(pe, s_v, gat + T * head)
                    for a, b in ((0, 512), (512, N)):
                        mm = pe.matmul(PSz[0:R, a:b], ident[0:h, head:head + 1].to_broadcast([h, R]),
                                       AT[0:h].rearrange("h t n -> h (t n)")[:, a:b], start=True, stop=True)
                    mm.then_inc(s_bc, 1)

                def turn(s):
                    t = place(s)[1]
                    if kind == "average":
                        src = C[0:R, t, :]
                    else:
                        pe.wait_ge(s_e, soft + s + 1)
                        src = W[0:R, s % 4, :]
                    wait(pe, s_pt, every + s - 1)
                    for b in range(T):
                        tr = pe.transpose(PSz[0:R, 1024 * (1 + s % 2) + b * P:1024 * (1 + s % 2) + b * P + R],
                                          src[:, b * R:(b + 1) * R], ident[0:R, 0:R])
                    tr.then_inc(s_tp, 1)

                def sum_up(s):
                    head, t = place(s)
                    pe.wait_ge(s_pt, every + s + 1)
                    wide = c > 512
                    wait(pe, s_out, every + s if wide else every + s - 1)
                    for half in range(2 if wide else 1):
                        cw = c // 2 if wide else c
                        col = head * c + half * cw
                        bank = 6 + (half if wide else s % 2)
                        for b in range(T):
                            mm = pe.matmul(PS[0:R, bank, 0:cw], PT[0:R, s % 2, b, :],
                                           F[0:R, b, col:col + cw], start=(b == 0), stop=(b == T - 1))
                    mm.then_inc(s_op, 1)

                pe.wait_ge(s_line, 2 * T * LINEARS_DONE[n])
                if kind == "gat":
                    pe.wait_ge(s_att, gats + 1)
                    for t in range(T):
                        tr = pe.transpose(PSz[0:h, t * P:t * P + R], a_s[:, t, 0:h], ident[0:R, 0:R])
                    tr.then_inc(s_astp, 1)
                    pe.wait_ge(s_ast, gats + 1)
                    broadcast(0)
                for s in range(units):
                    if kind == "gat" and place(s)[1] == T - 1 and place(s)[0] + 1 < h:
                        broadcast(place(s)[0] + 1)
                    turn(s)
                    if s:
                        sum_up(s - 1)
                sum_up(units - 1)

            def route(n, m):
                e = N_EXP[n]
                pe.wait_ge(s_rw, 48 * (n + 1))
                for t in range(T):
                    pe.wait_ge(s_trc, 2 * T * m + 2 * t + 2)
                    for k in range(KD):
                        mm = pe.matmul(PS[0:R, 4, t * 8:t * 8 + e], XT[:, k, t * R:(t + 1) * R], rw[:, k, 0:e],
                                       start=(k == 0), stop=(k == KD - 1))
                mm.then_inc(s_rtp, 1)

            def mix_bias(n):
                e = N_EXP[n]
                pe.wait_ge(s_comb, n + 1)
                for t in range(T):
                    tr = pe.transpose(PSz[0:8, t * P:t * P + R], comb[:, t, :], ident[0:R, 0:R])
                tr.then_inc(s_mbt, 1)
                pe.wait_ge(s_mbc, n + 1)
                for t in range(T):
                    g = T * n + t
                    wait(pe, s_mixd, g - 1)
                    for half in range(2):
                        mm = pe.matmul(PS[0:R, 4 + 2 * (g % 2) + half, 0:384], AT[0:e, t, :],
                                       mixb[0:e, half * 384:(half + 1) * 384], start=True, stop=True)
                    mm.then_inc(s_mixp, 1)

            def expert_out(done, t, u, lhs, rhs, last_u=None):
                wait(pe, s_md, done - 1)
                k_all = len(lhs)
                for half in range(2):
                    for k in range(k_all):
                        mm = pe.matmul(PS[0:R, 4 + 2 * (u % 2) + half, 0:384], lhs[k](t),
                                       rhs[k][:, half * 384:(half + 1) * 384], start=(k == 0), stop=(k == k_all - 1))
                mm.then_inc(s_mb, 1)

            def ranks():
                pe.wait_ge(s_pick, 1)
                for t in range(T):
                    for b in range(t + 1):
                        pe.matmul(PS[0:R, 5, t * 8:(t + 1) * 8], before[:] if b == t else ones[0:R, 0:R],
                                  pick[:, 2, b, :], start=(b == 0), stop=(b == t))
                for t in range(T):
                    mm = pe.matmul(PS[:, 6, 0:8], ones[0:R, :], pick[:, 2, t, :], start=(t == 0), stop=(t == T - 1))
                mm.then_inc(s_rank, 1)

            def mixture0():
                def turn(u):
                    pe.wait_ge(s_ux, u * 16 + 16)
                    wait(pe, s_ug, u * (NG * FC))
                    for b in range(KD // 2):
                        for k in range(2):
                            for s in range(SU):
                                tr = pe.transpose(PS[:, b, k * TU + s * P:k * TU + (s + 1) * P],
                                                  urows[:, s, (2 * b + k) * P:(2 * b + k + 1) * P], ident[:])
                        tr.then_inc(s_ut, 1)

                def three(out, w, x, first, last):
                    for n, (i, j) in enumerate(((0, 0), (0, 1), (1, 0))):
                        mm = pe.matmul(out, w(i), x(j), start=first and n == 0, stop=last and n == 2)
                    return mm

                def first(u, g, columns=TU):
                    pe.wait_ge(s_lo1, u * NG + g + 1)
                    if g == 0:
                        pe.wait_ge(s_ul, u * (KD // 2) + KD // 2)
                    for c in range(FC):
                        q = g * FC + c
                        wait(pe, s_ug, u * (NG * FC) + q - 3)
                        for k in range(KD):
                            mm = three(PS[:, q % 4, 0:columns],
                                       lambda i: w1s[:, g % 2, i, (k * FC + c) * P:(k * FC + c + 1) * P],
                                       lambda j: urowsT2[:, j, k * TU:k * TU + columns], k == 0, k == KD - 1)
                        mm.then_inc(s_ua, 1)

                def second(u, g, tiles):
                    pe.wait_ge(s_lo2, u * NG + g + 1)
                    if g == 0:
                        wait(pe, s_uy, u * SU)
                    pe.wait_ge(s_hl, u * NG + g + 1)
                    for s in range(tiles):
                        for half in range(2):
                            for c in range(FC):
                                mm = three(PS[:, 4 + 2 * s + half, 0:384],
                                           lambda i: hid2[:, g % 2, i, c * TU + s * P:c * TU + (s + 1) * P],
                                           lambda j: w2s[:, g % 2, j, c * D + half * 384:c * D + (half + 1) * 384],
                                           g == 0 and c == 0, g == NG - 1 and c == FC - 1)
                    mm.then_inc(s_ub, 1)

                def groups(u, columns):
                    for g in range(NG - 1):
                        first(u, g + 1, columns)
                        second(u, g, -(-columns // P))
                    turn(u + 1)

                def unit(u):
                    quarters = pe.value_load(empty[0:1, bass.ds(u, 1)], min_val=0, max_val=3)
                    with pe.If(quarters > 1):
                        groups(u, TU // 2)
                        second(u, NG - 1, SU // 2)
                    with pe.Else():
                        with pe.If(quarters > 0):
                            groups(u, 3 * TU // 4)
                        with pe.Else():
                            groups(u, TU)
                        second(u, NG - 1, SU)
                    first(u + 1, 0)

                pe.wait_ge(s_plan, 3)
                units = pe.value_load(nunits[0:1, 0:1], min_val=1, max_val=NU)
                turn(0)
                first(0, 0)
                unit(0)
                with pe.Fori(1, NU) as u:
                    with pe.If(u < units):
                        unit(u)

            def mixture1():
                w1 = WB[:, 0:3456].rearrange("p (e k f) -> p e k f", e=6, k=KD)
                w2 = WB[0:96, 3456:3456 + 4608].rearrange("p (e d) -> p e d", e=6)
                hT = Oz[0:96, 0:2 * N].rearrange("p (u n) -> p u n", u=2)
                pe.wait_ge(s_m2w, 48)
                for e in range(6):
                    for hf, (a, b) in enumerate(HALVES):
                        q = 2 * e + hf
                        wait(pe, s_mg, q - 3)
                        for k in range(KD):
                            mm = pe.matmul(PS[0:96, q % 4, 0:b - a], w1[:, e, k, :], XT[:, k, a:b],
                                           start=(k == 0), stop=(k == KD - 1))
                        mm.then_inc(s_ma, 1)
                    pe.wait_ge(s_mg, 2 * e + 2)
                    for t in range(T):
                        d = T * e + t
                        expert_out(d, t, d, [lambda t: hT[:, e % 2, t * R:(t + 1) * R]], [w2[:, e, :]])

            def mixture2():
                def two_experts(j):
                    for u in range(2):
                        pe.wait_ge(s_l3, j * 4 + 2 * u + 2)
                        for t in range(T):
                            d = u * T + t
                            wait(pe, s_md, MB3 + d + j * (2 * T) - 1)
                            for half in range(2):
                                for k in range(KD):
                                    for n, (a, b) in enumerate(((0, 0), (0, 1), (1, 0))):
                                        col = k % 3 * D + half * 384
                                        mm = pe.matmul(PS[:, 4 + 2 * ((MB3 + d) % 2) + half, 0:384],
                                                       XT2[:, a, k, t * R:t * R + P],
                                                       w3s[:, 2 * u + k // 3, b, col:col + 384],
                                                       start=(k == 0 and n == 0), stop=(k == KD - 1 and n == 2))
                            mm.then_inc(s_mb, 1)

                pe.wait_ge(s_xl, 1)
                two_experts(0)
                with pe.Fori(1, 4) as j:
                    two_experts(j)

            def bit_layer():
                w1 = WB[:, 0:768].rearrange("p (k o) -> p k o", k=KD)
                pe.wait_ge(s_babs, 1)
                pe.matmul(PS[:, 4, 0:2], ones[:], ws[:, 0:2], start=True, stop=True).then_inc(s_bpe, 1)
                transpose_rows(5, O)
                pe.wait_ge(s_bwq, 1)
                for t in range(T):
                    pe.wait_ge(s_trc, 2 * T * 5 + 2 * t + 2)
                    for k in range(KD):
                        mm = pe.matmul(PS[0:R, 5 + t // 3, (t % 3) * P:(t % 3 + 1) * P],
                                       XT[:, k, t * R:(t + 1) * R], w1[:, k, :], start=(k == 0), stop=(k == KD - 1))
                mm.then_inc(s_bpe, 1)
                pe.wait_ge(s_bq2, 1)
                for t in range(T):
                    tr = pe.transpose(PSz[0:64, t * P:t * P + R], O[0:R, t, 0:64], ident[0:R, 0:R])
                tr.then_inc(s_bpe, 1)
                pe.wait_ge(s_bqt, 1)
                for t in range(T):
                    wait(pe, s_badd, t - 1)
                    for half in range(2):
                        mm = pe.matmul(PS[0:R, 4 * (t % 2) + 2 + half, 0:384], hidT[:, t, :],
                                       WB[0:64, 768 + half * 384:768 + (half + 1) * 384], start=True, stop=True)
                    mm.then_inc(s_bout, 1)

            pe.wait_ge(s_const, 112)
            for g in range(2):
                transpose_rows(g, XN)
                linear(2 * g)
                linear(2 * g + 1)
                edges(g)
                attend(g)
            transpose_rows(2, XN)
            route(0, 2)
            mix_bias(0)
            pe.wait_ge(s_mixd, T)
            ranks()
            mixture0()
            transpose_rows(3, XN)
            linear(4)
            attend(2)
            transpose_rows(4, O)
            linear(5)
            attend(3)
            bit_layer()
            transpose_rows(6, XN)
            linear(6)
            attend(4)
            transpose_rows(7, XN)
            route(1, 7)
            mix_bias(1)
            pe.wait_ge(s_mixd, 2 * T)
            mixture1()
            transpose_rows(8, XN)
            linear(7)
            attend(5)
            transpose_rows(9, O)
            linear(8)
            attend(6)
            transpose_rows(10, XN)
            route(2, 10)
            mix_bias(2)
            pe.wait_ge(s_mixd, 3 * T)
            mixture2()

        @block.scalar
        def _(act):
            def transpose_rows(n):
                per = TR_CHUNKS[n] // 2
                for t in range(T):
                    for half in range(2):
                        g = 2 * T * n + 2 * t + half
                        act.wait_ge(s_trp, g + 1)
                        act.copy(XT[:, half * per:(half + 1) * per, t * R:(t + 1) * R],
                                 PS[:, g % 4, 0:per * R].rearrange("p (k n) -> p k n", k=per)).then_inc(s_trc, 1)

            def log_counts(n):
                act.wait_ge(s_many, n + 1)
                act.activation(mask(n), mask(n), ACT.Ln).then_inc(s_ln, 1)

            def edge_relu(i, u, g):
                base = ET * g
                act.wait_ge(s_zt, base + i + 1)
                wait(act, s_dot, base + i - 1)
                act.activation(zr[:, u % 2, :, :].rearrange("p k c -> p (k c)"),
                               PSz[:, 0:D], ACT.Relu).then_inc(s_zr, 1)

            def edges(g):
                turn = TURN // EU
                for i in range(EU):
                    edge_relu(i, i, g)
                with act.Fori(1, turn) as j:
                    for u in range(EU):
                        edge_relu(j * EU + u, u, g)
                for i in range(TURN, TURN + EU):
                    edge_relu(i, i % EU, g)
                    if g == 0 and i == TURN + 1:
                        log_counts(0)
                with act.Fori(turn + 1, ER) as j:
                    for u in range(EU):
                        edge_relu(j * EU + u, u, g)
                for i in range(ER * EU, ET):
                    edge_relu(i, i % EU, g)
                if g == 0:
                    log_counts(1)

            def attend(n):
                h, kind = HEADS[n]["h"], HEADS[n]["kind"]
                soft = units_before(n, ("table", "gat"))
                every = units_before(n, ("table", "gat", "average"))
                gats = sum(s["kind"] == "gat" for s in HEADS[:n])
                heads = sum(s["h"] for s in HEADS[:n] if s["kind"] == "gat")
                units = T * h
                place = unit_place(n)
                if kind == "gat":
                    act.wait_ge(s_astp, gats + 1)
                    act.copy(AT[0:h], PSz[0:h, 0:T * P].rearrange("h (t n) -> h t n", t=T)[:, :, 0:R])\
                       .then_inc(s_ast, 1)
                for s in range(units + 2):
                    if kind == "gat" and s < units:
                        head, t = place(s)
                        act.wait_ge(s_bc, heads + head + 1)
                        wait(act, s_tp, every + s - 3)
                        act.activation(W[0:R, s % 4, :], PSz[0:R, 0:N], ACT.Identity,
                                       bias=a_d[:, t, head:head + 1]).then_inc(s_v, 1)
                    if kind != "average" and 1 <= s <= units:
                        v = s - 1
                        act.wait_ge(s_lm, soft + v + 1)
                        act.activation(W[0:R, v % 4, :], W[0:R, v % 4, :], ACT.Exp, bias=nmx[:, v % 4:v % 4 + 1],
                                       accum_out=den[:, v % 4:v % 4 + 1]).then_inc(s_e, 1)
                    if s >= 2:
                        v = s - 2
                        act.wait_ge(s_tp, every + v + 1)
                        wait(act, s_op, every + v - 1)
                        act.copy(PT[0:R, v % 2],
                                 PSz[0:R, 1024 * (1 + v % 2):1024 * (1 + v % 2) + T * P]
                                 .rearrange("p (b n) -> p b n", b=T)[:, :, 0:R]).then_inc(s_pt, 1)

            def elu_exp(g):
                for t in range(T):
                    act.wait_ge(s_neg, T * g + t + 1)
                    act.activation(F[0:R, t, 0:D], F[0:R, t, 0:D], ACT.Exp).then_inc(s_elu, 1)

            def route(n):
                act.wait_ge(s_gap, n + 1)
                act.activation(gate[:, 1, :], gate[:, 0, :], ACT.Exp)
                e = N_EXP[n]
                for t in range(T):
                    a = act.activation(comb2[:, t, 0:e], LG[:, t, 0:e], ACT.Exp, bias=gate[:, 2, t:t + 1],
                                       accum_out=gate[:, 3, t:t + 1])
                a.then_inc(s_gex, 1)

            def mix_bias(n):
                act.wait_ge(s_mbt, n + 1)
                act.copy(AT[0:8], PSz[0:8, 0:T * P].rearrange("h (t n) -> h t n", t=T)[:, :, 0:R])\
                   .then_inc(s_mbc, 1)

            def mixture0():
                def round_rows(u):
                    for b in range(KD // 2):
                        act.wait_ge(s_ut, u * (KD // 2) + b + 1)
                        act.copy(urowsT2[:, 0, 2 * b * TU:2 * (b + 1) * TU], PS[:, b, 0:2 * TU]).then_inc(s_uc, 1)

                def round_first(u, g):
                    act.wait_ge(s_w1[g % 2], u * (16 * NG // 2) + 16 * (g // 2 + 1))
                    wait(act, s_ua, u * (NG * FC) + (g - 1) * FC)
                    act.copy(w1s[:, g % 2, 0, :], uw1[g % 2][:, 0:G1 - FC]).then_inc(s_hi1, 1)

                def round_second(u, g):
                    act.wait_ge(s_w2[g % 2], u * (16 * NG // 2) + 16 * (g // 2 + 1))
                    wait(act, s_ub, u * NG + g - 1)
                    act.copy(w2s[:, g % 2, 0, :], uw2[g % 2]).then_inc(s_hi2, 1)

                def hidden(u, g):
                    wait(act, s_hl, u * NG + g - 1)
                    for c in range(FC):
                        q = g * FC + c
                        act.wait_ge(s_ua, u * (NG * FC) + q + 1)
                        act.activation(hid[:, g % 2, c * TU:(c + 1) * TU], PS[:, q % 4, 0:TU], ACT.Gelu,
                                       bias=b1c[:, g % 2, c:c + 1]).then_inc(s_ug, 1)

                def unit(u):
                    for g in range(NG):
                        hidden(u, g)
                        if g + 2 < NG:
                            round_first(u, g + 2)
                        else:
                            round_first(u + 1, g + 2 - NG)
                        if g + 1 < NG:
                            round_second(u, g + 1)
                    round_second(u + 1, 0)
                    round_rows(u + 1)

                act.wait_ge(s_plan, 2)
                units = act.value_load(nunits[0:1, 0:1], min_val=1, max_val=NU)
                round_rows(0)
                round_first(0, 0)
                round_second(0, 0)
                round_first(0, 1)
                unit(0)
                with act.Fori(1, NU) as u:
                    with act.If(u < units):
                        unit(u)

            def mixture1():
                hT = Oz[0:96, 0:2 * N].rearrange("p (u n) -> p u n", u=2)
                act.wait_ge(s_m2w, 48)
                for e in range(6):
                    wait(act, s_mb, T * (e - 1))
                    for hf, (a, b) in enumerate(HALVES):
                        q = 2 * e + hf
                        act.wait_ge(s_ma, q + 1)
                        act.activation(hT[:, e % 2, a:b], PS[0:96, q % 4, 0:b - a], ACT.Gelu,
                                       bias=WB[0:96, 8064 + e:8065 + e]).then_inc(s_mg, 1)

            def mixture2():
                def round_expert(e, u):
                    wait(act, s_mb, MB3 + (e - 1) * T)
                    for half in range(2):
                        act.wait_ge(s_m3w[half], e * 16 + 16)
                        act.copy(w3s[:, 2 * u + half, 0, :], uw3[half]).then_inc(s_h3, 1)

                act.wait_ge(s_sec, 7)
                act.wait_ge(s_trc, 2 * T * 11)
                act.copy(XT2[:, 0, :, 0:N], XT[:, 0:KD, :]).then_inc(s_xh, 1)
                for e in range(2):
                    for half in range(2):
                        act.wait_ge(s_m3w[half], e * 16 + 16)
                        act.copy(w3s[:, 2 * e + half, 0, :], uw3[half]).then_inc(s_h3, 1)
                for u in range(2):
                    round_expert(2 + u, u)
                with act.Fori(2, 4) as j:
                    for u in range(2):
                        round_expert(j * 2 + u, u)

            def bit_layer():
                act.wait_ge(s_bw, 32)
                act.wait_ge(s_bclr, 1)
                act.activation(WB[:, 1536:2304], WB[:, 0:768], ACT.Abs, accum_out=ws[:, 0:1])
                act.activation(WB[0:64, 2304:3072], WB[0:64, 768:1536], ACT.Abs, accum_out=ws[0:64, 1:2])\
                   .then_inc(s_babs, 1)
                for t in range(T):
                    act.wait_ge(s_by, t + 1)
                    act.activation(F[0:R, t, 0:D], O[0:R, t, 0:D], ACT.Abs).then_inc(s_bya, 1)
                transpose_rows(5)
                act.wait_ge(s_bh, 1)
                act.activation(F[0:R, 0:T, 0:64], O[0:R, 0:T, 192:256], ACT.Silu).then_inc(s_bsil, 1)
                act.wait_ge(s_by2, 1)
                act.activation(F[0:R, 0:T, 512:576], O[0:R, 0:T, 64:128], ACT.Abs).then_inc(s_bya, 1)
                act.wait_ge(s_bpe, 3)
                act.copy(hidT, PSz[0:64, 0:T * P].rearrange("h (t n) -> h t n", t=T)[:, :, 0:R]).then_inc(s_bqt, 1)

            for g in range(2):
                transpose_rows(g)
                edges(g)
                attend(g)
                elu_exp(g)
            transpose_rows(2)
            route(0)
            mix_bias(0)
            mixture0()
            transpose_rows(3)
            attend(2)
            transpose_rows(4)
            attend(3)
            bit_layer()
            log_counts(2)
            transpose_rows(6)
            attend(4)
            transpose_rows(7)
            route(1)
            mix_bias(1)
            mixture1()
            transpose_rows(8)
            attend(5)
            transpose_rows(9)
            attend(6)
            transpose_rows(10)
            route(2)
            mix_bias(2)
            mixture2()

        @block.vector
        def _(dve):
            linked = [0]

            def link(ins):
                linked[0] += 1
                ins.then_inc(s_link, 1)
                dve.wait_ge(s_link, linked[0])

            def params(g):
                dve.wait_ge(s_par, 16 * par_total[g + 1])
                return PARAMS[g][0]

            def rows(t, buf, width=D):
                return buf[0:R, t, 0:width]

            def layer_norm(n, src, dst, tr=None, w=None, b=None, width=D):
                for t in range(T):
                    for half in range(2):
                        ins = dve.bn_stats(stats[:, t, half, :], src[0:R, t, half * 384:(half + 1) * 384])
                link(ins)
                for t in range(T):
                    ins = dve.bn_aggr(mv[:, t, :], stats[:, t].rearrange("p h s -> p (h s)"))
                link(ins)
                dve.tensor_scalar(var[:], mv[:, :, 1], LN_EPS, None, ALU.add).then_inc(s_var, 1)
                dve.wait_ge(s_rstd, n + 1)
                for t in range(T):
                    if w is None:
                        ins = dve.tensor_scalar(rows(t, dst), rows(t, src), mv[:, t, 0:1], rstd[:, t:t + 1],
                                                ALU.subtract, ALU.mult)
                    else:
                        link(dve.scalar_tensor_tensor(out=rows(t, dst), in0=rows(t, src), scalar=mv[:, t, 0:1],
                                                      in1=w, op0=ALU.subtract, op1=ALU.mult))
                        ins = dve.scalar_tensor_tensor(out=rows(t, dst), in0=rows(t, dst), scalar=rstd[:, t:t + 1],
                                                       in1=b, op0=ALU.mult, op1=ALU.add)
                    if tr is not None:
                        ins.then_inc(s_rows, 1)
                if tr is None:
                    link(ins)

            def onehots(tile, n, slot, p):
                wait(dve, s_ohu, n - 1)
                a, b = PASSES[p][0] * R, PASSES[p][1] * R
                dve.tensor_scalar(oh[:, slot, 0, 0:N], iota, idf[:, 0, bass.ds(tile, 1)], None, ALU.is_equal)
                dve.tensor_scalar(oh[:, slot, 1, a:b], iota[:, a:b], idf[:, 1, bass.ds(tile, 1)], None,
                                  ALU.is_equal).then_inc(s_oh, 1)

            def counts_out(p):
                a, b = PASSES[p]
                dve.wait_ge(s_ohu, (CT, CT + ET)[p])
                dve.tensor_copy(mask(p, C), PSz[0:R, 2048:2048 + (b - a) * N]).then_inc(s_cnt, 1)
                dve.wait_ge(s_cnt, p + 1)

            def mask_start(n):
                dve.tensor_scalar(mask(n), mask(n, C), 1.0, None, ALU.max).then_inc(s_many, 1)

            def mask_end(n):
                a, b = MASK_PARTS[n]
                off = Oz[0:R, 2 * (N + 1):2 * (N + 1) + (b - a) * N]
                link(dve.tensor_scalar(off, mask(n, C), 0.5, NEGBIG, ALU.is_lt, ALU.mult))
                dve.wait_ge(s_ln, n + 1)
                link(dve.tensor_tensor(mask(n), mask(n), off, ALU.add))

            def edge_rows(n, g, side):
                buf = (F, O)[side]
                for t in range(T):
                    for half in range(2):
                        q = 2 * T * n + 2 * t + half
                        dve.wait_ge(s_linp, q + 1)
                        dve.tensor_tensor(buf[0:R, t, half * 384:(half + 1) * 384], PS[0:R, 4 + q % 4, 0:384],
                                          PB[0:R, side * D + half * 384:side * D + (half + 1) * 384], ALU.add)\
                           .then_inc(s_line, 1)
                    if g:
                        link(dve.memset(buf[0:R, t, D:GW], 0.0))
                    dve.wait_ge(s_line, q + 1)
                    link(dve.scalar_tensor_tensor(out=TMP[:, 0:D], in0=rows(t, buf), scalar=0.2,
                                                  in1=par(2, D), op0=ALU.mult, op1=ALU.mult))
                    h = HEADS[g]["h"]
                    dve.tensor_reduce(buf[0:R, t, D:D + h], TMP[:, 0:D].rearrange("p (h c) -> p h c", h=h),
                                      AX_X, ALU.add).then_inc(s_frow, 1)

            def edges(g):
                base = ET * g

                def add(i, u, rounds):
                    dve.wait_ge(s_gat[u], rounds + 32 * (ER + (u < ET % EU)) * g + 32)
                    dve.tensor_tensor(gs[u], gs[u], gd[u], ALU.add).then_inc(s_z, 1)

                def finish(i, u):
                    dve.wait_ge(s_dot, base + i + 1)
                    wait(dve, s_sc, 16 * (base + i - 7))
                    dve.wait_ge(s_z, base + i + 1)
                    dve.tensor_tensor(lgr[:, u, :], PS[:, 2 + u % 2, 0:8], gs[u][:, D:GW], ALU.add)\
                       .then_inc(s_lg, 1)

                def counting(i, p):
                    if g == 0:
                        for v in range(2):
                            onehots(i * 2 + v - CT * p, i * 2 + v, v, p)

                turn = TURN // EU
                for i in range(2 * EU):
                    add(i, i % EU, 32 * (i // EU))
                    if i >= 2:
                        finish(i - 2, (i - 2) % EU)
                    counting(i, 0)
                with dve.Fori(2, turn) as j:
                    for u in range(EU):
                        add(j * EU + u, u, j * 32)
                        finish(j * EU + (u - 2), (u - 2) % EU)
                        counting(j * EU + u, 0)
                for i in range(TURN, TURN + EU):
                    add(i, i % EU, 32 * (i // EU))
                    finish(i - 2, (i - 2) % EU)
                    if g == 0 and i == TURN:
                        counts_out(0)
                    counting(i, 1)
                    if g == 0 and i == TURN + 1:
                        dve.wait_ge(s_zeroed, LOGITS0)
                        dve.wait_ge(s_zslots, SLOTS0)
                        mask_start(0)
                    if g == 0 and i == TURN + 4:
                        mask_end(0)
                with dve.Fori(turn + 1, ER) as j:
                    for u in range(EU):
                        add(j * EU + u, u, j * 32)
                        finish(j * EU + (u - 2), (u - 2) % EU)
                        counting(j * EU + u, 1)
                for i in range(ER * EU, ET):
                    add(i, i % EU, 32 * (i // EU))
                    finish(i - 2, (i - 2) % EU)
                    counting(i, 1)
                for i in (ET - 2, ET - 1):
                    finish(i, i % EU)
                if g == 0:
                    for n in range(2 * ET, CT + ET):
                        onehots(n - CT, n, n % 2, 1)
                    counts_out(1)
                    mask_start(1)
                    mask_end(1)

            def attend(n):
                h, c, kind = HEADS[n]["h"], HEADS[n]["c"], HEADS[n]["kind"]
                soft = units_before(n, ("table", "gat"))
                gat = units_before(n, ("gat",))
                every = units_before(n, ("table", "gat", "average"))
                units = T * h
                place = unit_place(n)

                def front(s):
                    head, t = place(s)
                    r = s % 4
                    w = W[0:R, r, :]
                    if kind == "gat":
                        dve.wait_ge(s_v, gat + s + 1)
                        link(dve.scalar_tensor_tensor(out=w, in0=w, scalar=0.2, in1=w, op0=ALU.mult, op1=ALU.max))
                        src = w
                    else:
                        wait(dve, s_tp, every + s - 3)
                        if n == 0:
                            dve.wait_ge(s_lt[t % 2], 16 * (t // 2 + 1))
                            src = ltile[:, t % 2, :, head]
                        else:
                            dve.wait_ge(s_lt[1], 16 * 3)
                            src = ltile1[:, t, :]
                    link(dve.tensor_tensor_reduce(out=w, in0=src, in1=NEG[0:R, t, :], scale=1.0, scalar=NEGBIG / 10,
                                                  op0=ALU.add, op1=ALU.max, accum_out=mx[:, r:r + 1]))
                    dve.tensor_scalar(nmx[:, r:r + 1], mx[:, r:r + 1], -1.0, None, ALU.mult).then_inc(s_lm, 1)

                def back(s):
                    r = s % 4
                    dve.wait_ge(s_e, soft + s + 1)
                    link(dve.tensor_scalar(rden[:, s % 8:s % 8 + 1], den[:, r:r + 1], TINY, None, ALU.add))
                    dve.reciprocal(rden[:, s % 8:s % 8 + 1], rden[:, s % 8:s % 8 + 1]).then_inc(s_p, 1)

                def evacuate(s):
                    head, t = place(s)
                    dve.wait_ge(s_op, every + s + 1)
                    if kind == "average":
                        scale = dinv[:, t:t + 1]
                    else:
                        dve.wait_ge(s_p, soft + s + 1)
                        scale = rden[:, s % 8:s % 8 + 1]
                    if c > 512:
                        o, i = O[0:R, t, 0:c].rearrange("p (a c) -> p a c", a=2), PS[0:R, 6:8, 0:c // 2]
                    else:
                        o, i = O[0:R, t, head * c:(head + 1) * c], PS[0:R, 6 + s % 2, 0:c]
                    dve.tensor_scalar(o, i, scale, None, ALU.mult).then_inc(s_out, 1)

                for s in range(units + 3):
                    if kind != "average" and s < units:
                        front(s)
                    if kind != "average" and 1 <= s <= units:
                        back(s - 1)
                    if s >= 3:
                        evacuate(s - 3)
                dve.wait_ge(s_out, every + units)

            def elu(g):
                for t in range(T):
                    dve.tensor_scalar(rows(t, F), rows(t, O), 0.0, None, ALU.min).then_inc(s_neg, 1)
                for t in range(T):
                    dve.wait_ge(s_elu, T * g + t + 1)
                    link(dve.scalar_tensor_tensor(out=rows(t, O), in0=rows(t, O), scalar=0.0, in1=rows(t, F),
                                                  op0=ALU.max, op1=ALU.add))
                    if g == 0:
                        ins = dve.scalar_tensor_tensor(out=rows(t, O), in0=rows(t, O), scalar=-1.0, in1=rows(t, XN),
                                                       op0=ALU.add, op1=ALU.add)
                    else:
                        ins = dve.tensor_scalar(rows(t, O), rows(t, O), -1.0, None, ALU.add)
                link(ins)

            def attention_terms(n, width, h):
                for t in range(T):
                    hw = width // 2
                    for half in range(2):
                        q = 2 * T * n + 2 * t + half
                        dve.wait_ge(s_linp, q + 1)
                        dve.tensor_copy(F[0:R, t, half * hw:(half + 1) * hw], PS[0:R, 4 + q % 4, 0:hw])\
                           .then_inc(s_line, 1)
                    dve.wait_ge(s_line, q + 1)
                    for side, (tmp, a) in enumerate(((TMP, a_s), (TMP2, a_d))):
                        link(dve.tensor_tensor(tmp[:, 0:width], rows(t, F, width), par(side, width), ALU.mult))
                        ins = dve.tensor_reduce(a[:, t, 0:h], tmp[:, 0:width].rearrange("p (h c) -> p h c", h=h),
                                                AX_X, ALU.add)
                        if side == 0 or t < T - 1:
                            link(ins)
                ins.then_inc(s_att, 1)

            def scaled_rows(n):
                for t in range(T):
                    for half in range(2):
                        q = 2 * T * n + 2 * t + half
                        dve.wait_ge(s_linp, q + 1)
                        dve.tensor_scalar(F[0:R, t, half * 384:(half + 1) * 384], PS[0:R, 4 + q % 4, 0:384],
                                          dinv[:, t:t + 1], None, ALU.mult).then_inc(s_line, 1)

            def bias_relu(width, slot):
                for t in range(T):
                    link(dve.tensor_tensor(rows(t, O, width), rows(t, O, width), par(slot, width), ALU.add))
                    ins = dve.tensor_scalar(rows(t, O, width), rows(t, O, width), 0.0, None, ALU.max)
                    ins.then_inc(s_rows, 1)

            def add_to_x(slot, last=True):
                for t in range(T):
                    if slot is not None:
                        link(dve.tensor_tensor(rows(t, O), rows(t, O), par(slot, D), ALU.add))
                    ins = dve.tensor_tensor(X[:, t, :], X[:, t, :], rows(t, O), ALU.add)
                link(ins)

            def route(n):
                e = N_EXP[n]
                dve.wait_ge(s_rtp, n + 1)
                dve.wait_ge(s_rw, 48 * (n + 1))
                if e < 8:
                    dve.memset(LG[:, :, e:8], NEGBIG)
                for t in range(T):
                    ins = dve.tensor_tensor(LG[:, t, 0:e], PS[0:R, 4, t * 8:t * 8 + e], rb[:, 0:e], ALU.add)
                link(ins)
                for t in range(T):
                    ins = dve.max(top[:, t, :], LG[:, t, :])
                link(ins)
                for t in range(T):
                    ins = dve.max_index(topi[:, t, :], top[:, t, :], LG[:, t, :])
                dve.tensor_tensor(gate[:, 0, :], top[:, :, 1], top[:, :, 0], ALU.subtract)
                dve.tensor_scalar(gate[:, 2, :], top[:, :, 0], -1.0, None, ALU.mult).then_inc(s_gap, 1)
                dve.wait_ge(s_gap, n + 1)
                link(dve.tensor_copy(topf[:], topi[:]))
                dve.wait_ge(s_gex, n + 1)
                link(dve.tensor_scalar(gate[:, 4, :], gate[:, 1, :], 1.0, None, ALU.add))
                if n == 2:
                    link(dve.scalar_tensor_tensor(out=gate[:, 4, :], in0=gate[:, 3, :], scalar=1.0e-9,
                                                  in1=gate[:, 4, :], op0=ALU.mult, op1=ALU.add))
                link(dve.reciprocal(gate[:, 5, :], gate[:, 4, :]))
                link(dve.tensor_tensor(gate[:, 6, :], gate[:, 5, :], gate[:, 1, :], ALU.mult))
                for t in range(T):
                    dve.tensor_scalar(comb[:, t, :], iota8[0:R], topf[:, t, 0:1], gate[:, 5, t:t + 1],
                                      ALU.is_equal, ALU.mult)
                    ins = dve.tensor_scalar(comb2[:, t, :], iota8[0:R], topf[:, t, 1:2], gate[:, 6, t:t + 1],
                                            ALU.is_equal, ALU.mult)
                link(ins)
                dve.tensor_tensor(comb[:], comb[:], comb2[:], ALU.add).then_inc(s_comb, 1)
                dve.wait_ge(s_comb, n + 1)

            def in_halves(ap):
                return ap.rearrange("p (a c) -> p a c", a=2)

            def mix_bias(n):
                for t in range(T):
                    g = T * n + t
                    dve.wait_ge(s_mixp, g + 1)
                    bank = 4 + 2 * (g % 2)
                    dve.tensor_tensor(in_halves(X[:, t, :]), PS[0:R, bank:bank + 2, 0:384], in_halves(X[:, t, :]),
                                      ALU.add).then_inc(s_mixd, 1)
                dve.wait_ge(s_mixd, T * (n + 1))

            def add_expert(done, t, parity, e):
                dve.wait_ge(s_mb, done + 1)
                wait(dve, s_md, done)
                bank = 4 + 2 * (parity % 2)
                dve.scalar_tensor_tensor(out=in_halves(X[:, t, :]), in0=PS[0:R, bank:bank + 2, 0:384],
                                         scalar=comb[:, t, bass.ds(e, 1)] if not isinstance(e, int) else comb[:, t, e:e + 1],
                                         in1=in_halves(X[:, t, :]), op0=ALU.mult, op1=ALU.add).then_inc(s_md, 1)

            def make_plan():
                for t in range(T):
                    for k in range(2):
                        ins = dve.tensor_scalar(pick[:, k, t, :], iota8[0:R], topf[:, t, k:k + 1], None, ALU.is_equal)
                link(ins)
                dve.tensor_tensor(pick[:, 2], pick[:, 0], pick[:, 1], ALU.add).then_inc(s_pick, 1)
                dve.wait_ge(s_rank, 1)
                scratch = uexpf[:, 0:NU]
                units, start, end = plan[:, 0, :], plan[:, 1, :], plan[:, 2, :]
                link(dve.tensor_scalar(units, PS[:, 6, 0:8], 0.5, None, ALU.is_gt))
                for full in range(TU, N, TU):
                    link(dve.scalar_tensor_tensor(out=units, in0=PS[:, 6, 0:8], scalar=full + 0.5, in1=units,
                                                  op0=ALU.is_gt, op1=ALU.add))
                link(dve.tensor_copy(plan[:, 2, 0:1], plan[:, 0, 0:1]))
                for e in range(1, 8):
                    link(dve.tensor_tensor(plan[:, 2, e:e + 1], plan[:, 2, e - 1:e], plan[:, 0, e:e + 1], ALU.add))
                link(dve.tensor_tensor(start, end, units, ALU.subtract))
                for t in range(T):
                    ins = dve.scalar_tensor_tensor(out=place_of[:, t, :], in0=start[0:R], scalar=float(TU),
                                                   in1=PS[0:R, 5, t * 8:(t + 1) * 8], op0=ALU.mult, op1=ALU.add)
                link(ins)
                for k in range(2):
                    ins = dve.tensor_tensor(pick[:, k], pick[:, k], place_of[:], ALU.mult)
                link(ins)
                for k in range(2):
                    ins = dve.tensor_reduce(slotf[:, k, :], pick[:, k], AX_X, ALU.add)
                link(ins)
                dve.wait_ge(s_rows, 3 * T)
                dve.tensor_copy(slots[:], slotf[:]).then_inc(s_slots, 1)
                link(dve.memset(uexpf[:], 0.0))
                for e in range(8):
                    link(dve.scalar_tensor_tensor(out=uexpf[:], in0=iotaU[:], scalar=plan[:, 2, e:e + 1], in1=uexpf[:],
                                                  op0=ALU.is_ge, op1=ALU.add))
                dve.tensor_scalar(uexp[:], uexpf[:], 7.0, None, ALU.min).then_inc(s_plan, 1)
                dve.tensor_copy(nunits[:], plan[:, 2, 7:8]).then_inc(s_plan, 1)
                left, last = plan[:, 3, :], plan[:, 4, :]
                link(dve.tensor_scalar(left, units, 4.0, None, ALU.mult))
                for full in range(0, N, TU // 4):
                    link(dve.scalar_tensor_tensor(out=last, in0=PS[:, 6, 0:8], scalar=full + 0.5, in1=left,
                                                  op0=ALU.is_gt, op1=ALU.subtract))
                    link(dve.tensor_scalar(left, last, -1.0, None, ALU.mult))
                link(dve.tensor_scalar(last, end, -1.0, None, ALU.add))
                link(dve.memset(emptyf[:], 0.0))
                for e in range(8):
                    link(dve.tensor_scalar(scratch, iotaU[:, 0:NU], plan[:, 4, e:e + 1], plan[:, 3, e:e + 1],
                                           ALU.is_equal, ALU.mult))
                    link(dve.tensor_tensor(emptyf[:], emptyf[:], scratch, ALU.add))
                dve.memset(PS[:, 3, 0:TU], 0.0)
                link(dve.memset(PS[:, 6:8, 0:384], 0.0))
                dve.tensor_copy(empty[:], emptyf[:]).then_inc(s_plan, 1)

            def mixture0():
                def split_rows(u):
                    for b in range(KD // 2):
                        dve.wait_ge(s_uc, u * (KD // 2) + b + 1)
                        part = slice(2 * b * TU, 2 * (b + 1) * TU)
                        dve.tensor_tensor(urowsT2[:, 1, part], PS[:, b, 0:2 * TU], urowsT2[:, 0, part].bitcast(F32),
                                          ALU.subtract).then_inc(s_ul, 1)

                def split_first(u, g):
                    dve.wait_ge(s_hi1, u * NG + g + 1)
                    wait(dve, s_ug, u * (NG * FC) + (g - 1) * FC)
                    dve.tensor_copy(b1c[:, g % 2, :], uw1[g % 2][:, G1 - FC:G1])
                    dve.tensor_tensor(w1s[:, g % 2, 1, :], uw1[g % 2][:, 0:G1 - FC], w1s[:, g % 2, 0, :].bitcast(F32),
                                      ALU.subtract).then_inc(s_lo1, 1)

                def split_second(u, g):
                    dve.wait_ge(s_hi2, u * NG + g + 1)
                    dve.tensor_tensor(w2s[:, g % 2, 1, :], uw2[g % 2], w2s[:, g % 2, 0, :].bitcast(F32),
                                      ALU.subtract).then_inc(s_lo2, 1)

                def split_hidden(u, g):
                    dve.wait_ge(s_ug, u * (NG * FC) + (g + 1) * FC)
                    wait(dve, s_ub, u * NG + g - 1)
                    dve.tensor_copy(hid2[:, g % 2, 0, :], hid[:, g % 2, :]).then_inc(s_hh, 1)
                    dve.wait_ge(s_hh, u * NG + g + 1)
                    dve.tensor_tensor(hid2[:, g % 2, 1, :], hid[:, g % 2, :], hid2[:, g % 2, 0, :].bitcast(F32),
                                      ALU.subtract).then_inc(s_hl, 1)

                def unit(u):
                    for g in range(NG):
                        split_hidden(u, g)
                        if g + 2 < NG:
                            split_first(u, g + 2)
                        else:
                            split_first(u + 1, g + 2 - NG)
                        if g + 1 < NG:
                            split_second(u, g + 1)
                    split_second(u + 1, 0)
                    split_rows(u + 1)
                    dve.wait_ge(s_ub, u * NG + NG)
                    wait(dve, s_us, u * 16)
                    for s in range(SU):
                        dve.tensor_copy(in_halves(uout[:, s, :]), PS[:, 4 + 2 * s:6 + 2 * s, 0:384]).then_inc(s_uy, 1)

                dve.wait_ge(s_plan, 2)
                units = dve.value_load(nunits[0:1, 0:1], min_val=1, max_val=NU)
                split_rows(0)
                split_first(0, 0)
                split_second(0, 0)
                split_first(0, 1)
                unit(0)
                with dve.Fori(1, NU) as u:
                    with dve.If(u < units):
                        unit(u)
                dve.wait_ge(s_ua, units * (NG * FC) + FC)
                dve.nop().then_inc(s_left, 1)
                for k in range(2):
                    dve.wait_ge(s_yg[k], 16 * T)
                    for t in range(T):
                        ins = dve.scalar_tensor_tensor(out=X[:, t, :], in0=picked[:, k, t, :],
                                                       scalar=gate[:, 5 + k, t:t + 1], in1=X[:, t, :],
                                                       op0=ALU.mult, op1=ALU.add)
                    link(ins)

            def mixture1():
                for e in range(6):
                    for t in range(T):
                        add_expert(T * e + t, t, T * e + t, e)

            def mixture2():
                def split_expert(e, u):
                    for half in range(2):
                        dve.wait_ge(s_h3, e * 2 + half + 1)
                        dve.tensor_tensor(w3s[:, 2 * u + half, 1, :], uw3[half], w3s[:, 2 * u + half, 0, :].bitcast(F32),
                                          ALU.subtract).then_inc(s_l3, 1)

                def two_experts(j, more=True):
                    for u in range(2):
                        for t in range(T):
                            d = u * T + t
                            add_expert(j * (2 * T) + MB3 + d, t, MB3 + d, j * 2 + u)
                        if more:
                            split_expert(j * 2 + u + 2, u)

                for k in range(KD):
                    ins = dve.tensor_scalar(XT2[:, 0, k, N:NP], ident[:, 0:NP - N], 0.0, None, ALU.mult)
                    ins = dve.tensor_scalar(XT2[:, 1, k, N:NP], ident[:, 0:NP - N], 0.0, None, ALU.mult)
                dve.wait_ge(s_xh, 1)
                dve.tensor_tensor(XT2[:, 1, :, 0:N], XT[:, 0:KD, :], XT2[:, 0, :, 0:N].bitcast(F32), ALU.subtract)\
                   .then_inc(s_xl, 1)
                for e in range(2):
                    split_expert(e, e)
                two_experts(0)
                with dve.Fori(1, 3) as j:
                    two_experts(j)
                two_experts(3, more=False)

            def bit_layer():
                dve.memset(ws[:], 0.0).then_inc(s_bclr, 1)
                params(4)
                for t in range(T):
                    ins = dve.tensor_tensor_reduce(out=rows(t, O), in0=rows(t, XN), in1=rows(t, XN), scale=1.0,
                                                   scalar=0.0, op0=ALU.mult, op1=ALU.add, accum_out=bs[0:R, 0, t:t + 1])
                link(ins)
                dve.tensor_scalar(var[:], bs[0:R, 0, :], 1.0 / D, 1.0e-6, ALU.mult, ALU.add).then_inc(s_var, 1)
                dve.wait_ge(s_rstd, 7)
                for t in range(T):
                    dve.scalar_tensor_tensor(out=rows(t, O), in0=rows(t, XN), scalar=rstd[:, t:t + 1], in1=par(0, D),
                                             op0=ALU.mult, op1=ALU.mult).then_inc(s_by, 1)
                dve.wait_ge(s_bpe, 1)
                dve.tensor_scalar(ws[:, 2:3], PS[:, 4, 0:1], 1.0 / (P * D), 1.0e-5, ALU.mult, ALU.max)
                link(dve.tensor_scalar(ws[:, 3:4], PS[:, 4, 1:2], 1.0 / (64 * D), 1.0e-5, ALU.mult, ALU.max))
                link(dve.reciprocal(ws[:, 4:6], ws[:, 2:4]))
                for w, k in ((WB[:, 0:768], 4), (WB[0:64, 768:1536], 5)):
                    np_ = w.shape[0]
                    link(dve.tensor_scalar(w, w, ws[0:np_, k:k + 1], -1.0, ALU.mult, ALU.max))
                    link(dve.tensor_scalar(w, w, ROUND, ROUND + 1.0, ALU.add, ALU.min))
                    ins = dve.tensor_scalar(w, w, ROUND, None, ALU.subtract)
                ins.then_inc(s_bwq, 1)

                def quantise(width, src_abs, at, k):
                    for t in range(T):
                        dve.wait_ge(s_bya, (t + 1) if k == 0 else (T + 1))
                        ins = dve.tensor_reduce(bs[0:R, 1 + k, t:t + 1], src_abs(t), AX_X, ALU.max)
                    link(ins)
                    link(dve.tensor_scalar(bs[0:R, 1 + k, :], bs[0:R, 1 + k, :], 1.0e-5, None, ALU.max))
                    link(dve.reciprocal(bs[0:R, 3 + k, :], bs[0:R, 1 + k, :]))
                    link(dve.tensor_scalar(bs[0:R, 3 + k, :], bs[0:R, 3 + k, :], 127.0, None, ALU.mult))
                    link(dve.tensor_scalar(bs[0:R, 5 + k, :], bs[0:R, 1 + k, :], 1.0 / 127.0, ws[0:R, 2 + k:3 + k],
                                           ALU.mult, ALU.mult))
                    for t in range(T):
                        y, q = at(t)
                        link(dve.tensor_scalar(q, y, bs[0:R, 3 + k, t:t + 1], -128.0, ALU.mult, ALU.max))
                        link(dve.tensor_scalar(q, q, ROUND, ROUND + 127.0, ALU.add, ALU.min))
                        ins = dve.tensor_scalar(q, q, ROUND, None, ALU.subtract)
                        if k == 0:
                            ins.then_inc(s_rows, 1)
                    if k == 1:
                        ins.then_inc(s_bq2, 1)

                quantise(D, lambda t: rows(t, F), lambda t: (rows(t, O), rows(t, O)), 0)
                dve.wait_ge(s_bpe, 2)
                for t in range(T):
                    ins = dve.tensor_scalar(O[0:R, t, 128:256], PS[0:R, 5 + t // 3, (t % 3) * P:(t % 3 + 1) * P],
                                            bs[0:R, 5, t:t + 1], None, ALU.mult)
                ins.then_inc(s_bh, 1)
                dve.wait_ge(s_bh, 1)
                dve.wait_ge(s_bsil, 1)
                link(dve.tensor_tensor(O[0:R, 0:T, 0:64], F[0:R, 0:T, 0:64], O[0:R, 0:T, 128:192], ALU.mult))
                for t in range(T):
                    ins = dve.tensor_tensor_reduce(out=O[0:R, t, 64:128], in0=O[0:R, t, 0:64], in1=O[0:R, t, 0:64],
                                                   scale=1.0, scalar=0.0, op0=ALU.mult, op1=ALU.add,
                                                   accum_out=bs[0:R, 7, t:t + 1])
                link(ins)
                dve.tensor_scalar(var[:], bs[0:R, 7, :], 1.0 / 64, 1.0e-6, ALU.mult, ALU.add).then_inc(s_var, 1)
                dve.wait_ge(s_rstd, 8)
                for t in range(T):
                    ins = dve.scalar_tensor_tensor(out=O[0:R, t, 64:128], in0=O[0:R, t, 0:64],
                                                   scalar=rstd[:, t:t + 1], in1=PB[0:R, D:D + 64],
                                                   op0=ALU.mult, op1=ALU.mult)
                ins.then_inc(s_by2, 1)
                dve.wait_ge(s_by2, 1)
                quantise(64, lambda t: F[0:R, t, 512:576], lambda t: (O[0:R, t, 64:128], O[0:R, t, 0:64]), 1)
                for t in range(T):
                    dve.wait_ge(s_bout, t + 1)
                    bank = 4 * (t % 2) + 2
                    dve.scalar_tensor_tensor(out=in_halves(X[:, t, :]), in0=PS[0:R, bank:bank + 2, 0:384],
                                             scalar=bs[0:R, 6, t:t + 1], in1=in_halves(X[:, t, :]),
                                             op0=ALU.mult, op1=ALU.add).then_inc(s_badd, 1)
                dve.wait_ge(s_badd, T)

            def announce(s):
                dve.nop().then_inc(s, 1)

            def section_end():
                announce(s_sec)

            dve.memset(mhalf[:], -0.5).then_inc(s_mh, 1)
            dve.memset(NEG[:], 0.0).then_inc(s_zero, 1)
            dve.memset(ones[:], 1.0)
            dve.wait_ge(s_idx, 16)
            dve.tensor_copy(idf[:, 0, 0:ET], idx[:, :, 0])
            link(dve.tensor_copy(idf[:, 1, 0:ET], idx[:, :, 1]))
            keyf = W[:, 0, 0:ET]
            link(dve.scalar_tensor_tensor(out=keyf, in0=idf[:, 1, 0:ET], scalar=float(N), in1=idf[:, 0, 0:ET],
                                          op0=ALU.mult, op1=ALU.add))
            link(dve.tensor_copy(key[:], keyf))
            dve.memset(idf[:, :, ET:CT], -1.0)
            for a in range(E - (ET - 1) * P, P, 32):
                ins = dve.memset(idf[a:a + 32, :, ET - 1:ET], -1.0)
            ins.then_inc(s_keys, 1)
            dve.wait_ge(s_keys, 1)
            dve.wait_ge(s_const, 112)
            for a in range(2):
                for k in range(KD):
                    ins = dve.tensor_scalar(blk[:, a, k, :], hmask[:, a, k, :], attc[:, a, k:k + 1], 0.8,
                                            ALU.mult, ALU.mult)
            link(ins)
            dve.wait_ge(s_x, 16)
            layer_norm(0, X, XN, tr=0)

            for g in range(2):
                params(g)
                edge_rows(2 * g, g, 0)
                edge_rows(2 * g + 1, g, 1)
                edges(g)
                attend(g)
                elu(g)
                layer_norm(1 + g, O, XN if g == 0 else O, tr=1 if g == 0 else None, w=par(3, D), b=par(4, D))
                if g == 0:
                    dve.wait_ge(s_rows, 2 * T)
                else:
                    add_to_x(None)
                announce(s_pfree)
            section_end()
            layer_norm(3, X, XN, tr=2)
            route(0)
            mix_bias(0)
            make_plan()
            mixture0()
            section_end()
            layer_norm(4, X, XN, tr=3)
            params(2)
            attention_terms(4, 1024, 8)
            attend(2)
            bias_relu(1024, 2)
            dve.wait_ge(s_rows, 5 * T)
            announce(s_pfree)
            params(3)
            attention_terms(5, 768, 1)
            attend(3)
            add_to_x(2)
            announce(s_pfree)
            section_end()
            layer_norm(5, X, XN)
            bit_layer()
            announce(s_pfree)
            section_end()
            for t in range(T):
                ins = dve.tensor_tensor(C[0:R, t, t * R:(t + 1) * R], C[0:R, t, t * R:(t + 1) * R],
                                        ident[0:R, 0:R], ALU.add)
            link(ins)
            mask_start(2)
            link(dve.tensor_reduce(bs[0:R, 8, :], C[0:R], AX_X, ALU.add))
            layer_norm(8, X, XN, tr=6)
            dve.tensor_copy(var[:], bs[0:R, 8, :]).then_inc(s_var, 1)
            dve.wait_ge(s_rstd, 10)
            link(dve.tensor_copy(dinv[:], rstd[:]))
            params(5)
            scaled_rows(6)
            attend(4)
            add_to_x(0)
            announce(s_pfree)
            section_end()
            layer_norm(10, X, XN, tr=7)
            route(1)
            mix_bias(1)
            mixture1()
            dve.wait_ge(s_md, MB3)
            section_end()
            layer_norm(11, X, XN, tr=8)
            params(6)
            mask_end(2)
            attention_terms(7, 768, 4)
            attend(5)
            bias_relu(768, 2)
            dve.wait_ge(s_rows, 10 * T)
            announce(s_pfree)
            params(7)
            attention_terms(8, 768, 4)
            attend(6)
            add_to_x(2)
            announce(s_pfree)
            section_end()
            layer_norm(12, X, XN, tr=10)
            route(2)
            mix_bias(2)
            mixture2()
            dve.wait_ge(s_md, MB3 + 8 * T)
            section_end()
    return nc


def _layout(inputs):
    a = {k: np.ascontiguousarray(v) for k, v in inputs.items()}

    def cols(w):
        k = w.shape[0] // P
        return np.ascontiguousarray(w.reshape(k, P, w.shape[1]).transpose(1, 0, 2).reshape(P, -1))

    out = {"x": a["x"]}
    ends = np.stack([a["src"], a["dst"]], -1)
    ends = np.concatenate([ends, ends[:ET * P - E]])
    out["edges"] = np.ascontiguousarray(ends.reshape(ET, P, 2).transpose(1, 0, 2))
    out["iota"] = np.ascontiguousarray(np.broadcast_to(np.arange(N, dtype=np.float32), (P, N)))
    out["iota8"] = np.ascontiguousarray(np.broadcast_to(np.arange(8, dtype=np.float32), (P, 8)))
    out["iotaU"] = np.ascontiguousarray(np.broadcast_to(np.arange(NU + 1, dtype=np.float32), (P, NU + 1)))
    out["before"] = np.triu(np.ones((R, R), np.float32), 1)
    out["ident"] = np.eye(P, dtype=np.float32)
    out["attc"] = np.ascontiguousarray(np.stack([a["L0_gnn_attn1"].reshape(KD, P).T,
                                                 a["L0_gnn_attno"].reshape(KD, P).T], 1))
    feature = np.arange(D).reshape(KD, P).T
    hm = np.zeros((P, 2, KD, 8), np.float32)
    for h in range(8):
        hm[:, 0, :, h] = feature // 96 == h
    hm[:, 1, :, 0] = 1.0
    out["hmask"] = hm
    for n in ("L0_gnn_W1s", "L0_gnn_W1d", "L0_gnn_Wos", "L0_gnn_Wod", "L2_gnn_W", "L3_gnn_W1", "L3_gnn_W2"):
        out[n] = cols(a[n])
    for n in ("L1_gnn_W1", "L1_gnn_W2", "L1_ffn_w_in"):
        out[n] = cols(a[n].T)
    out["L1_ffn_w_out"] = np.ascontiguousarray(a["L1_ffn_w_out"].T)
    for n in ("L0_ffn_router_w", "L2_ffn_gate_w"):
        out[n] = cols(a[n]).reshape(P, KD, -1)
    out["L3_ffn_router_w"] = cols(a["L3_ffn_router_w"].T).reshape(P, KD, -1)
    for n in ("L0_ffn_b2", "L2_ffn_b2", "L3_ffn_expert_b"):
        out[n] = a[n]
    w1 = a["L0_ffn_w1"].reshape(8, KD, P, NG, FC * P).transpose(0, 3, 2, 1, 4).reshape(8 * NG, P, -1)
    b1 = a["L0_ffn_b1"].reshape(8 * NG, FC, P).transpose(0, 2, 1)
    out["L0_ffn_w1"] = np.ascontiguousarray(np.concatenate([w1, b1], 2))
    out["L0_ffn_w2"] = np.ascontiguousarray(
        a["L0_ffn_w2"].reshape(8, NG, FC, P, D).transpose(0, 1, 3, 2, 4).reshape(8 * NG, P, -1))
    out["L2_ffn_w1"] = np.ascontiguousarray(a["L2_ffn_w1"].reshape(6, KD, P, 96).transpose(2, 0, 1, 3).reshape(P, -1))
    out["L2_ffn_w2"] = np.ascontiguousarray(a["L2_ffn_w2"].transpose(1, 0, 2).reshape(96, -1))
    out["L2_ffn_b1"] = np.ascontiguousarray(a["L2_ffn_b1"].T)
    out["L3_ffn_expert_w"] = np.ascontiguousarray(
        a["L3_ffn_expert_w"].transpose(0, 2, 1).reshape(8, KD, P, D).transpose(0, 2, 1, 3).reshape(8, P, -1))
    for n, v in a.items():
        if n not in out and n not in ("src", "dst", "L0_ffn_b1"):
            out[n] = v.reshape(1, -1)
    return out


def kernel(**inputs):
    import concourse.bacc as bacc
    from concourse.bass_utils import run_bass_kernel_spmd

    nc = bacc.Bacc("TRN2", target_bir_lowering=False, num_devices=1)
    arrays, aps = {}, {}
    for name, v in _layout(inputs).items():
        arrays["in_" + name] = v
        aps[name] = nc.dram_tensor("in_" + name, v.shape, mybir.dt.from_np(v.dtype), kind="ExternalInput").ap()
    out = nc.dram_tensor("out_0", (N, D), F32, kind="ExternalOutput").ap()
    build(nc, aps, out)
    r = run_bass_kernel_spmd(nc, [arrays], core_ids=[0])
    return r.results[0]["out_0"]
```
